# Optimizing a Trainium2 kernel written in Bass

```python
import numpy as np
import jax
import jax.numpy as jnp

def _softmax(x, axis=-1):
    return jax.nn.softmax(x, axis=axis)

def _gelu(x):
    return jax.nn.gelu(x, approximate=True)

def _silu(x):
    return jax.nn.silu(x)

def _sigmoid(x):
    return jax.nn.sigmoid(x)

def _layernorm(x, axis=-1, eps=1e-05):
    m = jnp.mean(x, axis=axis, keepdims=True)
    v = jnp.var(x, axis=axis, keepdims=True)
    return (x - m) / jnp.sqrt(v + eps)

def _scatter_add(tgt, idx, src, axis=0):
    return tgt.at[idx].add(src)

def _segment_sum(src, seg, n):
    return jax.ops.segment_sum(src, seg, n)
kernel_name = 'mk_xattn_ffn_d4_seqx_r8_94c0ba'

def setup_inputs(seed: int=0):
    np.random.seed(seed)
    _w = jnp.asarray

    def _rec_inputs():
        import jax
        import jax.numpy as jnp
        _rk = jax.random.key(seed)
        x = -0.0005146 + 1 * jax.random.normal(jax.random.fold_in(_rk, 1), (32, 64, 128), jnp.float32)
        _lenS = 64 - jax.random.randint(jax.random.fold_in(_rk, 7), (32,), 0, max(1, 64 // 4) + 1, jnp.int32)
        _lenS2 = 64 - jax.random.randint(jax.random.fold_in(_rk, 8), (32,), 0, max(1, 64 // 4) + 1, jnp.int32)
        _ctx_1024P = jax.random.normal(jax.random.fold_in(_rk, 11), (32, 16, 128), jnp.float32)
        _ctx_1024c = jax.random.dirichlet(jax.random.fold_in(_rk, 511), 0.3 * jnp.ones((16,), jnp.float32), (32, 64))
        _ctx_1024t = jnp.einsum('bsk,bkd->bsd', _ctx_1024c, _ctx_1024P)
        _ctx_1024t = _ctx_1024t * jax.lax.rsqrt(jnp.mean(jnp.square(_ctx_1024t)) + 1e-12) * 0.953939
        ctx_1024 = -0.000392918 + 0.999932 * (_ctx_1024t + 0.3 * jax.random.normal(jax.random.fold_in(_rk, 611), (32, 64, 128), jnp.float32))
        return (x, ctx_1024)
    x, ctx_1024 = _rec_inputs()

    def _L0_xattn_setup():
        import jax, jax.numpy as jnp
        import numpy as np
        DIM = 128
        DIM_HEAD = 64
        HEADS = 16
        INNER = DIM_HEAD * HEADS
        EPS = 1e-05

        def layer_norm(x, g, b):
            m = jnp.mean(x, axis=-1, keepdims=True)
            v = jnp.mean(jnp.square(x - m), axis=-1, keepdims=True)
            return (x - m) * jax.lax.rsqrt(v + EPS) * g + b
        key = jax.random.key(seed)
        ks = jax.random.split(key, 8)
        B, N_IMG, N_LAT = (4, 512, 64)
        std = 1.0 / np.sqrt(DIM)
        return {'image_embeds': jax.random.normal(ks[0], (B, N_IMG, DIM), dtype=jnp.float32), 'latents': jax.random.normal(ks[1], (B, N_LAT, DIM), dtype=jnp.float32), 'ln1_g': jnp.ones((DIM,), jnp.float32), 'ln1_b': jnp.zeros((DIM,), jnp.float32), 'ln2_g': jnp.ones((DIM,), jnp.float32), 'ln2_b': jnp.zeros((DIM,), jnp.float32), 'Wq': jax.random.normal(ks[2], (DIM, INNER), dtype=jnp.float32) * std, 'Wkv': jax.random.normal(ks[3], (DIM, 2 * INNER), dtype=jnp.float32) * std, 'Wo': jax.random.normal(ks[4], (INNER, DIM), dtype=jnp.float32) * std}
    _L0_xattn_all = _L0_xattn_setup()
    _L0_xattn_in = {k: v for k, v in _L0_xattn_all.items() if k in ('ln1_g', 'ln1_b', 'ln2_g', 'ln2_b', 'Wq', 'Wkv', 'Wo')}
    del _L0_xattn_all

    def _L0_ffn_setup():
        import jax, jax.numpy as jnp
        import numpy as np
        B, S, H, F, G = (8, 256, 128, 512, 128)
        EPS = 1e-05

        def _dequant(q, scales, g):
            K, N = q.shape
            w = (q.astype(jnp.float32) - 128.0).reshape(K // g, g, N) * scales[:, None, :]
            return w.reshape(K, N)
        key = jax.random.key(seed)
        ks = jax.random.split(key, 8)
        x = jax.random.normal(ks[0], (B, S, H), dtype=jnp.float32)
        ln_gamma = jnp.ones((H,), jnp.float32)
        ln_beta = jnp.zeros((H,), jnp.float32)
        fc1_q = jax.random.randint(ks[1], (H, F), 0, 32, dtype=jnp.int32)
        fc2_q = jax.random.randint(ks[2], (F, H), 0, 32, dtype=jnp.int32)
        fc1_scales = jax.random.uniform(ks[3], (H // G, F), jnp.float32) * 0.02 + 0.001
        fc2_scales = jax.random.uniform(ks[4], (F // G, H), jnp.float32) * 0.02 + 0.001
        fc1_bias = jax.random.normal(ks[5], (F,), jnp.float32) * 0.02
        fc2_bias = jax.random.normal(ks[6], (H,), jnp.float32) * 0.02
        return {'x': x, 'ln_gamma': ln_gamma, 'ln_beta': ln_beta, 'fc1_q': fc1_q, 'fc1_scales': fc1_scales, 'fc1_bias': fc1_bias, 'fc2_q': fc2_q, 'fc2_scales': fc2_scales, 'fc2_bias': fc2_bias}
    _L0_ffn_all = _L0_ffn_setup()
    _L0_ffn_in = {k: v for k, v in _L0_ffn_all.items() if k in ('ln_gamma', 'ln_beta', 'fc1_q', 'fc1_scales', 'fc1_bias', 'fc2_q', 'fc2_scales', 'fc2_bias')}
    del _L0_ffn_all

    def _L1_xattn_setup():
        import jax, jax.numpy as jnp
        import numpy as np
        C = 128
        B, SQ, SKV = (4, 256, 256)
        key = jax.random.key(seed)
        ks = jax.random.split(key, 10)
        s = 1.0 / np.sqrt(C)
        return {'x': jax.random.normal(ks[0], (B, SQ, C), jnp.float32), 'content_embeddings': jax.random.normal(ks[1], (B, SKV, C), jnp.float32), 'Wq': jax.random.normal(ks[2], (C, C), jnp.float32) * s, 'bq': jnp.zeros((C,), jnp.float32), 'Wk': jax.random.normal(ks[3], (C, C), jnp.float32) * s, 'bk': jnp.zeros((C,), jnp.float32), 'Wv': jax.random.normal(ks[4], (C, C), jnp.float32) * s, 'bv': jnp.zeros((C,), jnp.float32), 'Wo': jax.random.normal(ks[5], (C, C), jnp.float32) * s, 'bo': jnp.zeros((C,), jnp.float32)}
    _L1_xattn_all = _L1_xattn_setup()
    _L1_xattn_in = {k: v for k, v in _L1_xattn_all.items() if k in ('Wq', 'bq', 'Wk', 'bk', 'Wv', 'bv', 'Wo', 'bo')}
    del _L1_xattn_all

    def _L1_ffn_setup():
        import jax, jax.numpy as jnp
        import numpy as np
        D = 128
        E = 8
        K = 2
        NUM_ITER = 2
        DT = 0.1
        H = 64
        CTX = 2 * D

        def _gelu(t):
            return jax.nn.gelu(t, approximate=False)

        def _inl(ctrl, x, v, mu):
            alpha_raw, beta_raw, gate_raw = jnp.split(ctrl, 3, axis=-1)
            alpha = jax.nn.sigmoid(alpha_raw)
            beta = jax.nn.softplus(beta_raw)
            gate = jax.nn.sigmoid(gate_raw)
            error = x - mu
            v_next = alpha * v - beta * error
            x_next = x + DT * gate * v_next
            return (x_next, v_next)
        key = jax.random.key(seed)
        ks = jax.random.split(key, 20)
        s = 0.02
        inp = {'x': jax.random.normal(ks[0], (4, 512, D), jnp.float32), 'w_r1': jax.random.normal(ks[1], (D, D // 4), jnp.float32) * s, 'b_r1': jnp.zeros((D // 4,), jnp.float32), 'w_r2': jax.random.normal(ks[2], (D // 4, E), jnp.float32) * s, 'b_r2': jnp.zeros((E,), jnp.float32), 'w_h1': jax.random.normal(ks[3], (D, D // 4), jnp.float32) * s, 'b_h1': jnp.zeros((D // 4,), jnp.float32), 'w_h2': jax.random.normal(ks[4], (D // 4, 1), jnp.float32) * s, 'b_h2': jnp.zeros((1,), jnp.float32), 'expert_w1': jax.random.normal(ks[5], (E, CTX, H), jnp.float32) * s, 'expert_b1': jnp.zeros((E, H), jnp.float32), 'expert_w2': jax.random.normal(ks[6], (E, H, 3 * D), jnp.float32) * s, 'expert_b2': jnp.zeros((E, 3 * D), jnp.float32), 'w_s1': jax.random.normal(ks[7], (CTX, H), jnp.float32) * s, 'b_s1': jnp.zeros((H,), jnp.float32), 'w_s2': jax.random.normal(ks[8], (H, 3 * D), jnp.float32) * s, 'b_s2': jnp.zeros((3 * D,), jnp.float32), 'shared_weight': jnp.asarray(0.5, jnp.float32), 'w_f1': jax.random.normal(ks[9], (D, 2 * D), jnp.float32) * s, 'b_f1': jnp.zeros((2 * D,), jnp.float32), 'w_f2': jax.random.normal(ks[10], (2 * D, D), jnp.float32) * s, 'b_f2': jnp.zeros((D,), jnp.float32), 'integration_weight': jnp.full((D,), 0.5, jnp.float32), 'mu': jnp.zeros((D,), jnp.float32)}
        return inp
    _L1_ffn_all = _L1_ffn_setup()
    _L1_ffn_in = {k: v for k, v in _L1_ffn_all.items() if k in ('w_r1', 'b_r1', 'w_r2', 'b_r2', 'w_h1', 'b_h1', 'w_h2', 'b_h2', 'expert_w1', 'expert_b1', 'expert_w2', 'expert_b2', 'w_s1', 'b_s1', 'w_s2', 'b_s2', 'shared_weight', 'w_f1', 'b_f1', 'w_f2', 'b_f2', 'integration_weight', 'mu')}
    del _L1_ffn_all

    def _L2_xattn_setup():
        import jax, jax.numpy as jnp
        import numpy as np
        EMBED_DIM = 128
        NUM_HEADS = 16
        HEAD_DIM = EMBED_DIM // NUM_HEADS
        key = jax.random.key(seed)
        ks = jax.random.split(key, 11)
        s = 1.0 / np.sqrt(EMBED_DIM)
        inp = {'query': jax.random.normal(ks[0], (4, 256, EMBED_DIM), jnp.float32), 'key': jax.random.normal(ks[1], (4, 256, EMBED_DIM), jnp.float32), 'value': jax.random.normal(ks[2], (4, 256, EMBED_DIM), jnp.float32), 'Wq': jax.random.uniform(ks[3], (EMBED_DIM, EMBED_DIM), jnp.float32, -s, s), 'bq': jax.random.uniform(ks[4], (EMBED_DIM,), jnp.float32, -s, s), 'Wk': jax.random.uniform(ks[5], (EMBED_DIM, EMBED_DIM), jnp.float32, -s, s), 'bk': jax.random.uniform(ks[6], (EMBED_DIM,), jnp.float32, -s, s), 'Wv': jax.random.uniform(ks[7], (EMBED_DIM, EMBED_DIM), jnp.float32, -s, s), 'bv': jax.random.uniform(ks[8], (EMBED_DIM,), jnp.float32, -s, s), 'Wo': jax.random.uniform(ks[9], (EMBED_DIM, EMBED_DIM), jnp.float32, -s, s), 'bo': jax.random.uniform(ks[10], (EMBED_DIM,), jnp.float32, -s, s)}
        return inp
    _L2_xattn_all = _L2_xattn_setup()
    _L2_xattn_in = {k: v for k, v in _L2_xattn_all.items() if k in ('Wq', 'bq', 'Wk', 'bk', 'Wv', 'bv', 'Wo', 'bo')}
    del _L2_xattn_all

    def _L2_ffn_setup():
        import jax, jax.numpy as jnp
        import numpy as np

        def _ste(w, w_q):
            return w + jax.lax.stop_gradient(w_q - w)

        def quantize_w8_per(w, axis):
            amax = jnp.clip(jnp.max(jnp.abs(w), axis=axis, keepdims=True), 1e-08, None)
            scale = 127.0 / amax
            w_q = jnp.clip(jnp.round(w * scale), -128.0, 127.0) / scale
            return _ste(w, w_q)

        def quantize_a16(x):
            amax = jnp.clip(jnp.max(jnp.abs(x)), 1e-08, None)
            scale = 32767.0 / amax
            x_q = jnp.clip(jnp.round(x * scale), -32768.0, 32767.0) / scale
            return _ste(x, x_q)
        key = jax.random.key(seed)
        k1, k2, k3 = jax.random.split(key, 3)
        d_model, d_ff = (128, 512)
        x = jax.random.normal(k1, (4, 256, d_model), dtype=jnp.float32)
        W_in = jax.random.normal(k2, (d_model, d_ff), dtype=jnp.float32) / np.sqrt(d_model)
        b_in = jnp.zeros((d_ff,), dtype=jnp.float32)
        W_out = jax.random.normal(k3, (d_ff, d_model), dtype=jnp.float32) / np.sqrt(d_ff)
        b_out = jnp.zeros((d_model,), dtype=jnp.float32)
        return {'x': x, 'W_in': W_in, 'b_in': b_in, 'W_out': W_out, 'b_out': b_out}
    _L2_ffn_all = _L2_ffn_setup()
    _L2_ffn_in = {k: v for k, v in _L2_ffn_all.items() if k in ('W_in', 'b_in', 'W_out', 'b_out')}
    del _L2_ffn_all

    def _L3_xattn_setup():
        import jax, jax.numpy as jnp
        import numpy as np
        from jax import lax
        E = 128
        H = 16
        DH = E // H
        TOP_K = 64
        WIN = 32
        key = jax.random.key(seed)
        ks = jax.random.split(key, 12)
        B, S = (2, 256)
        std = 1.0 / np.sqrt(E)
        inp = {'query': jax.random.normal(ks[0], (B, S, E), jnp.float32), 'key': jax.random.normal(ks[1], (B, S, E), jnp.float32), 'value': jax.random.normal(ks[2], (B, S, E), jnp.float32), 'Wq': jax.random.normal(ks[3], (E, E), jnp.float32) * std, 'bq': jnp.zeros((E,), jnp.float32), 'Wk': jax.random.normal(ks[4], (E, E), jnp.float32) * std, 'bk': jnp.zeros((E,), jnp.float32), 'Wv': jax.random.normal(ks[5], (E, E), jnp.float32) * std, 'bv': jnp.zeros((E,), jnp.float32), 'Wo': jax.random.normal(ks[6], (E, E), jnp.float32) * std, 'bo': jnp.zeros((E,), jnp.float32)}
        return inp
    _L3_xattn_all = _L3_xattn_setup()
    _L3_xattn_in = {k: v for k, v in _L3_xattn_all.items() if k in ('Wq', 'bq', 'Wk', 'bk', 'Wv', 'bv', 'Wo', 'bo')}
    del _L3_xattn_all

    def _L3_ffn_setup():
        import jax, jax.numpy as jnp
        import numpy as np
        D_MODEL = 128
        N_EXPERTS = 8
        TOP_K = 2
        B, S = (4, 256)
        key = jax.random.key(seed)
        k_x, k_g, k_w = jax.random.split(key, 3)
        x = jax.random.normal(k_x, (B, S, D_MODEL), dtype=jnp.float32)
        gate_w = jax.random.normal(k_g, (N_EXPERTS, D_MODEL), dtype=jnp.float32) * (1.0 / np.sqrt(D_MODEL))
        bound = float(np.sqrt(6.0 / (D_MODEL + D_MODEL)))
        weight = jax.random.uniform(k_w, (N_EXPERTS, D_MODEL, D_MODEL), dtype=jnp.float32, minval=-bound, maxval=bound)
        return {'x': x, 'gate_w': gate_w, 'weight': weight}
    _L3_ffn_all = _L3_ffn_setup()
    _L3_ffn_in = {k: v for k, v in _L3_ffn_all.items() if k in ('gate_w', 'weight')}
    del _L3_ffn_all
    return {'x': x, 'ctx_1024': ctx_1024, 'L0_xattn_ln1_g': _L0_xattn_in['ln1_g'], 'L0_xattn_ln1_b': _L0_xattn_in['ln1_b'], 'L0_xattn_ln2_g': _L0_xattn_in['ln2_g'], 'L0_xattn_ln2_b': _L0_xattn_in['ln2_b'], 'L0_xattn_Wq': _L0_xattn_in['Wq'], 'L0_xattn_Wkv': _L0_xattn_in['Wkv'], 'L0_xattn_Wo': _L0_xattn_in['Wo'], 'L0_ffn_ln_gamma': _L0_ffn_in['ln_gamma'], 'L0_ffn_ln_beta': _L0_ffn_in['ln_beta'], 'L0_ffn_fc1_q': _L0_ffn_in['fc1_q'], 'L0_ffn_fc1_scales': _L0_ffn_in['fc1_scales'], 'L0_ffn_fc1_bias': _L0_ffn_in['fc1_bias'], 'L0_ffn_fc2_q': _L0_ffn_in['fc2_q'], 'L0_ffn_fc2_scales': _L0_ffn_in['fc2_scales'], 'L0_ffn_fc2_bias': _L0_ffn_in['fc2_bias'], 'L1_xattn_Wq': _L1_xattn_in['Wq'], 'L1_xattn_bq': _L1_xattn_in['bq'], 'L1_xattn_Wk': _L1_xattn_in['Wk'], 'L1_xattn_bk': _L1_xattn_in['bk'], 'L1_xattn_Wv': _L1_xattn_in['Wv'], 'L1_xattn_bv': _L1_xattn_in['bv'], 'L1_xattn_Wo': _L1_xattn_in['Wo'], 'L1_xattn_bo': _L1_xattn_in['bo'], 'L1_ffn_w_r1': _L1_ffn_in['w_r1'], 'L1_ffn_b_r1': _L1_ffn_in['b_r1'], 'L1_ffn_w_r2': _L1_ffn_in['w_r2'], 'L1_ffn_b_r2': _L1_ffn_in['b_r2'], 'L1_ffn_w_h1': _L1_ffn_in['w_h1'], 'L1_ffn_b_h1': _L1_ffn_in['b_h1'], 'L1_ffn_w_h2': _L1_ffn_in['w_h2'], 'L1_ffn_b_h2': _L1_ffn_in['b_h2'], 'L1_ffn_expert_w1': _L1_ffn_in['expert_w1'], 'L1_ffn_expert_b1': _L1_ffn_in['expert_b1'], 'L1_ffn_expert_w2': _L1_ffn_in['expert_w2'], 'L1_ffn_expert_b2': _L1_ffn_in['expert_b2'], 'L1_ffn_w_s1': _L1_ffn_in['w_s1'], 'L1_ffn_b_s1': _L1_ffn_in['b_s1'], 'L1_ffn_w_s2': _L1_ffn_in['w_s2'], 'L1_ffn_b_s2': _L1_ffn_in['b_s2'], 'L1_ffn_shared_weight': _L1_ffn_in['shared_weight'], 'L1_ffn_w_f1': _L1_ffn_in['w_f1'], 'L1_ffn_b_f1': _L1_ffn_in['b_f1'], 'L1_ffn_w_f2': _L1_ffn_in['w_f2'], 'L1_ffn_b_f2': _L1_ffn_in['b_f2'], 'L1_ffn_integration_weight': _L1_ffn_in['integration_weight'], 'L1_ffn_mu': _L1_ffn_in['mu'], 'L2_xattn_Wq': _L2_xattn_in['Wq'], 'L2_xattn_bq': _L2_xattn_in['bq'], 'L2_xattn_Wk': _L2_xattn_in['Wk'], 'L2_xattn_bk': _L2_xattn_in['bk'], 'L2_xattn_Wv': _L2_xattn_in['Wv'], 'L2_xattn_bv': _L2_xattn_in['bv'], 'L2_xattn_Wo': _L2_xattn_in['Wo'], 'L2_xattn_bo': _L2_xattn_in['bo'], 'L2_ffn_W_in': _L2_ffn_in['W_in'], 'L2_ffn_b_in': _L2_ffn_in['b_in'], 'L2_ffn_W_out': _L2_ffn_in['W_out'], 'L2_ffn_b_out': _L2_ffn_in['b_out'], 'L3_xattn_Wq': _L3_xattn_in['Wq'], 'L3_xattn_bq': _L3_xattn_in['bq'], 'L3_xattn_Wk': _L3_xattn_in['Wk'], 'L3_xattn_bk': _L3_xattn_in['bk'], 'L3_xattn_Wv': _L3_xattn_in['Wv'], 'L3_xattn_bv': _L3_xattn_in['bv'], 'L3_xattn_Wo': _L3_xattn_in['Wo'], 'L3_xattn_bo': _L3_xattn_in['bo'], 'L3_ffn_gate_w': _L3_ffn_in['gate_w'], 'L3_ffn_weight': _L3_ffn_in['weight']}

def reference(x, ctx_1024, L0_xattn_ln1_g, L0_xattn_ln1_b, L0_xattn_ln2_g, L0_xattn_ln2_b, L0_xattn_Wq, L0_xattn_Wkv, L0_xattn_Wo, L0_ffn_ln_gamma, L0_ffn_ln_beta, L0_ffn_fc1_q, L0_ffn_fc1_scales, L0_ffn_fc1_bias, L0_ffn_fc2_q, L0_ffn_fc2_scales, L0_ffn_fc2_bias, L1_xattn_Wq, L1_xattn_bq, L1_xattn_Wk, L1_xattn_bk, L1_xattn_Wv, L1_xattn_bv, L1_xattn_Wo, L1_xattn_bo, L1_ffn_w_r1, L1_ffn_b_r1, L1_ffn_w_r2, L1_ffn_b_r2, L1_ffn_w_h1, L1_ffn_b_h1, L1_ffn_w_h2, L1_ffn_b_h2, L1_ffn_expert_w1, L1_ffn_expert_b1, L1_ffn_expert_w2, L1_ffn_expert_b2, L1_ffn_w_s1, L1_ffn_b_s1, L1_ffn_w_s2, L1_ffn_b_s2, L1_ffn_shared_weight, L1_ffn_w_f1, L1_ffn_b_f1, L1_ffn_w_f2, L1_ffn_b_f2, L1_ffn_integration_weight, L1_ffn_mu, L2_xattn_Wq, L2_xattn_bq, L2_xattn_Wk, L2_xattn_bk, L2_xattn_Wv, L2_xattn_bv, L2_xattn_Wo, L2_xattn_bo, L2_ffn_W_in, L2_ffn_b_in, L2_ffn_W_out, L2_ffn_b_out, L3_xattn_Wq, L3_xattn_bq, L3_xattn_Wk, L3_xattn_bk, L3_xattn_Wv, L3_xattn_bv, L3_xattn_Wo, L3_xattn_bo, L3_ffn_gate_w, L3_ffn_weight):
    import jax
    import jax.numpy as jnp

    def _L0_xattn_ref(image_embeds, latents, ln1_g, ln1_b, ln2_g, ln2_b, Wq, Wkv, Wo):
        import jax, jax.numpy as jnp
        import numpy as np
        DIM = 128
        DIM_HEAD = 64
        HEADS = 16
        INNER = DIM_HEAD * HEADS
        EPS = 1e-05

        def layer_norm(x, g, b):
            m = jnp.mean(x, axis=-1, keepdims=True)
            v = jnp.mean(jnp.square(x - m), axis=-1, keepdims=True)
            return (x - m) * jax.lax.rsqrt(v + EPS) * g + b
        B, S_lat, _ = latents.shape
        x = layer_norm(image_embeds, ln1_g, ln1_b)
        l = layer_norm(latents, ln2_g, ln2_b)
        q = l @ Wq
        kv_in = jnp.concatenate([x, l], axis=1)
        kv = kv_in @ Wkv
        k, v = jnp.split(kv, 2, axis=-1)

        def to_heads(t):
            return t.reshape(t.shape[0], t.shape[1], HEADS, DIM_HEAD).transpose(0, 2, 1, 3)
        q, k, v = (to_heads(q), to_heads(k), to_heads(v))
        scale = 1.0 / np.sqrt(np.sqrt(DIM_HEAD))
        w = jnp.einsum('bhqd,bhkd->bhqk', q * scale, k * scale)
        w = jax.nn.softmax(w.astype(jnp.float32), axis=-1).astype(q.dtype)
        out = jnp.einsum('bhqk,bhkd->bhqd', w, v)
        out = out.transpose(0, 2, 1, 3).reshape(B, S_lat, INNER)
        return out @ Wo

    def _L0_ffn_ref(x, ln_gamma, ln_beta, fc1_q, fc1_scales, fc1_bias, fc2_q, fc2_scales, fc2_bias):
        import jax, jax.numpy as jnp
        import numpy as np
        B, S, H, F, G = (8, 256, 128, 512, 128)
        EPS = 1e-05

        def _dequant(q, scales, g):
            K, N = q.shape
            w = (q.astype(jnp.float32) - 128.0).reshape(K // g, g, N) * scales[:, None, :]
            return w.reshape(K, N)
        residual = x
        mu = jnp.mean(x, axis=-1, keepdims=True)
        var = jnp.mean(jnp.square(x - mu), axis=-1, keepdims=True)
        h = (x - mu) * jax.lax.rsqrt(var + EPS) * ln_gamma + ln_beta
        hf = h.reshape(-1, H)
        w1 = _dequant(fc1_q, fc1_scales, G)
        y = hf @ w1 + fc1_bias
        y = jax.nn.silu(y)
        w2 = _dequant(fc2_q, fc2_scales, G)
        z = y @ w2 + fc2_bias
        return residual + 0.5 * z.reshape(residual.shape)

    def _L1_xattn_ref(x, content_embeddings, Wq, bq, Wk, bk, Wv, bv, Wo, bo):
        import jax, jax.numpy as jnp
        import numpy as np
        C = 128
        B, SQ, SKV = (4, 256, 256)
        queries = x @ Wq.T + bq
        keys = content_embeddings @ Wk.T + bk
        values = content_embeddings @ Wv.T + bv
        scale = 1.0 / jnp.sqrt(jnp.asarray(C, x.dtype))
        scores = jnp.einsum('bqc,bkc->bqk', queries, keys) * scale
        attn = jax.nn.softmax(scores, axis=-1)
        attended = jnp.einsum('bqk,bkc->bqc', attn, values)
        out = x + attended
        return out @ Wo.T + bo

    def _L1_ffn_ref(x, w_r1, b_r1, w_r2, b_r2, w_h1, b_h1, w_h2, b_h2, expert_w1, expert_b1, expert_w2, expert_b2, w_s1, b_s1, w_s2, b_s2, shared_weight, w_f1, b_f1, w_f2, b_f2, integration_weight, mu):
        import jax, jax.numpy as jnp
        import numpy as np
        D = 128
        E = 8
        K = 2
        NUM_ITER = 2
        DT = 0.1
        H = 64
        CTX = 2 * D

        def _gelu(t):
            return jax.nn.gelu(t, approximate=False)

        def _inl(ctrl, x, v, mu):
            alpha_raw, beta_raw, gate_raw = jnp.split(ctrl, 3, axis=-1)
            alpha = jax.nn.sigmoid(alpha_raw)
            beta = jax.nn.softplus(beta_raw)
            gate = jax.nn.sigmoid(gate_raw)
            error = x - mu
            v_next = alpha * v - beta * error
            x_next = x + DT * gate * v_next
            return (x_next, v_next)
        B, N, Dm = x.shape
        xf = x.reshape(B * N, Dm)
        logits = _gelu(xf @ w_r1 + b_r1) @ w_r2 + b_r2
        probs = jax.nn.softmax(logits, axis=-1)
        top_p, top_i = jax.lax.top_k(probs, K)
        top_p = top_p / jnp.sum(top_p, axis=-1, keepdims=True)
        flat_idx = top_i.reshape(-1)
        flat_w = top_p.reshape(-1, 1)
        v = jnp.zeros_like(xf)
        integrated = xf
        for _ in range(NUM_ITER):
            ctx = jnp.concatenate([integrated, v], axis=-1)
            shared_ctrl = _gelu(ctx @ w_s1 + b_s1) @ w_s2 + b_s2
            x_shared, v_shared = _inl(shared_ctrl, integrated, v, mu)
            sw = jax.nn.sigmoid(shared_weight)
            ctx_e = jnp.repeat(ctx, K, axis=0)
            x_e = jnp.repeat(integrated, K, axis=0)
            v_e = jnp.repeat(v, K, axis=0)
            w1 = expert_w1[flat_idx]
            b1 = expert_b1[flat_idx]
            w2 = expert_w2[flat_idx]
            b2 = expert_b2[flat_idx]
            hidden = _gelu(jnp.einsum('tc,tch->th', ctx_e, w1) + b1)
            ctrl = jnp.einsum('th,tho->to', hidden, w2) + b2
            x_r, v_r = _inl(ctrl, x_e, v_e, mu)
            x_r = (x_r * flat_w).reshape(B * N, K, Dm).sum(axis=1)
            v_r = (v_r * flat_w).reshape(B * N, K, Dm).sum(axis=1)
            x_next = sw * x_shared + (1.0 - sw) * x_r
            v_next = sw * v_shared + (1.0 - sw) * v_r
            halt = jax.nn.sigmoid(_gelu(x_next @ w_h1 + b_h1) @ w_h2 + b_h2)
            refined = _gelu(x_next @ w_f1 + b_f1) @ w_f2 + b_f2
            integrated = integrated + halt * refined * integration_weight
            v = v_next
        return integrated.reshape(B, N, Dm)

    def _L2_xattn_ref(query, key, value, Wq, bq, Wk, bk, Wv, bv, Wo, bo):
        import jax, jax.numpy as jnp
        import numpy as np
        EMBED_DIM = 128
        NUM_HEADS = 16
        HEAD_DIM = EMBED_DIM // NUM_HEADS
        B, T, E = query.shape
        S = key.shape[1]
        H, D = (NUM_HEADS, HEAD_DIM)
        q = (query @ Wq.T + bq).reshape(B, T, H, D).transpose(0, 2, 1, 3)
        k = (key @ Wk.T + bk).reshape(B, S, H, D).transpose(0, 2, 1, 3)
        v = (value @ Wv.T + bv).reshape(B, S, H, D).transpose(0, 2, 1, 3)
        scores = jnp.einsum('bhtd,bhsd->bhts', q, k) / np.sqrt(D)
        causal = jnp.triu(jnp.full((T, S), -jnp.inf, jnp.float32), k=1)
        scores = scores + causal[None, None]
        attn = jax.nn.softmax(scores, axis=-1)
        out = jnp.einsum('bhts,bhsd->bhtd', attn, v)
        out = out.transpose(0, 2, 1, 3).reshape(B, T, E)
        out = out @ Wo.T + bo
        return out

    def _L2_ffn_ref(x, W_in, b_in, W_out, b_out):
        import jax, jax.numpy as jnp
        import numpy as np

        def _ste(w, w_q):
            return w + jax.lax.stop_gradient(w_q - w)

        def quantize_w8_per(w, axis):
            amax = jnp.clip(jnp.max(jnp.abs(w), axis=axis, keepdims=True), 1e-08, None)
            scale = 127.0 / amax
            w_q = jnp.clip(jnp.round(w * scale), -128.0, 127.0) / scale
            return _ste(w, w_q)

        def quantize_a16(x):
            amax = jnp.clip(jnp.max(jnp.abs(x)), 1e-08, None)
            scale = 32767.0 / amax
            x_q = jnp.clip(jnp.round(x * scale), -32768.0, 32767.0) / scale
            return _ste(x, x_q)
        W_in_sim = quantize_w8_per(W_in, axis=0)
        W_out_sim = quantize_w8_per(W_out, axis=1)
        x_sim = quantize_a16(x)
        hidden = jax.nn.gelu(x_sim @ W_in_sim + b_in, approximate=False)
        hidden_sim = quantize_a16(hidden)
        out = hidden_sim @ W_out_sim + b_out
        return out

    def _L3_xattn_ref(query, key, value, Wq, bq, Wk, bk, Wv, bv, Wo, bo):
        import jax, jax.numpy as jnp
        import numpy as np
        from jax import lax
        E = 128
        H = 16
        DH = E // H
        TOP_K = 64
        WIN = 32
        B, S, _ = query.shape
        q = (query @ Wq.T + bq).reshape(B, S, H, DH).transpose(0, 2, 1, 3)
        k = (key @ Wk.T + bk).reshape(B, S, H, DH).transpose(0, 2, 1, 3)
        v = (value @ Wv.T + bv).reshape(B, S, H, DH).transpose(0, 2, 1, 3)
        scale = jnp.asarray(1.0 / np.sqrt(DH), q.dtype)
        scores = jnp.einsum('bhqd,bhkd->bhqk', q, k) * scale
        idx = jnp.arange(S)
        outside = (jnp.abs(idx[:, None] - idx[None, :]) > WIN // 2).astype(scores.dtype)
        scores = scores + outside
        kth = lax.top_k(scores, TOP_K)[0][..., -1:]
        scores = jnp.where(scores >= kth, scores, jnp.zeros((), scores.dtype))
        attn = jax.nn.softmax(scores, axis=-1)
        out = jnp.einsum('bhqk,bhkd->bhqd', attn, v)
        out = out.transpose(0, 2, 1, 3).reshape(B, S, H * DH)
        return out @ Wo.T + bo

    def _L3_ffn_ref(x, gate_w, weight):
        import jax, jax.numpy as jnp
        import numpy as np
        D_MODEL = 128
        N_EXPERTS = 8
        TOP_K = 2
        B, S = (4, 256)
        logits = jnp.einsum('bsd,ed->bse', x, gate_w)
        topk_vals, topk_idx = jax.lax.top_k(logits, TOP_K)
        topk_weights = jax.nn.softmax(topk_vals, axis=-1)
        one_hot = jax.nn.one_hot(topk_idx, N_EXPERTS, dtype=x.dtype)
        weights_full = jnp.einsum('bsk,bske->bse', topk_weights, one_hot)
        expert_out = jnp.einsum('bsd,edh->bseh', x, weight)
        out = jnp.einsum('bse,bseh->bsh', weights_full, expert_out)
        return out
    x = x + _L0_xattn_ref(ctx_1024, _layernorm(x, axis=-1), L0_xattn_ln1_g, L0_xattn_ln1_b, L0_xattn_ln2_g, L0_xattn_ln2_b, L0_xattn_Wq, L0_xattn_Wkv, L0_xattn_Wo)
    x = x + _L0_ffn_ref(_layernorm(x, axis=-1), L0_ffn_ln_gamma, L0_ffn_ln_beta, L0_ffn_fc1_q, L0_ffn_fc1_scales, L0_ffn_fc1_bias, L0_ffn_fc2_q, L0_ffn_fc2_scales, L0_ffn_fc2_bias)
    x = x + _L1_xattn_ref(_layernorm(x, axis=-1), ctx_1024, L1_xattn_Wq, L1_xattn_bq, L1_xattn_Wk, L1_xattn_bk, L1_xattn_Wv, L1_xattn_bv, L1_xattn_Wo, L1_xattn_bo)
    x = x + _L1_ffn_ref(_layernorm(x, axis=-1), L1_ffn_w_r1, L1_ffn_b_r1, L1_ffn_w_r2, L1_ffn_b_r2, L1_ffn_w_h1, L1_ffn_b_h1, L1_ffn_w_h2, L1_ffn_b_h2, L1_ffn_expert_w1, L1_ffn_expert_b1, L1_ffn_expert_w2, L1_ffn_expert_b2, L1_ffn_w_s1, L1_ffn_b_s1, L1_ffn_w_s2, L1_ffn_b_s2, L1_ffn_shared_weight, L1_ffn_w_f1, L1_ffn_b_f1, L1_ffn_w_f2, L1_ffn_b_f2, L1_ffn_integration_weight, L1_ffn_mu)
    x = x + _L2_xattn_ref(_layernorm(x, axis=-1), ctx_1024, ctx_1024, L2_xattn_Wq, L2_xattn_bq, L2_xattn_Wk, L2_xattn_bk, L2_xattn_Wv, L2_xattn_bv, L2_xattn_Wo, L2_xattn_bo)
    x = x + _L2_ffn_ref(_layernorm(x, axis=-1), L2_ffn_W_in, L2_ffn_b_in, L2_ffn_W_out, L2_ffn_b_out)
    x = x + _L3_xattn_ref(_layernorm(x, axis=-1), ctx_1024, ctx_1024, L3_xattn_Wq, L3_xattn_bq, L3_xattn_Wk, L3_xattn_bk, L3_xattn_Wv, L3_xattn_bv, L3_xattn_Wo, L3_xattn_bo)
    x = x + _L3_ffn_ref(_layernorm(x, axis=-1), L3_ffn_gate_w, L3_ffn_weight)
    return x

_drawn_inputs = setup_inputs


def setup_inputs(seed=0):
    import zlib

    import numpy as np

    out = dict(_drawn_inputs(seed))
    spreads = {'L0_xattn_ln1_g': (1.0, 0.2),
     'L0_xattn_ln1_b': (0.0, 0.1),
     'L0_xattn_ln2_g': (1.0, 0.2),
     'L0_xattn_ln2_b': (0.0, 0.1),
     'L0_ffn_ln_gamma': (1.0, 0.2),
     'L0_ffn_ln_beta': (0.0, 0.1),
     'L1_xattn_bq': (0.0, 0.8),
     'L1_xattn_bk': (0.0, 0.8),
     'L1_xattn_bv': (0.0, 0.8),
     'L1_xattn_bo': (0.0, 0.8),
     'L1_ffn_b_r1': (0.0, 0.8),
     'L1_ffn_b_r2': (0.0, 0.8),
     'L1_ffn_b_h1': (0.0, 0.8),
     'L1_ffn_expert_b1': (0.0, 0.8),
     'L1_ffn_expert_b2': (0.0, 0.8),
     'L1_ffn_b_s1': (0.0, 0.8),
     'L1_ffn_b_s2': (0.0, 0.8),
     'L1_ffn_b_f1': (0.0, 0.8),
     'L1_ffn_b_f2': (0.0, 0.8),
     'L1_ffn_integration_weight': (0.5, 0.6),
     'L1_ffn_mu': (0.0, 0.8),
     'L2_ffn_b_in': (0.0, 0.8),
     'L2_ffn_b_out': (0.0, 0.8),
     'L3_xattn_bq': (0.0, 0.8),
     'L3_xattn_bk': (0.0, 0.8),
     'L3_xattn_bv': (0.0, 0.8),
     'L3_xattn_bo': (0.0, 0.8)}
    factors = {'L0_ffn_fc1_scales': 3.633,
     'L0_ffn_fc1_bias': 8.0,
     'L0_ffn_fc2_bias': 8.0,
     'L1_xattn_Wq': 8.0,
     'L1_xattn_Wk': 8.0,
     'L1_xattn_Wv': 8.0,
     'L1_xattn_Wo': 8.0,
     'L1_ffn_w_r1': 8.0,
     'L1_ffn_w_r2': 8.0,
     'L1_ffn_w_h1': 8.0,
     'L1_ffn_w_h2': 8.0,
     'L1_ffn_expert_w1': 8.0,
     'L1_ffn_expert_w2': 8.0,
     'L1_ffn_w_s1': 8.0,
     'L1_ffn_w_s2': 8.0,
     'L1_ffn_w_f1': 8.0,
     'L1_ffn_w_f2': 8.0,
     'L2_xattn_Wq': 8.0,
     'L2_xattn_bq': 8.0,
     'L2_xattn_Wk': 8.0,
     'L2_xattn_bk': 8.0,
     'L2_xattn_Wv': 8.0,
     'L2_xattn_bv': 8.0,
     'L2_xattn_Wo': 8.0,
     'L2_xattn_bo': 8.0,
     'L2_ffn_W_in': 8.0,
     'L2_ffn_W_out': 8.0,
     'L3_xattn_Wq': 8.0,
     'L3_xattn_Wk': 8.0,
     'L3_xattn_Wv': 8.0,
     'L3_xattn_Wo': 8.0,
     'L3_ffn_gate_w': 8.0,
     'L3_ffn_weight': 8.0}
    for name, (base, spread) in spreads.items():
        noise = np.random.default_rng([zlib.crc32(name.encode()), seed]).standard_normal(out[name].shape)
        drawn = base * np.exp(spread * noise) if base else spread * noise
        out[name] = jnp.asarray(drawn.astype(out[name].dtype))
    for name, factor in factors.items():
        out[name] = (out[name] * factor).astype(out[name].dtype)
    return out
```

```python
from contextlib import ExitStack

import numpy as np
import concourse.bass as bass
from concourse import mybir

F32 = mybir.dt.float32
BF16 = mybir.dt.bfloat16
I32 = mybir.dt.int32
U32 = mybir.dt.uint32
ALU = mybir.AluOpType
ACT = mybir.ActivationFunctionType
AX = mybir.AxisListType

B, S, D = 32, 64, 128
P = 128
TILES = B * S // P
BANKS = 8
EPS = 1e-5
OFF = -1e30

H0, DH0 = 16, 64
H2 = 16
DH2 = D // H2
WIN = 32
F0 = 512
FC = F0 // P
E, HE = 8, 64
EC = E * HE // P
C1 = 512
MAGIC = 12582912.0


class At:

    def __init__(self, n, pair=None):
        self.n, self.pair = n, pair

    def __sub__(self, k):
        return At(self.n - k, self.pair)

    def times(self, a, b=0):
        v = a * self.n + b
        return v if self.pair is None else self.pair * (2 * a) + v

    def valid(self, tiles):
        return 0 <= self.n < tiles


class Banks:

    def __init__(self):
        self.count = [0] * BANKS

    def plan(self, order, tiles, last):
        fills = Fills({job: b if isinstance(b, tuple) else (b, b) for job, b, _ in order})
        for step in range(tiles + last):
            for job, _, lag in order:
                if 0 <= step - lag < tiles:
                    k = fills.banks[job][(step - lag) % 2]
                    fills.at[job, step - lag] = self.count[k]
                    self.count[k] += 1
        fills.per_pair = [sum((b[0] == k) + (b[1] == k) for b in fills.banks.values()) for k in range(BANKS)]
        return fills

    def plan_chunks(self, jobs, place, before, body, after, pairs):
        fills = Fills({})
        for (job, parity), k in place.items():
            fills.banks.setdefault(job, [None, None])[parity] = k
        loops = [[(x, n + 2 * p) for x, n in body] for p in range(pairs - 1)]
        for x, n in before + [xn for loop in loops for xn in loop] + after:
            for job in jobs.get(x, []):
                k = place[job, n % 2]
                fills.at[job, n] = self.count[k]
                self.count[k] += 1
        fills.per_pair = [sum(place[job, n % 2] == k for x, n in body for job in jobs.get(x, [])) for k in range(BANKS)]
        return fills


class Fills:
    def __init__(self, banks):
        self.at, self.banks, self.per_pair = {}, banks, None

    def bank(self, job, t):
        return self.banks[job][t.n % 2]

    def before(self, job, t, more=0):
        v = self.at[job, t.n] + more
        return v if t.pair is None else t.pair * self.per_pair[self.bank(job, t)] + v


def run_steps(engine, tiles, last, body):
    lead = last + last % 2
    for n in range(lead):
        body(At(n))
    if tiles > lead:
        with engine.Fori(0, (tiles - lead) // 2) as pair:
            body(At(lead, pair))
            body(At(lead + 1, pair))
    for n in range(max(tiles, lead), tiles + last):
        body(At(n))


def pack(parts):
    at, n = {}, 0
    for name, width in parts:
        at[name] = (n, width)
        n += width
    return at, n


VECS, NVECS = pack([
    ("ln1_g", 1), ("ln1_b", 1), ("ln2_g", 1), ("ln2_b", 1), ("f0_g", 1), ("f0_b", 1), ("f0_b1", FC),
    ("a1_bq", 1), ("a1_bk", 1), ("a1_bv", 1), ("a2_bq", 1), ("a2_bk", 1), ("a2_bv", 1),
    ("a3_bq", 1), ("a3_bk", 1), ("a3_bv", 1), ("f2_bin", FC),
    ("b_r1", 1), ("b_h1", 1), ("b_h2", 1), ("b_e1", EC), ("b_s1", 1), ("b_s2", 3), ("b_f1", 2),
    ("b_f2", 1), ("iw", 1), ("mu", 1), ("shared", 1),
])
ROWS, NROWS = pack([("f0_b2", D), ("a1_bo", D), ("a2_bo", D), ("a3_bo", D), ("f2_bo", D),
                    ("f0_s1", F0), ("f0_s2", FC * D), ("b_r2", E)])
W0, NW0 = pack([("q", 1024), ("k", 1024), ("v", 1024), ("o", 1024)])
WA, NWA = pack([(f"{a}{w}", D) for a in ("a1", "a2", "a3") for w in "qkvo"])
W1F, NW1F = pack([("e1x", 512), ("e1v", 512), ("e2", EC * 384), ("s1x", HE), ("s1v", HE), ("s2", 384),
                  ("r1", 32), ("r2", E), ("h1", 32), ("h2", P), ("f1", 256), ("f2", 256)])
W2F, NW2F = pack([("in", F0), ("out", F0)])
W3F, NW3F = pack([("gate", E), ("w", E * D)])
CONST, NCONST = pack([("ident", P), ("two", HE), ("head", H2), ("half", 2), ("iota", E), ("m1", P),
                      ("m2", S), ("m3", S), ("sel", EC * P), ("selw", 2 * P)])


def build(nc, A, out, stop=99):
    banks = Banks()
    ctx = ExitStack()
    with ctx:
        def sb(name, shape, dt=F32):
            return ctx.enter_context(nc.sbuf_tensor(name, shape, dt))

        sems = {}

        def sem(name):
            if name not in sems:
                sems[name] = ctx.enter_context(nc.semaphore(name))
            return sems[name]

        x_tok = sb("x_tok", [P, TILES * D])
        lnT = sb("lnT", [P, B * S])
        cT = sb("cT", [P, B * S])
        ctx_tok = sb("ctx_tok", [P, TILES * D])
        vecs = sb("vecs", [P, NVECS])
        rows = sb("rows", [P, NROWS])
        w0 = sb("w0", [P, NW0])
        wa = sb("wa", [P, NWA])
        w1f = sb("w1f", [P, NW1F])
        w2f = w0[:, 0:NW2F]
        w3f = w0[:, NW2F:NW2F + NW3F]
        const = sb("const", [P, NCONST])
        w0q = sb("w0q", [P, 2, F0], I32)

        def col(table, at, name, i=0, n=1):
            s, _ = at[name]
            return table[:, s + i:s + i + n]

        def vec(name, i=0):
            return col(vecs, VECS, name, i)

        def over(table, sizes):
            views, n = [], 0
            for size in sizes:
                views.append(table[:, n:n + size])
                n += size
            return views

        def mat(table, at, name):
            s, n = at[name]
            return table[:, s:s + n]

        ident = mat(const, CONST, "ident")

        identb = sb("identb", [P, P], BF16)
        m1b = sb("m1b", [P, P], BF16)
        m23b = sb("m23b", [P, 2, 512], BF16)
        sclA = sb("sclA", [P, H0, D])
        prjB = sb("prjB", [P, H0, D])
        f0w1 = sb("f0w1", [P, F0])
        f0w2 = sb("f0w2", [P, FC, D])
        f0hb = sb("f0hb", [P, D])
        bqs = sb("bqs", [P, 3])
        epsv = sb("epsv", [P, 2])

        selb = sb("selb", [96, EC, P], BF16)
        be2b = sb("be2b", [96, 3 * D], BF16)
        DERIVED = ("sw", "omsw", "hba", "hbg", "hbh2", "hiw", "tanh", "x")
        derived = sb("derived", [P, len(DERIVED)])

        def dv(name):
            return derived[:, DERIVED.index(name):DERIVED.index(name) + 1]

        NORMS = 5
        st = sb("st", [P, 2, NORMS, 6])
        mv = sb("mv", [P, 2, NORMS, 2])
        ve = sb("ve", [P, 2, NORMS])
        rstd = sb("rstd", [P, 2, NORMS])
        yln = sb("yln", [P, 2, NORMS, D])

        ARENA = 18 * 1024 - 512
        arena = sb("arena", [P, ARENA])
        used = {"n": 0}

        def carve(n, start=None, dt=None):
            if start is not None:
                used["n"] = start
            a = arena[:, used["n"]:used["n"] + n]
            used["n"] += n
            assert used["n"] <= ARENA, used
            return a

        be2 = arena[0:96, ARENA - 3 * D:ARENA]
        be2p = arena[0:96, ARENA - 3 * D - 9 * D // 2:ARENA - 3 * D].bitcast(BF16).rearrange("p (q o) -> p q o", q=3)

        psum = ctx.enter_context(nc.psum_tensor("psum", [P, BANKS, 512], F32))

        def ps(k, n=512, m=0):
            return psum[:, k, m:m + n]

        full = [sem(f"bank_full{k}") for k in range(BANKS)]
        free = [sem(f"bank_free{k}") for k in range(BANKS)]

        def fill(pe, plan, job, t):
            pe.wait_ge(free[plan.bank(job, t)], plan.before(job, t, 1))

        def filled(eng, plan, job, t):
            eng.wait_ge(full[plan.bank(job, t)], plan.before(job, t, 1))

        def stored(eng, plan, job, t):
            eng.wait_ge(free[plan.bank(job, t)], plan.before(job, t, 2))

        pe_parts, act_parts, dve_parts, pool_parts, sp_parts = [], [], [], [], []

        LOADS = [("x_tok", x_tok[:, :], A["x_tok"]), ("ctx_tok", ctx_tok[:, :], A["ctx_tok"]),
                 ("vecs", vecs[:, :], A["vecs"]), ("const", const[:, :], A["const"]),
                 ("w0", w0[:, :], A["w0"]), ("rows", rows[:, :], A["rows"].partition_broadcast(P)),
                 ("w0q", w0q[:, :, :], A["w0q"]), ("cT", cT[:, :], A["cT"]), ("wa", wa[:, :], A["wa"]),
                 ("w1f", w1f[:, :], A["w1f"])]
        LATER = [("w2f", w2f, A["w2f"]), ("w3f", w3f, A["w3f"])]
        loaded = {name: sem(f"loaded_{name}") for name, _, _ in LOADS + LATER}

        def have(eng, *names):
            for n in names:
                eng.wait_ge(loaded[n], 16)

        def sp_load(sp):
            for name, dst, src in LOADS:
                sp.dma_start(dst, src).then_inc(loaded[name], 16)

        def sp_load_be2(sp):
            sp.wait_ge(zeroed, 1)
            for q in range(3):
                sp.dma_start(be2[32 * q:32 * q + E, :], A["b_e2"]).then_inc(loaded_be2, 16)

        sp_parts.append(sp_load)
        sp_parts.append(sp_load_be2)

        setup_plan = banks.plan([(f"A{c}", c, 0) for c in range(4)] + [(f"B{c}", 4 + c, 0) for c in range(4)], 1, 0)
        consts_ready = sem("consts_ready")
        bqs_ready = sem("bqs_ready")
        f0w_ready = sem("f0w_ready")
        f0_int = sem("f0_int")
        f1_derived_ready = sem("f1_derived_ready")
        sw_tanh = sem("sw_tanh")
        derived_step = sem("derived_step")
        zeroed = sem("zeroed")
        loaded_be2 = sem("loaded_be2")
        T0 = At(0)

        def pool_setup(pool):
            for k in range(BANKS):
                pool.memset(epsv[:, 0:1] if k % 2 == 0 else epsv[:, 1:2], EPS if k % 2 == 0 else -0.5) \
                    .then_inc(free[k], 1) if k < 2 else pool.sem_inc(free[k], 1)
            pool.wait_ge(free[0], 1)
            pool.wait_ge(free[1], 1)
            pool.memset(be2[:, :], 0.0).then_inc(zeroed, 1)

        def pe_setup(pe):
            have(pe, "w0")
            for c in range(4):
                fill(pe, setup_plan, f"A{c}", T0)
                for j in range(4):
                    h = 8 * (c // 2) + 2 * j + c % 2
                    p = 64 * (h % 2)
                    m = nc.tensor.matmul(ps(c, D, j * D), mat(w0, W0, "q")[p:p + 64, (h // 2) * D:(h // 2 + 1) * D],
                                         mat(w0, W0, "k")[p:p + 64, (h // 2) * D:(h // 2 + 1) * D], start=True, stop=True)
                m.then_inc(full[c], 1)
            for c in range(4):
                fill(pe, setup_plan, f"B{c}", T0)
                for j in range(4):
                    h = 8 * (c // 2) + 2 * j + c % 2
                    p = 64 * (h % 2)
                    m = nc.tensor.matmul(ps(4 + c, D, j * D), mat(w0, W0, "v")[p:p + 64, (h // 2) * D:(h // 2 + 1) * D],
                                         mat(w0, W0, "o")[p:p + 64, (h // 2) * D:(h // 2 + 1) * D], start=True, stop=True)
                m.then_inc(full[4 + c], 1)

        def act_setup(act):
            act.preload_act_table(ACT.Exp)
            for c in range(4):
                filled(act, setup_plan, f"A{c}", T0)
                nc.scalar.activation(sclA[:, 8 * (c // 2) + c % 2:8 * (c // 2) + 8:2, :], ps(c).rearrange("p (h d) -> p h d", h=4), ACT.Copy, scale=1.0 / 8.0).then_inc(free[c], 1)
            have(act, "vecs")
            nc.scalar.activation(dv("tanh"), vec("shared"), ACT.Tanh, scale=0.5).then_inc(sw_tanh, 1)
            for n, scale in enumerate((D ** -0.5, DH2 ** -0.5, DH2 ** -0.5)):
                nc.scalar.activation(bqs[:, n:n + 1], vec(f"a{n + 1}_bq"), ACT.Copy, scale=scale).then_inc(bqs_ready, 1)

        def dve_setup(dve):
            have(dve, "const")
            nc.vector.tensor_copy(identb[:, :], ident)
            nc.vector.tensor_copy(m1b[:, :], mat(const, CONST, "m1"))
            for n in range(2):
                m = nc.vector.tensor_copy(m23b[:, n, :].rearrange("p (h k) -> p h k", k=S),
                                          mat(const, CONST, f"m{n + 2}").unsqueeze(1).to_broadcast((P, 8, S)))
            m.then_inc(consts_ready, 1)
            nc.vector.tensor_copy(selb[:, :, :], mat(const, CONST, "sel")[0:96, :])
            for c in range(4):
                filled(dve, setup_plan, f"B{c}", T0)
                nc.vector.tensor_copy(prjB[:, 8 * (c // 2) + c % 2:8 * (c // 2) + 8:2, :], ps(4 + c).rearrange("p (h d) -> p h d", h=4)).then_inc(free[4 + c], 1)

            have(dve, "w0q", "rows")
            nc.vector.tensor_copy(f0w1[:, :], w0q[:, 0, :]).then_inc(f0_int, 1)
            nc.vector.tensor_copy(f0w2[:, :, :], w0q[:, 1, :]).then_inc(f0_int, 1)
            nc.vector.tensor_scalar(f0hb[:, :], mat(rows, ROWS, "f0_b2"), 0.5, None, ALU.mult).then_inc(f0_int, 1)
            dve.wait_ge(f0_int, 2)
            nc.vector.scalar_tensor_tensor(out=f0w1[:, :], in0=f0w1[:, :], scalar=-128.0, in1=mat(rows, ROWS, "f0_s1"),
                                           op0=ALU.add, op1=ALU.mult).then_inc(f0w_ready, 1)
            nc.vector.tensor_scalar(f0w2[:, :, :], f0w2[:, :, :], -128.0, 0.5, ALU.add, ALU.mult).then_inc(f0_int, 1)
            dve.wait_ge(f0_int, 4)
            nc.vector.tensor_tensor(f0w2[:, :, :].rearrange("p c d -> p (c d)"), f0w2[:, :, :].rearrange("p c d -> p (c d)"),
                                    mat(rows, ROWS, "f0_s2"), ALU.mult).then_inc(f0w_ready, 1)

        def dve_setup2(dve):
            have(dve, "vecs")
            link_n = [0]

            def link(m):
                link_n[0] += 1
                m.then_inc(derived_step, 1)
                dve.wait_ge(derived_step, link_n[0])

            nc.vector.tensor_scalar(dv("hba"), vec("b_s2", 0), 0.5, None, ALU.mult)
            nc.vector.tensor_scalar(dv("hbg"), vec("b_s2", 2), 0.5, None, ALU.mult)
            nc.vector.tensor_scalar(dv("hbh2"), vec("b_h2"), 0.5, None, ALU.mult)
            nc.vector.tensor_scalar(dv("hiw"), vec("iw"), 0.5, None, ALU.mult)
            dve.wait_ge(sw_tanh, 1)
            nc.vector.tensor_scalar(dv("omsw"), dv("tanh"), -0.5, 0.5, ALU.mult, ALU.add)
            nc.vector.tensor_scalar(dv("sw"), dv("tanh"), 0.5, 0.5, ALU.mult, ALU.add).then_inc(f1_derived_ready, 1)
            dve.wait_ge(loaded_be2, 48)
            link(nc.vector.tensor_copy(be2p[:, 0, :], be2[:, :]))
            link(nc.vector.tensor_tensor(be2[:, :], be2[:, :], be2p[:, 0, :], ALU.subtract))
            link(nc.vector.tensor_copy(be2p[:, 1, :], be2[:, :]))
            link(nc.vector.tensor_tensor(be2[:, :], be2[:, :], be2p[:, 1, :], ALU.subtract))
            link(nc.vector.tensor_copy(be2p[:, 2, :], be2[:, :]))
            for q in range(3):
                m = nc.vector.tensor_copy(be2b[32 * q:32 * q + 32, :], be2p[32 * q:32 * q + 32, q, :])
            m.then_inc(f1_derived_ready, 1)

        pe_parts.append(pe_setup)
        act_parts.append(act_setup)
        dve_parts.append(dve_setup)
        dve_parts.append(dve_setup2)
        pool_parts.append(pool_setup)

        class Norm:

            def __init__(self, name, i):
                self.i, self.tiles = i, 0
                self.stats_done, self.var_done, self.eps_added, self.rstd_done, self.y_ready = (
                    sem(f"{name}_{x}") for x in ("stats", "var", "eps", "rstd", "y"))

            def take(self):
                self.tiles += TILES
                return self.tiles - TILES

            def stats(self, dve, src, t, base):
                u, n = t.n % 2, t.times(1, base + 1)
                carry(dve, "dve")
                nc.vector.bn_stats(st[:, u, self.i, :], src).then_inc(self.stats_done, 1)
                dve.wait_ge(self.stats_done, n)
                carry(dve, "dve")
                nc.vector.bn_aggr(mv[:, u, self.i, :], st[:, u, self.i, :]).then_inc(self.var_done, 1)

            def root(self, pool, t, base):
                u, n = t.n % 2, t.times(1, base + 1)
                pool.wait_ge(self.var_done, n)
                pool.tensor_tensor(ve[:, u, self.i:self.i + 1], mv[:, u, self.i, 1:2], epsv[:, 0:1], ALU.add) \
                    .then_inc(self.eps_added, 1)
                pool.wait_ge(self.eps_added, n)
                pool.tensor_tensor(rstd[:, u, self.i:self.i + 1], ve[:, u, self.i:self.i + 1], epsv[:, 1:2], ALU.pow) \
                    .then_inc(self.rstd_done, 1)

            def apply(self, dve, src, t, base):
                u, n = t.n % 2, t.times(1, base + 1)
                dve.wait_ge(self.rstd_done, n)
                nc.vector.tensor_scalar(yln[:, u, self.i, :], src, mv[:, u, self.i, 0:1], rstd[:, u, self.i:self.i + 1],
                                        ALU.subtract, ALU.mult).then_inc(self.y_ready, 1)

        def carry(eng, name):
            eng.sem_inc(sem(f"{name}_carried"), 1)

        normA = Norm("norm", 0)
        normB = Norm("norm2", 1)
        norm0 = Norm("norm0", 2)
        norm02 = Norm("norm02", 3)
        normC = Norm("normc", 4)
        normF = Norm("normf", 2)

        tails = []

        def cols(table, t, n=P):
            return table[:, t.n * n:(t.n + 1) * n] if t.pair is None else table[:, bass.ds(t.times(n), n)]

        def xt(t):
            return cols(x_tok, t)

        class Tail:

            def __init__(self, plan, bias, double=False, affine=None, ready=None, job="lnt", norm=None):
                self.job, self.norm = job, norm or normA
                self.ready = ready
                self.plan, self.bias, self.double, self.affine = plan, bias, double, affine
                self.l = len(tails)
                self.base = self.norm.take()
                self.base2 = normB.take() if double else None
                self.prev = tails[-1] if tails else None
                self.bias_added = sem(f"bias_added{self.l}")
                tails.append(self)

            def add(self, dve, t, job="out", scale=None, stats=True):
                k = self.plan.bank(job, t)
                filled(dve, self.plan, job, t)
                if self.prev is not None and self.prev.bias:
                    n = len(self.prev.bias)
                    dve.wait_ge(self.prev.bias_added, t.times(n, n))
                if scale is None:
                    nc.vector.tensor_tensor(xt(t), xt(t), ps(k, P), ALU.add).then_inc(free[k], 1)
                else:
                    nc.vector.scalar_tensor_tensor(out=xt(t), in0=ps(k, P), scalar=scale, in1=xt(t),
                                                   op0=ALU.mult, op1=ALU.add).then_inc(free[k], 1)
                if stats:
                    self.stats(dve, t, job)

            def stats(self, dve, t, job="out"):
                stored(dve, self.plan, job, t)
                self.norm.stats(dve, xt(t), t, self.base)

            def root(self, pool, t):
                self.norm.root(pool, t, self.base)

            def turned(self, dve, t):
                k = self.plan.bank(self.job, t)
                if t.n >= 2:
                    filled(dve, self.plan, self.job, t - 2)
                elif t.pair is not None:
                    dve.wait_ge(full[k], self.plan.before(self.job, t, 1 - self.plan.per_pair[k]))

            def apply(self, dve, t):
                if not self.double:
                    self.turned(dve, t)
                self.norm.apply(dve, xt(t), t, self.base)

            def add_bias(self, pool, t):
                n = len(self.bias)
                if n:
                    pool.wait_ge(self.norm.y_ready, t.times(1, self.base + 1))
                for k, b in enumerate(self.bias):
                    b = yln[:, t.n % 2, self.norm.i, :] if isinstance(b, str) else b
                    if k:
                        pool.wait_ge(self.bias_added, t.times(n, k))
                    carry(pool, "pool")
                    pool.tensor_tensor(xt(t), xt(t), b, ALU.add).then_inc(self.bias_added, 1)

            def stats2(self, dve, t):
                dve.wait_ge(self.norm.y_ready, t.times(1, self.base + 1))
                normB.stats(dve, yln[:, t.n % 2, self.norm.i, :], t, self.base2)

            def root2(self, pool, t):
                normB.root(pool, t, self.base2)

            def apply2(self, dve, t):
                self.turned(dve, t)
                normB.apply(dve, yln[:, t.n % 2, self.norm.i, :], t, self.base2)

            def turn(self, pe, t):
                norm, base = (normB, self.base2) if self.double else (self.norm, self.base)
                k = self.plan.bank(self.job, t)
                fill(pe, self.plan, self.job, t)
                pe.wait_ge(norm.y_ready, t.times(1, base + 1))
                nc.tensor.transpose(ps(k, P), yln[:, t.n % 2, norm.i, :], ident).then_inc(full[k], 1)

            def store(self, act, t):
                k = self.plan.bank(self.job, t)
                filled(act, self.plan, self.job, t)
                if self.affine:
                    m = nc.scalar.activation(cols(lnT, t), ps(k, P), ACT.Identity, bias=vec(self.affine + "_b"),
                                             scale=vec(self.affine + "_g"))
                else:
                    m = nc.scalar.activation(cols(lnT, t), ps(k, P), ACT.Copy)
                m.then_inc(free[k], 1)
                if self.ready is not None:
                    stored(act, self.plan, self.job, t)
                    act.sem_inc(self.ready, 1)

        def lnT_of(eng, tail, t):
            if tail.ready is not None:
                eng.wait_ge(tail.ready, t.times(1, 1))
            else:
                stored(eng, tail.plan, tail.job, t)

        a0 = banks.plan([("s0a", 0, 3), ("s0b", 1, 3), ("s1a", 2, 3), ("s1b", 3, 3), ("out", 4, 4),
                         ("q0", 5, 2), ("q1", 6, 2), ("q2", 7, 2), ("q3", 4, 2), ("key", 5, 2),
                         ("lat", 7, 1), ("lnt", 6, 6),
                         ("t0a", 7, 3), ("t0b", 4, 3), ("u0a", 5, 3), ("u0b", 6, 3),
                         ("t1a", 7, 3), ("t1b", 4, 3), ("u1a", 5, 3), ("u1b", 6, 3)], TILES, 6)
        tail_a0 = Tail(a0, ["y", f0hb[:, :]], double=True, affine="f0", ready=sem("a0_lnT_ready"))
        used["n"] = 0
        kvT = carve(2 * 2 * P).rearrange("p (u b k) -> p u b k", u=2, b=2)
        kvk = carve(2 * 2 * D).rearrange("p (u b d) -> p u b d", u=2, b=2)
        q0T = carve(2 * H0 * P).rearrange("p (u b h q) -> p u b h q", u=2, b=2, h=H0)
        e0 = carve(2 * 8 * P).rearrange("p (b g k) -> p b g k", b=2, g=8)
        p0 = carve(2 * 8 * P).rearrange("p (b g k) -> p b g k", b=2, g=8)
        pT0 = carve(2 * 8 * P).rearrange("p (b g q) -> p b g q", b=2, g=8)
        u0T = carve(2 * H0 * P).rearrange("p (u h q) -> p u h q", u=2, h=H0)
        negmax0 = sb("negmax0", [P, 2, 8])
        sum0 = sb("sum0", [P, 2, 8])
        rsum0 = sb("rsum0", [P, 2, 8])
        a0_max = sem("a0_max")
        a0_rsum = sem("a0_rsum")
        a0_probs = sem("a0_probs")

        def a0_pe(pe, step):
            t = step - 3
            if t.valid(TILES):
                u = t.n % 2
                for b in range(2):
                    for half in range(2):
                        job = f"s{b}{'ab'[half]}"
                        fill(pe, a0, job, t)
                        if b == 0 and half == 0:
                            for c in range(4):
                                stored(pe, a0, f"q{c}", t)
                        for j in range(4):
                            h = 8 * half + 2 * j
                            m = nc.tensor.matmul(ps(a0.bank(job, t), P, j * P), q0T[:, u, b, h:h + 2, :].rearrange("p h q -> p (h q)"),
                                                 kvT[:, u, b, :], start=True, stop=True)
                        m.then_inc(full[a0.bank(job, t)], 1)
            t = step - 4
            if t.valid(TILES):
                u = t.n % 2
                fill(pe, a0, "out", t)
                for job in ("u0a", "u0b", "u1a", "u1b"):
                    stored(pe, a0, job, t)
                for h in range(H0):
                    m = nc.tensor.matmul(ps(a0.bank("out", t), D), u0T[:, u, h, :], prjB[:, h, :], start=h == 0, stop=h == H0 - 1)
                m.then_inc(full[a0.bank("out", t)], 1)
            t = step - 2
            if t.valid(TILES):
                u = t.n % 2
                stored(pe, a0, "lat", t)
                for c in range(4):
                    fill(pe, a0, f"q{c}", t)
                    for j in range(4):
                        m = nc.tensor.matmul(ps(a0.bank(f"q{c}", t), P, j * P), sclA[:, 4 * c + j, :], kvT[:, u, :, S:P],
                                             start=True, stop=True)
                    m.then_inc(full[a0.bank(f"q{c}", t)], 1)
                fill(pe, a0, "key", t)
                for b in range(2):
                    m = nc.tensor.transpose(ps(a0.bank("key", t), P, b * P), kvT[:, u, b, :], ident)
                m.then_inc(full[a0.bank("key", t)], 1)
            t = step - 1
            if t.valid(TILES):
                u = t.n % 2
                fill(pe, a0, "lat", t)
                pe.wait_ge(normC.y_ready, t.times(1, 1))
                nc.tensor.transpose(ps(a0.bank("lat", t), P), yln[:, u, normC.i, :], ident)
                pe.wait_ge(norm02.y_ready, t.times(1, 1))
                nc.tensor.transpose(ps(a0.bank("lat", t), P, P), yln[:, u, norm02.i, :], ident).then_inc(full[a0.bank("lat", t)], 1)
            t = step - 6
            if t.valid(TILES):
                tail_a0.turn(pe, t)
            t = step - 3
            if t.valid(TILES):
                u = t.n % 2
                for b in range(2):
                    for half in range(2):
                        job = f"t{b}{'ab'[half]}"
                        fill(pe, a0, job, t)
                        pe.wait_ge(a0_probs, t.times(4, 2 * b + half + 1))
                        for j in range(4):
                            m = nc.tensor.transpose(ps(a0.bank(job, t), P, j * P), p0[:, b, 4 * half + j, :], ident)
                        m.then_inc(full[a0.bank(job, t)], 1)
                    if b == 0:
                        stored(pe, a0, "key", t)
                    for half in range(2):
                        job = f"u{b}{'ab'[half]}"
                        fill(pe, a0, job, t)
                        stored(pe, a0, f"t{b}{'ab'[half]}", t)
                        nc.tensor.matmul(ps(a0.bank(job, t)), kvk[:, u, b, :], pT0[:, b, 4 * half:4 * half + 4, :],
                                         start=True, stop=True).then_inc(full[a0.bank(job, t)], 1)

        def a0_act(act, step):
            t = step - 3
            if t.valid(TILES):
                for b in range(2):
                    for half in range(2):
                        filled(act, a0, f"s{b}{'ab'[half]}", t)
                    act.wait_ge(a0_max, t.times(2, b + 1))
                    for half in range(2):
                        k = a0.bank(f"s{b}{'ab'[half]}", t)
                        for j in range(4):
                            g = 4 * half + j
                            m = nc.scalar.activation(e0[:, b, g, :], ps(k, P, j * P), ACT.Exp, bias=negmax0[:, b, g:g + 1],
                                                     accum_out=sum0[:, b, g:g + 1])
                        m.then_inc(free[k], 1)
            t = step - 2
            if t.valid(TILES):
                k = a0.bank("key", t)
                filled(act, a0, "key", t)
                nc.scalar.activation(kvk[:, t.n % 2, :, :], ps(k, 2 * P), ACT.Copy).then_inc(free[k], 1)
            t = step - 1
            if t.valid(TILES):
                u, k = t.n % 2, a0.bank("lat", t)
                filled(act, a0, "lat", t)
                nc.scalar.activation(kvT[:, u, :, 0:S], ps(k, P).rearrange("p (b k) -> p b k", b=2), ACT.Identity,
                                     bias=vec("ln1_b"), scale=vec("ln1_g"))
                nc.scalar.activation(kvT[:, u, :, S:P], ps(k, P, P).rearrange("p (b k) -> p b k", b=2), ACT.Identity,
                                     bias=vec("ln2_b"), scale=vec("ln2_g")).then_inc(free[k], 1)
            t = step - 6
            if t.valid(TILES):
                tail_a0.store(act, t)
            t = step - 3
            if t.valid(TILES):
                u = t.n % 2
                for b in range(2):
                    k = a0.bank(f"t{b}a", t)
                    filled(act, a0, f"t{b}a", t)
                    nc.scalar.activation(pT0[:, b, 0:4, :], ps(k), ACT.Copy).then_inc(free[k], 1)
                    for half in range(2):
                        k = a0.bank(f"u{b}{'ab'[half]}", t)
                        filled(act, a0, f"u{b}{'ab'[half]}", t)
                        nc.scalar.activation(u0T[:, u, 8 * half:8 * half + 8, b * S:(b + 1) * S],
                                             ps(k).rearrange("p (h q) -> p h q", h=8), ACT.Copy) \
                            .then_inc(free[k], 1)

        def a0_dve(dve, step):
            t = step - 3
            if t.valid(TILES):
                for b in range(2):
                    filled(dve, a0, f"s{b}a", t)
                    filled(dve, a0, f"s{b}b", t)
                    nc.vector.tensor_reduce(negmax0[:, b, :], psum[:, 2 * b:2 * b + 2, :].rearrange("p a (g k) -> p (a g) k", g=4),
                                            AX.X, ALU.max, negate=True).then_inc(a0_max, 1)
            t = step
            if t.valid(TILES):
                if t.n == 0:
                    have(dve, "x_tok", "ctx_tok")
                norm0.stats(dve, xt(t), t, 0)
                normC.stats(dve, cols(ctx_tok, t), t, 0)
            t = step - 1
            if t.valid(TILES):
                norm02.stats(dve, yln[:, t.n % 2, norm0.i, :], t, 0)
            t = step - 5
            if t.valid(TILES):
                tail_a0.stats2(dve, t)
            t = step - 3
            if t.valid(TILES):
                stored(dve, a0, "s0a", t)
                stored(dve, a0, "s0b", t)
                nc.vector.reciprocal(rsum0[:, 0, :], sum0[:, 0, :]).then_inc(a0_rsum, 1)
            t = step - 4
            if t.valid(TILES):
                tail_a0.add(dve, t)
            t = step - 3
            if t.valid(TILES):
                stored(dve, a0, "s1a", t)
                stored(dve, a0, "s1b", t)
                nc.vector.reciprocal(rsum0[:, 1, :], sum0[:, 1, :]).then_inc(a0_rsum, 1)
            t = step - 2
            if t.valid(TILES):
                for c in range(4):
                    k = a0.bank(f"q{c}", t)
                    filled(dve, a0, f"q{c}", t)
                    nc.vector.tensor_copy(q0T[:, t.n % 2, :, 4 * c:4 * c + 4, :], ps(k).rearrange("p (h b q) -> p b h q", h=4, b=2)).then_inc(free[k], 1)
            t = step
            if t.valid(TILES):
                norm0.apply(dve, xt(t), t, 0)
                normC.apply(dve, cols(ctx_tok, t), t, 0)
            t = step - 1
            if t.valid(TILES):
                norm02.apply(dve, yln[:, t.n % 2, norm0.i, :], t, 0)
            t = step - 4
            if t.valid(TILES):
                tail_a0.apply(dve, t)
            t = step - 5
            if t.valid(TILES):
                tail_a0.apply2(dve, t)
            t = step - 3
            if t.valid(TILES):
                for b in range(2):
                    k = a0.bank(f"t{b}b", t)
                    filled(dve, a0, f"t{b}b", t)
                    nc.vector.tensor_copy(pT0[:, b, 4:8, :], ps(k)).then_inc(free[k], 1)

        def a0_pool(pool, step):
            t = step
            if t.valid(TILES):
                norm0.root(pool, t, 0)
                normC.root(pool, t, 0)
            t = step - 1
            if t.valid(TILES):
                norm02.root(pool, t, 0)
            t = step - 5
            if t.valid(TILES):
                tail_a0.root2(pool, t)
            for b in range(2):
                t = step - 3
                if t.valid(TILES):
                    pool.wait_ge(a0_rsum, t.times(2, b + 1))
                    for half in range(2):
                        g = slice(4 * half, 4 * half + 4)
                        pool.tensor_tensor(p0[:, b, g, :], e0[:, b, g, :], rsum0[:, b, g].unsqueeze(2).to_broadcast((P, 4, P)),
                                           ALU.mult).then_inc(a0_probs, 1)
                t = step - 4
                if b == 0 and t.valid(TILES):
                    tail_a0.root(pool, t)
            t = step - 5
            if t.valid(TILES):
                if t.n == 0:
                    pool.wait_ge(f0w_ready, 1)
                tail_a0.add_bias(pool, t)

        pe_parts.append(lambda e: run_steps(e, TILES, 6, lambda s: a0_pe(e, s)))
        act_parts.append(lambda e: run_steps(e, TILES, 6, lambda s: a0_act(e, s)))
        dve_parts.append(lambda e: run_steps(e, TILES, 6, lambda s: a0_dve(e, s)))
        pool_parts.append(lambda e: run_steps(e, TILES, 6, lambda s: a0_pool(e, s)))


        f0 = banks.plan([("out", (2, 3), 1), ("h", (0, 1), 0), ("lnt", 4, 2)], TILES, 2)
        tail_f0 = Tail(f0, [mat(rows, ROWS, "a1_bo")])
        hT0 = carve(2 * FC * P).rearrange("p (u c t) -> p u c t", u=2, c=FC)

        def f0_pe(pe, step):
            t = step - 1
            if t.valid(TILES):
                k = f0.bank("out", t)
                if t.n == 0:
                    pe.wait_ge(f0w_ready, 2)
                fill(pe, f0, "out", t)
                stored(pe, f0, "h", t)
                for c in range(FC):
                    m = nc.tensor.matmul(ps(k, D), hT0[:, t.n % 2, c, :], f0w2[:, c, :], start=c == 0, stop=c == FC - 1)
                m.then_inc(full[k], 1)
            t = step
            if t.valid(TILES):
                k = f0.bank("h", t)
                if t.n == 0:
                    pe.wait_ge(f0w_ready, 2)
                fill(pe, f0, "h", t)
                lnT_of(pe, tail_a0, t)
                for c in range(FC):
                    m = nc.tensor.matmul(ps(k, P, c * P), f0w1[:, c * P:(c + 1) * P], cols(lnT, t), start=True, stop=True)
                m.then_inc(full[k], 1)
            t = step - 2
            if t.valid(TILES):
                tail_f0.turn(pe, t)

        def f0_act(act, step):
            t = step
            if t.valid(TILES):
                k = f0.bank("h", t)
                filled(act, f0, "h", t)
                for c in range(FC):
                    m = nc.scalar.activation(hT0[:, t.n % 2, c, :], ps(k, P, c * P), ACT.Silu, bias=vec("f0_b1", c))
                m.then_inc(free[k], 1)
            t = step - 2
            if t.valid(TILES):
                tail_f0.store(act, t)

        def f0_dve(dve, step):
            t = step - 1
            if t.valid(TILES):
                tail_f0.add(dve, t)
                tail_f0.apply(dve, t)

        def f0_pool(pool, step):
            t = step - 1
            if t.valid(TILES):
                tail_f0.root(pool, t)
                tail_f0.add_bias(pool, t)

        pe_parts.append(lambda e: run_steps(e, TILES, 2, lambda s: f0_pe(e, s)))
        act_parts.append(lambda e: e.preload_act_table(ACT.Silu))
        act_parts.append(lambda e: run_steps(e, TILES, 2, lambda s: f0_act(e, s)))
        dve_parts.append(lambda e: run_steps(e, TILES, 2, lambda s: f0_dve(e, s)))
        pool_parts.append(lambda e: run_steps(e, TILES, 2, lambda s: f0_pool(e, s)))

        a1 = banks.plan([("s", (2, 3), 1), ("att", 5, 2), ("out", 6, 3), ("qk", 0, 0), ("v", 1, 0), ("lnt", 7, 4),
                         ("pt", 4, 1)], TILES, 4)
        tail_a1 = Tail(a1, [])
        buffers1 = [v.rearrange("p (u k) -> p u k", u=2) for v in over(ctx_tok, [2 * P] * 6)]
        ctile, v1, e1, p1, pT1, y1 = buffers1
        qk1 = ctx_tok[:, 12 * P:16 * P].rearrange("p (u w k) -> p u w k", u=2, w=2)
        sm1 = sb("sm1", [P, 2, 3])
        a1_ctile, a1_max, a1_exp, a1_rsum, a1_probs = (
            sem(f"a1_{x}") for x in ("ctile", "max", "exp", "rsum", "probs"))

        def wgt(n, w):
            return mat(wa, WA, f"a{n}{w}")

        def a1_pe(pe, step):
            t = step - 1
            if t.valid(TILES):
                u, k = t.n % 2, a1.bank("s", t)
                fill(pe, a1, "s", t)
                nc.tensor.matmul(ps(k, P), identb[:, :], m1b[:, :], start=True, stop=False)
                stored(pe, a1, "qk", t)
                nc.tensor.matmul(ps(k, P), qk1[:, u, 0, :], qk1[:, u, 1, :], start=False, stop=True).then_inc(full[k], 1)
            t = step - 2
            if t.valid(TILES):
                u, k = t.n % 2, a1.bank("att", t)
                fill(pe, a1, "att", t)
                stored(pe, a1, "v", t)
                stored(pe, a1, "pt", t)
                nc.tensor.matmul(ps(k, P), v1[:, u, :], pT1[:, u, :], start=True, stop=True).then_inc(full[k], 1)
            t = step - 3
            if t.valid(TILES):
                u, k = t.n % 2, a1.bank("out", t)
                fill(pe, a1, "out", t)
                stored(pe, a1, "att", t)
                nc.tensor.matmul(ps(k, D), y1[:, u, :], wgt(1, "o"), start=True, stop=True).then_inc(full[k], 1)
            t = step
            if t.valid(TILES):
                u, k = t.n % 2, a1.bank("qk", t)
                if t.n == 0:
                    have(pe, "wa")
                    pe.wait_ge(consts_ready, 1)
                fill(pe, a1, "qk", t)
                pe.wait_ge(a1_ctile, t.times(1, 1))
                nc.tensor.matmul(ps(k, P, P), wgt(1, "k"), ctile[:, u, :], start=True, stop=True)
                lnT_of(pe, tail_f0, t)
                nc.tensor.matmul(ps(k, P), wgt(1, "q"), cols(lnT, t), start=True, stop=True).then_inc(full[k], 1)
                k = a1.bank("v", t)
                fill(pe, a1, "v", t)
                nc.tensor.matmul(ps(k, P), ctile[:, u, :], wgt(1, "v"), start=True, stop=True).then_inc(full[k], 1)
            t = step - 4
            if t.valid(TILES):
                tail_a1.turn(pe, t)
            t = step - 1
            if t.valid(TILES):
                u, k = t.n % 2, a1.bank("pt", t)
                fill(pe, a1, "pt", t)
                pe.wait_ge(a1_probs, t.times(1, 1))
                nc.tensor.transpose(ps(k, P), p1[:, u, :], ident).then_inc(full[k], 1)

        def a1_act(act, step):
            t = step - 1
            if t.valid(TILES):
                u, k = t.n % 2, a1.bank("s", t)
                act.wait_ge(a1_max, t.times(1, 1))
                nc.scalar.activation(e1[:, u, :], ps(k, P), ACT.Exp, bias=sm1[:, u, 0:1], accum_out=sm1[:, u, 1:2]) \
                    .then_inc(free[k], 1)
            t = step
            if t.valid(TILES):
                u, k = t.n % 2, a1.bank("qk", t)
                if t.n == 0:
                    act.wait_ge(bqs_ready, 3)
                filled(act, a1, "qk", t)
                nc.scalar.activation(qk1[:, u, 0, :], ps(k, P), ACT.Identity, bias=bqs[:, 0:1], scale=D ** -0.5)
                nc.scalar.activation(qk1[:, u, 1, :], ps(k, P, P), ACT.Identity, bias=vec("a1_bk")).then_inc(free[k], 1)
            t = step - 4
            if t.valid(TILES):
                tail_a1.store(act, t)
            t = step - 1
            if t.valid(TILES):
                u, k = t.n % 2, a1.bank("pt", t)
                filled(act, a1, "pt", t)
                nc.scalar.activation(pT1[:, u, :], ps(k, P), ACT.Copy).then_inc(free[k], 1)

        def a1_dve(dve, step):
            t = step - 1
            if t.valid(TILES):
                u, k = t.n % 2, a1.bank("s", t)
                filled(dve, a1, "s", t)
                nc.vector.tensor_reduce(sm1[:, u, 0:1], ps(k, P), AX.X, ALU.max, negate=True).then_inc(a1_max, 1)
            t = step - 2
            if t.valid(TILES):
                u, k = t.n % 2, a1.bank("att", t)
                filled(dve, a1, "att", t)
                nc.vector.scalar_tensor_tensor(out=y1[:, u, :], in0=ps(k, P), scalar=vec("a1_bv"), in1=cols(lnT, t),
                                               op0=ALU.add, op1=ALU.add).then_inc(free[k], 1)
            t = step
            if t.valid(TILES):
                u, k = t.n % 2, a1.bank("v", t)
                filled(dve, a1, "v", t)
                nc.vector.tensor_copy(v1[:, u, :], ps(k, P)).then_inc(free[k], 1)
            t = step - 1
            if t.valid(TILES):
                u = t.n % 2
                stored(dve, a1, "s", t)
                nc.vector.reciprocal(sm1[:, u, 2:3], sm1[:, u, 1:2]).then_inc(a1_rsum, 1)
                dve.wait_ge(a1_rsum, t.times(1, 1))
                nc.vector.tensor_scalar(p1[:, u, :], e1[:, u, :], sm1[:, u, 2:3], None, ALU.mult).then_inc(a1_probs, 1)
            t = step - 3
            if t.valid(TILES):
                tail_a1.add(dve, t)
                tail_a1.apply(dve, t)

        def a1_pool(pool, step):
            t = step
            if t.valid(TILES):
                if t.n == 0:
                    have(pool, "cT")
                if t.n >= 2:
                    filled(pool, a1, "v", t - 2)
                pool.tensor_copy(ctile[:, t.n % 2, :], cols(cT, t)).then_inc(a1_ctile, 1)
            t = step - 3
            if t.valid(TILES):
                tail_a1.root(pool, t)

        pe_parts.append(lambda e: run_steps(e, TILES, 4, lambda s: a1_pe(e, s)))
        act_parts.append(lambda e: e.preload_act_table(ACT.Exp))
        act_parts.append(lambda e: run_steps(e, TILES, 4, lambda s: a1_act(e, s)))
        dve_parts.append(lambda e: run_steps(e, TILES, 4, lambda s: a1_dve(e, s)))
        pool_parts.append(lambda e: run_steps(e, TILES, 4, lambda s: a1_pool(e, s)))

        PAIRS = B * S // C1 // 2
        TC = C1 // P
        SRC = ("s", 0, 1)
        ITER = range(2)
        ALPHA, BETA, GATE = range(3)

        def parts(it):
            return (BETA, GATE) if it == 0 else (ALPHA, BETA, GATE)

        def turn(new, it, old, it_old):
            return ([(x, new) for x in (("R", "H0", "L", "O", "W") if it == 0 else ("H1",))] + [(f"D{it_old}", old), (f"M{it}", new)]
                    + [(f"E{it_old}", old), (f"Ca{it}", new), (f"Cb{it}", new)] + [(f"F{it_old}", old), (f"G{it_old}", old)]
                    + [(f"Cc{it}", new)])

        def pair_stages(a, following):
            b = a + 1
            stages = turn(b, 0, a, 0) + turn(a, 1, b, 0) + turn(b, 1, a, 1) + [("Z", a)]
            if following:
                return stages + [("X", a + 2)] + turn(a + 2, 0, b, 1) + [("Z", b), ("X", a + 3)]
            return stages + [(x, b) for x in ("D1", "E1", "F1", "G1", "Z")]

        OWN = ["R", "H0", "L", "O", "W", "M0", "Ca0", "Cb0", "F0", "G0", "Cc0", "H1", "M1", "Ca1", "Cb1", "F1", "G1", "Cc1", "Z"]
        BEFORE = [("X", 0), ("X", 1)] + [(x, 0) for x in OWN[:8] + ["Cc0"]]
        BODY = pair_stages(0, True)
        AFTER = pair_stages(2 * (PAIRS - 1), False)

        def controls(x):
            it = int(x[-1])
            if x[1] == "a":
                return [(s, BETA) for s in SRC]
            others = [(s, p) for p in (GATE, ALPHA) if p in parts(it) for s in SRC]
            half = 3 if it else 2
            return others[:half] if x[1] == "b" else others[half:]

        JOBS = {"R": ["r1"], "L": ["lg"], "O": ["oh", "wt"], "W": ["cw0", "cw1"], "Z": ["xo"]}
        for it in ITER:
            JOBS[f"H{it}"] = [f"h{it}{c}" for c in range(EC)] + [f"hs{it}"]
            JOBS[f"M{it}"] = [f"m{it}{k}{c}" for k in range(2) for c in range(EC)]
            for x in (f"Ca{it}", f"Cb{it}", f"Cc{it}"):
                JOBS[x] = [f"c{it}{s}{p}" for s, p in controls(x)]
            JOBS[f"F{it}"] = [f"hh{it}", f"f1{it}0", f"f1{it}1"]
            JOBS[f"G{it}"] = [f"ha{it}", f"f2{it}"]
        places = {(job, n): 4 * n + i % 4 for n in range(2) for i, job in enumerate(j for x in OWN for j in JOBS.get(x, []))}
        f1 = banks.plan_chunks(JOBS, places, BEFORE, BODY, AFTER, PAIRS)

        used["n"] = 0
        f1_X = carve(2 * C1).rearrange("p (n t) -> p n t", n=2)
        f1_V = carve(2 * C1).rearrange("p (n t) -> p n t", n=2)
        f1_H = carve(2 * EC * C1).rearrange("p (n c t) -> p n c t", n=2, c=EC)
        f1_Hm = carve(2 * 2 * EC * C1).rearrange("p (n k c t) -> p n k c t", n=2, k=2, c=EC)
        f1_bb = carve(2 * 3 * C1).rearrange("p (n s t) -> p n s t", n=2, s=3)
        f1_Hs = w0[:, 0:2 * C1].rearrange("p (n t) -> p n t", n=2)
        f1_cw = w0[:, 2 * C1:8 * C1].rearrange("p (n s t) -> p n s t", n=2, s=3)
        f1_tg = f1_H[:, :, 0:3, :]
        f1_ta = [sclA[:, 0:12, :].rearrange("p h d -> p (h d)").rearrange("p (s t) -> p s t", s=3),
                 prjB[:, 0:12, :].rearrange("p h d -> p (h d)").rearrange("p (s t) -> p s t", s=3)]
        f1_N = [sclA[:, 12:16, :].rearrange("p h d -> p (h d)"),
                prjB[:, 12:16, :].rearrange("p h d -> p (h d)")]
        f1_lb = sb("f1_lb", [P, 2, 3, C1])
        f1_lg = sb("f1_lg", [P, 2, TC, E])
        f1_m8 = sb("f1_m8", [P, 2, TC, 8])
        f1_ix = sb("f1_ix", [P, 2, TC, 8], U32)
        f1_ixf = sb("f1_ixf", [P, 2, TC, 2])
        f1_d = sb("f1_d", [P, 2, TC])
        f1_th = sb("f1_th", [P, 2, TC])
        f1_w = sb("f1_w", [P, 2, TC, 2])
        f1_ohT, f1_oh = over(ctx_tok, [2 * C1, 2 * TC * 96])
        f1_ohT = f1_ohT[0:96, :].bitcast(BF16).rearrange("p (n s t) -> p n s t", n=2, s=2)
        f1_oh = f1_oh.bitcast(BF16).rearrange("p (n i s e) -> p n i s e", n=2, i=TC, s=2)
        f1_wT = w0q[0:2, :, :].bitcast(F32)

        def s1(name):
            return [sem(f"f1_{name}{n}") for n in range(2)]

        f1_xin, f1_gap, f1_tanh, f1_weights, f1_onehot = (s1(x) for x in ("xin", "gap", "tanh", "weights", "onehot"))
        f1_clamped, f1_exped, f1_log, f1_err, f1_beta, f1_betaerr = (
            s1(x) for x in ("clamped", "exped", "log", "err", "beta", "betaerr"))
        f1_v, f1_xnext, f1_x = (s1(x) for x in ("v", "xnext", "x"))
        f1_chain = sem("f1_chain")
        CHAIN = 32

        def f1n(t, per, k):
            k += t.n // 2 * per
            return k if t.pair is None else t.pair * per + k

        def tiles_ready(eng, tail, t):
            eng.wait_ge(free[tail.plan.banks["lnt"][0]], t.times(TC, tail.plan.at["lnt", 0] + TC + 1))

        def w1(name, a=0, b=None, rows_=P):
            s0, n = W1F[name]
            return w1f[0:rows_, s0 + a:s0 + (n if b is None else b)]

        def f1_pe(pe, x, t):
            n = t.n % 2
            it = int(x[-1]) if x[-1].isdigit() else 0

            def start(job):
                fill(pe, f1, job, t)
                return f1.bank(job, t)

            if x == "R":
                k = start("r1")
                pe.wait_ge(f1_xin[n], f1n(t, 1, 1))
                nc.tensor.matmul(psum[0:32, k, :], w1("r1"), f1_X[:, n, :], start=True, stop=True).then_inc(full[k], 1)
            if x == "L":
                k = start("lg")
                stored(pe, f1, "r1", t)
                for i in range(TC):
                    m = nc.tensor.matmul(ps(k, E, E * i), f1_bb[0:32, n, 1, i * P:(i + 1) * P], w1("r2", rows_=32), start=True, stop=True)
                m.then_inc(full[k], 1)
            if x == "O":
                k = start("oh")
                pe.wait_ge(f1_onehot[n], f1n(t, 2, 2))
                bank = psum[0:96, k, :].bitcast(BF16)
                for s in range(2):
                    for i in range(TC):
                        m = nc.tensor.transpose(bank[:, (s * TC + i) * P:(s * TC + i + 1) * P], f1_oh[:, n, i, s, :], identb[:, :])
                m.then_inc(full[k], 1)
                k = start("wt")
                pe.wait_ge(f1_weights[n], f1n(t, 2, 2))
                for i in range(TC):
                    m = nc.tensor.transpose(psum[0:2, k, i * P:(i + 1) * P], f1_w[:, n, i, :], ident)
                m.then_inc(full[k], 1)
            if x == "W":
                stored(pe, f1, "wt", t)
                for s in range(2):
                    k = start(f"cw{s}")
                    nc.tensor.matmul(ps(k), mat(const, CONST, "selw")[0:2, s * P:(s + 1) * P], f1_wT[:, n, :], start=True, stop=True) \
                        .then_inc(full[k], 1)
            if x[0] == "H":
                if it == 0:
                    pe.wait_ge(f1_xin[n], f1n(t, 1, 1))
                else:
                    pe.wait_ge(f1_x[n], f1n(t, 2, 1))
                    pe.wait_ge(f1_v[n], f1n(t, 1, 1))
                for c in range(EC + 1):
                    k = start(f"h{it}{c}" if c < EC else f"hs{it}")
                    o, a, b = (ps(k), c * P, (c + 1) * P) if c < EC else (psum[0:HE, k, :], 0, HE)
                    wx, wv = ("e1x", "e1v") if c < EC else ("s1x", "s1v")
                    m = nc.tensor.matmul(o, w1(wx, a, b), f1_X[:, n, :], start=True, stop=it == 0)
                    if it:
                        m = nc.tensor.matmul(o, w1(wv, a, b), f1_V[:, n, :], start=False, stop=True)
                    m.then_inc(full[k], 1)
            if x[0] == "M":
                if it == 0:
                    stored(pe, f1, "oh", t)
                for s in range(2):
                    for c in range(EC):
                        k = start(f"m{it}{s}{c}")
                        nc.tensor.matmul(ps(k), selb[:, c, :], f1_ohT[:, n, s, :], start=True, stop=True).then_inc(full[k], 1)
            if x[0] == "C":
                for s, p in controls(x):
                    k = start(f"c{it}{s}{p}")
                    if s == "s":
                        stored(pe, f1, f"hs{it}", t)
                        m = nc.tensor.matmul(ps(k), w1("s2", p * D, (p + 1) * D, HE), f1_Hs[0:HE, n, :], start=True, stop=True)
                    else:
                        nc.tensor.matmul(ps(k), be2b[:, p * D:(p + 1) * D], f1_ohT[:, n, s, :], start=True, stop=False)
                        for c in range(EC):
                            if p == BETA:
                                stored(pe, f1, f"m{it}{s}{c}", t)
                            m = nc.tensor.matmul(ps(k), w1("e2", c * 384 + p * D, c * 384 + (p + 1) * D), f1_Hm[:, n, s, c, :],
                                                 start=False, stop=c == EC - 1)
                    m.then_inc(full[k], 1)
            if x[0] == "F":
                pe.wait_ge(f1_xnext[n], f1n(t, 2, it + 1))
                k = start(f"hh{it}")
                nc.tensor.matmul(psum[0:32, k, :], w1("h1"), f1_N[n], start=True, stop=True).then_inc(full[k], 1)
                for j in range(2):
                    k = start(f"f1{it}{j}")
                    nc.tensor.matmul(ps(k), w1("f1", j * P, (j + 1) * P), f1_N[n], start=True, stop=True).then_inc(full[k], 1)
            if x[0] == "G":
                k = start(f"ha{it}")
                stored(pe, f1, f"hh{it}", t)
                nc.tensor.matmul(ps(k), w1("h2", rows_=32), f1_bb[0:32, n, 0, :], start=True, stop=True).then_inc(full[k], 1)
                k = start(f"f2{it}")
                for j in range(2):
                    stored(pe, f1, f"f1{it}{j}", t)
                    m = nc.tensor.matmul(ps(k), w1("f2", j * D, (j + 1) * D), f1_bb[:, n, 1 + j, :], start=j == 0, stop=j == 1)
                m.then_inc(full[k], 1)
            if x == "Z":
                k = start("xo")
                pe.wait_ge(f1_x[n], f1n(t, 2, 2))
                for i in range(TC):
                    m = nc.tensor.transpose(ps(k, P, i * P), f1_X[:, n, i * P:(i + 1) * P], ident)
                m.then_inc(full[k], 1)

        def f1_act(act, x, t):
            n = t.n % 2
            it = int(x[-1]) if x[-1].isdigit() else 0

            def take(job):
                filled(act, f1, job, t)
                return f1.bank(job, t)

            if x == "R":
                k = take("r1")
                nc.scalar.activation(f1_bb[0:32, n, 1, :], psum[0:32, k, :], ACT.Gelu, bias=vec("b_r1")[0:32, :]).then_inc(free[k], 1)
            if x == "L":
                act.wait_ge(f1_gap[n], f1n(t, 1, 1))
                nc.scalar.activation(f1_th[:, n, :], f1_d[:, n, :], ACT.Tanh, scale=0.5).then_inc(f1_tanh[n], 1)
            if x == "O":
                k = take("oh")
                nc.scalar.activation(f1_ohT[:, n, :, :].rearrange("p s t -> p (s t)"), psum[0:96, k, :].bitcast(BF16), ACT.Copy) \
                    .then_inc(free[k], 1)
                k = take("wt")
                nc.scalar.activation(f1_wT[:, n, :], psum[0:2, k, :], ACT.Copy).then_inc(free[k], 1)
            if x == "W":
                for s in range(2):
                    k = take(f"cw{s}")
                    nc.scalar.activation(f1_cw[:, n, 1 + s, :], ps(k), ACT.Identity, scale=dv("omsw")).then_inc(free[k], 1)
            if x[0] == "H":
                for c in range(EC):
                    k = take(f"h{it}{c}")
                    nc.scalar.activation(f1_H[:, n, c, :], ps(k), ACT.Gelu, bias=vec("b_e1", c)).then_inc(free[k], 1)
                k = take(f"hs{it}")
                nc.scalar.activation(f1_Hs[0:HE, n, :], psum[0:HE, k, :], ACT.Gelu, bias=vec("b_s1")[0:HE, :]).then_inc(free[k], 1)
            if x[0] == "C":
                for s, p in controls(x):
                    i = SRC.index(s)
                    k = take(f"c{it}{s}{p}")
                    if p == BETA:
                        m = nc.scalar.activation(f1_bb[:, n, i, :], ps(k), ACT.Identity, bias=vec("b_s2", BETA) if s == "s" else 0.0)
                    else:
                        o = f1_tg[:, n, i, :] if p == GATE else f1_ta[n][:, i, :]
                        bias = (dv("hbg") if p == GATE else dv("hba")) if s == "s" else 0.0
                        m = nc.scalar.activation(o, ps(k), ACT.Tanh, bias=bias, scale=0.5)
                    m.then_inc(free[k], 1)
            if x[0] == "D":
                act.preload_act_table_set("natural_log_exp_and_others")
                act.wait_ge(f1_clamped[n], f1n(t, 2, it + 1))
                nc.scalar.activation(f1_lb[:, n, :, :], f1_lb[:, n, :, :], ACT.Exp).then_inc(f1_exped[n], 1)
                act.wait_ge(f1_exped[n], f1n(t, 2, it + 1))
                nc.scalar.activation(f1_lb[:, n, :, :], f1_lb[:, n, :, :], ACT.Ln, bias=1.0).then_inc(f1_log[n], 1)
                act.preload_act_table(ACT.Gelu)
            if x[0] == "F":
                k = take(f"hh{it}")
                nc.scalar.activation(f1_bb[0:32, n, 0, :], psum[0:32, k, :], ACT.Gelu, bias=vec("b_h1")[0:32, :]).then_inc(free[k], 1)
                for j in range(2):
                    k = take(f"f1{it}{j}")
                    nc.scalar.activation(f1_bb[:, n, 1 + j, :], ps(k), ACT.Gelu, bias=vec("b_f1", j)).then_inc(free[k], 1)
            if x[0] == "G":
                k = take(f"ha{it}")
                if it == 0:
                    act.wait_ge(f1_v[n], f1n(t, 1, 1))
                nc.scalar.activation(f1_lb[:, n, 0, :], ps(k), ACT.Tanh, bias=dv("hbh2"), scale=0.5).then_inc(free[k], 1)

        def f1_dve(dve, x, t, chain):
            n = t.n % 2
            it = int(x[-1]) if x[-1].isdigit() else 0

            def link(m):
                chain[0] += 1
                m.then_inc(f1_chain, 1)
                dve.wait_ge(f1_chain, chain[0] if t.pair is None else t.pair * CHAIN + chain[0])

            if x == "L":
                k = f1.bank("lg", t)
                filled(dve, f1, "lg", t)
                b_r2 = mat(rows, ROWS, "b_r2").unsqueeze(1).to_broadcast((P, TC, E))
                nc.vector.tensor_tensor(f1_lg[:, n, :, :], ps(k, TC * E).rearrange("p (i e) -> p i e", i=TC), b_r2, ALU.add) \
                    .then_inc(free[k], 1)
                stored(dve, f1, "lg", t)
                carry(dve, "dve")
                for i in range(TC):
                    m = nc.vector.max(f1_m8[:, n, i, :], f1_lg[:, n, i, :])
                link(m)
                nc.vector.tensor_tensor(f1_d[:, n, :], f1_m8[:, n, :, 1], f1_m8[:, n, :, 0], ALU.subtract).then_inc(f1_gap[n], 1)
                for i in range(TC):
                    m = nc.vector.max_index(f1_ix[:, n, i, :], f1_m8[:, n, i, :], f1_lg[:, n, i, :])
                link(m)
                link(nc.vector.tensor_copy(f1_ixf[:, n, :, :], f1_ix[:, n, :, 0:2]))
                iota = mat(const, CONST, "iota").unsqueeze(1).unsqueeze(1).to_broadcast((P, TC, 3, E))
                for s in range(2):
                    o = f1_oh[:, n, :, s, :].rearrange("p i (r e) -> p i r e", r=3)[:, :, :, 0:E]
                    ix = f1_ixf[:, n, :, s:s + 1].unsqueeze(3).to_broadcast((P, TC, 3, E))
                    nc.vector.tensor_tensor(o, iota, ix, ALU.is_equal).then_inc(f1_onehot[n], 1)
                dve.wait_ge(f1_tanh[n], f1n(t, 1, 1))
                for s, sign in ((0, -0.5), (1, 0.5)):
                    nc.vector.tensor_scalar(f1_w[:, n, :, s], f1_th[:, n, :], sign, 0.5, ALU.mult, ALU.add).then_inc(f1_weights[n], 1)
            if x[0] == "M":
                for s in range(2):
                    for c in range(EC):
                        k = f1.bank(f"m{it}{s}{c}", t)
                        if s == 0:
                            stored(dve, f1, f"h{it}{c}", t)
                        filled(dve, f1, f"m{it}{s}{c}", t)
                        nc.vector.tensor_tensor(f1_Hm[:, n, s, c, :], f1_H[:, n, c, :], ps(k), ALU.mult).then_inc(free[k], 1)
            if x[:2] == "Ca":
                if it == 0:
                    dve.wait_ge(f1_xin[n], f1n(t, 1, 1))
                else:
                    dve.wait_ge(f1_x[n], f1n(t, 2, 1))
                nc.vector.tensor_scalar(f1_N[n], f1_X[:, n, :], -1.0, vec("mu"), ALU.mult, ALU.add).then_inc(f1_err[n], 1)
                for s in SRC:
                    stored(dve, f1, f"c{it}{s}{BETA}", t)
                nc.vector.tensor_scalar(f1_lb[:, n, :, :], f1_bb[:, n, :, :], 40.0, None, ALU.min).then_inc(f1_clamped[n], 1)
            if x[0] == "E":
                for s in SRC:
                    for p in parts(it):
                        stored(dve, f1, f"c{it}{s}{p}", t)
                if it:
                    v = f1_V[:, n, :].unsqueeze(1).to_broadcast((P, 3, C1))
                    link(nc.vector.scalar_tensor_tensor(out=f1_ta[n], in0=f1_ta[n], scalar=1.0, in1=v, op0=ALU.add, op1=ALU.mult))
                dve.wait_ge(f1_log[n], f1n(t, 2, it + 1))
                nc.vector.tensor_tensor(f1_lb[:, n, :, :], f1_bb[:, n, :, :], f1_lb[:, n, :, :], ALU.max).then_inc(f1_beta[n], 1)
                dve.wait_ge(f1_betaerr[n], f1n(t, 2, it + 1))
                if it:
                    link(nc.vector.scalar_tensor_tensor(out=f1_lb[:, n, :, :], in0=f1_ta[n], scalar=0.5, in1=f1_lb[:, n, :, :],
                                                        op0=ALU.mult, op1=ALU.add))
                link(nc.vector.tensor_tensor(f1_lb[:, n, :, :], f1_lb[:, n, :, :], f1_cw[:, n, :, :], ALU.mult))
                link(nc.vector.scalar_tensor_tensor(out=f1_tg[:, n, :, :], in0=f1_tg[:, n, :, :], scalar=1.0, in1=f1_lb[:, n, :, :],
                                                    op0=ALU.add, op1=ALU.mult))
                link(nc.vector.tensor_tensor(f1_tg[:, n, 0, :], f1_tg[:, n, 0, :], f1_tg[:, n, 1, :], ALU.add))
                link(nc.vector.tensor_tensor(f1_tg[:, n, 0, :], f1_tg[:, n, 0, :], f1_tg[:, n, 2, :], ALU.add))
                nc.vector.scalar_tensor_tensor(out=f1_N[n], in0=f1_tg[:, n, 0, :], scalar=0.05, in1=f1_X[:, n, :],
                                               op0=ALU.mult, op1=ALU.add).then_inc(f1_xnext[n], 1)
                if it == 0:
                    link(nc.vector.tensor_tensor(f1_V[:, n, :], f1_lb[:, n, 0, :], f1_lb[:, n, 1, :], ALU.add))
                    nc.vector.tensor_tensor(f1_V[:, n, :], f1_V[:, n, :], f1_lb[:, n, 2, :], ALU.add).then_inc(f1_v[n], 1)
            if x[0] == "G":
                k = f1.bank(f"f2{it}", t)
                filled(dve, f1, f"f2{it}", t)
                if it == 0:
                    dve.wait_ge(f1_v[n], f1n(t, 1, 1))
                nc.vector.tensor_scalar(f1_lb[:, n, 1, :], ps(k), vec("b_f2"), dv("hiw"), ALU.add, ALU.mult).then_inc(free[k], 1)
                stored(dve, f1, f"f2{it}", t)
                stored(dve, f1, f"ha{it}", t)
                link(nc.vector.scalar_tensor_tensor(out=f1_lb[:, n, 1, :], in0=f1_lb[:, n, 0, :], scalar=1.0, in1=f1_lb[:, n, 1, :],
                                                    op0=ALU.add, op1=ALU.mult))
                nc.vector.tensor_tensor(f1_X[:, n, :], f1_X[:, n, :], f1_lb[:, n, 1, :], ALU.add).then_inc(f1_x[n], 1)
            if x == "Z":
                k = f1.bank("xo", t)
                filled(dve, f1, "xo", t)
                nc.vector.tensor_tensor(cols(x_tok, t, C1), cols(x_tok, t, C1), ps(k), ALU.add).then_inc(free[k], 1)

        def f1_pool(pool, x, t):
            n = t.n % 2
            if x == "X":
                tiles_ready(pool, tail_a1, t)
                pool.tensor_copy(f1_X[:, n, :], cols(lnT, t, C1)).then_inc(f1_xin[n], 1)
            if x[0] == "E":
                it = int(x[-1])
                pool.wait_ge(f1_err[n], f1n(t, 2, it + 1))
                pool.wait_ge(f1_beta[n], f1n(t, 2, it + 1))
                err = f1_N[n].unsqueeze(1).to_broadcast((P, 3, C1))
                pool.tensor_tensor(f1_lb[:, n, :, :], f1_lb[:, n, :, :], err, ALU.mult).then_inc(f1_betaerr[n], 1)
            if x == "Z":
                filled(pool, f1, "xo", t)

        def f1_run(engine, stage):
            chain = [0]
            for x, n in BEFORE:
                stage(x, At(n), chain)
            start = chain[0]
            with engine.Fori(0, PAIRS - 1) as pair:
                for x, n in BODY:
                    stage(x, At(n, pair), chain)
            assert chain[0] - start in (0, CHAIN), chain
            chain[0] = start + (PAIRS - 1) * (chain[0] - start)
            for x, n in AFTER:
                stage(x, At(n), chain)

        def f1_dve_setup(dve):
            dve.wait_ge(f1_derived_ready, 1)
            nc.vector.memset(f1_oh, 0.0)
            for n in range(2):
                nc.vector.tensor_scalar(f1_cw[:, n, 0, :], f1_cw[:, n, 0, :], 0.0, dv("sw"), ALU.mult, ALU.add)

        def f1_pe_first(pe):
            have(pe, "w1f")
            pe.wait_ge(f1_derived_ready, 2)

        pe_parts.append(f1_pe_first)
        pe_parts.append(lambda e: f1_run(e, lambda x, t, c: f1_pe(e, x, t)))
        act_parts.append(lambda e: e.wait_ge(f1_derived_ready, 1))
        act_parts.append(lambda e: e.preload_act_table(ACT.Gelu))
        act_parts.append(lambda e: f1_run(e, lambda x, t, c: f1_act(e, x, t)))
        dve_parts.append(f1_dve_setup)
        dve_parts.append(lambda e: f1_run(e, lambda x, t, c: f1_dve(e, x, t, c)))
        pool_parts.append(lambda e: f1_run(e, lambda x, t, c: f1_pool(e, x, t)))

        def f1_over(eng):
            for n in range(2 * PAIRS - 2, 2 * PAIRS):
                stored(eng, f1, "xo", At(n))

        def sp_load_later(sp):
            f1_over(sp)
            for name, dst, src in LATER:
                sp.dma_start(dst, src).then_inc(loaded[name], 16)

        sp_parts.append(sp_load_later)

        PAIR2 = H2 // 2
        used["n"] = 0
        qm = carve(2 * 2 * H2 * S).rearrange("p (u b h q) -> p u b h q", u=2, b=2, h=H2)
        Vx = carve(2 * 2 * D).rearrange("p (u b d) -> p u b d", u=2, b=2)
        q2 = carve(2 * P).rearrange("p (u q) -> p u q", u=2)
        kT2 = carve(2 * P).rearrange("p (u k) -> p u k", u=2)
        vT2 = carve(2 * 2 * P).rearrange("p (u b r k) -> p u b r k", u=2, b=2, r=2)
        e2 = carve(2 * 2 * PAIR2 * S).rearrange("p (u b g k) -> p u b g k", u=2, b=2, g=PAIR2)
        pT2 = carve(2 * 4 * P).rearrange("p (b j q) -> p b j q", b=2, j=4)
        o2 = carve(2 * 2 * D).rearrange("p (u b d) -> p u b d", u=2, b=2)
        oT2 = carve(P)
        max2 = carve(2 * PAIR2).rearrange("p (b g) -> p b g", b=2)
        sum2 = carve(2 * PAIR2).rearrange("p (b g) -> p b g", b=2)
        rsum2 = carve(2 * PAIR2).rearrange("p (b g) -> p b g", b=2)
        rsm2 = carve(2 * PAIR2 * 2).rearrange("p (g r) -> p g r", r=2)

        def attention(n, before, bias, own=None):
            late = 0 if own is None else 2
            jobs = [("s0", 0, 2), ("s1", 1, 2), ("av", 4, 4), ("vt", 5, 2), ("out", 6, 6), ("cb", 5, 5),
                    ("qkv", 6, 0), ("t0", 2, 3), ("t1", 3, 3), ("lnt", 7, 8)]
            jobs = [(job, k, lag + late) for job, k, lag in jobs] + ([("lnt0", 7, 1)] if late else [])
            a = banks.plan(jobs, TILES, 8 + late)
            if late:
                before = Tail(a, own, job="lnt0", norm=normF)
            tail = Tail(a, bias)
            cleared, spread, maxed, exped, summed, inverted, masked, scaled = (
                sem(f"a{n}_{x}") for x in ("cleared", "spread", "max", "exp", "sum", "rsum", "masked", "scaled"))

            def on_pe(pe, first):
                step = first - late
                t = step - 2
                if t.valid(TILES):
                    u = t.n % 2
                    for b in range(2):
                        k = a.bank(f"s{b}", t)
                        fill(pe, a, f"s{b}", t)
                        nc.tensor.matmul(ps(k), identb[:, :], m23b[:, n - 2, :], start=True, stop=False)
                        if b == 0:
                            pe.wait_ge(spread, t.times(1, 1))
                        for g in range(PAIR2):
                            m = nc.tensor.matmul(ps(k, S, g * S), qm[:, u, b, 2 * g:2 * g + 2, :].rearrange("p h q -> p (h q)"),
                                                 kT2[:, u, b * S:(b + 1) * S], start=False, stop=g == PAIR2 - 1)
                        m.then_inc(full[k], 1)
                t = step - 4
                if t.valid(TILES):
                    k = a.bank("av", t)
                    fill(pe, a, "av", t)
                    stored(pe, a, "vt", t)
                    for b in range(2):
                        stored(pe, a, f"t{b}", t)
                        for j in range(4):
                            m = nc.tensor.matmul(ps(k, 32, b * D + j * 32), pT2[:, b, j, :], Vx[:, t.n % 2, b, j * 32:(j + 1) * 32],
                                                 start=True, stop=True)
                    m.then_inc(full[k], 1)
                t = step - 2
                if t.valid(TILES):
                    k = a.bank("vt", t)
                    fill(pe, a, "vt", t)
                    for b in range(2):
                        m = nc.tensor.transpose(ps(k, D, b * D), vT2[:, t.n % 2, b, :, :].rearrange("p r k -> p (r k)"), ident)
                    m.then_inc(full[k], 1)
                t = step - 6
                if t.valid(TILES):
                    k = a.bank("out", t)
                    fill(pe, a, "out", t)
                    stored(pe, a, "cb", t)
                    nc.tensor.matmul(ps(k, D), oT2, wgt(n, "o"), start=True, stop=True).then_inc(full[k], 1)
                t = step - 5
                if t.valid(TILES):
                    k = a.bank("cb", t)
                    fill(pe, a, "cb", t)
                    pe.wait_ge(scaled, t.times(1, 1))
                    for b in range(2):
                        m = nc.tensor.matmul(ps(k, S, b * S), o2[:, t.n % 2, b, :], mat(const, CONST, "two"), start=True, stop=True)
                    m.then_inc(full[k], 1)
                t = step
                if t.valid(TILES):
                    k = a.bank("qkv", t)
                    if t.n == 0:
                        have(pe, "cT")
                    fill(pe, a, "qkv", t)
                    nc.tensor.matmul(ps(k, P, P), wgt(n, "k"), cols(cT, t), start=True, stop=True)
                    nc.tensor.matmul(ps(k, P, 2 * P), wgt(n, "v"), cols(cT, t), start=True, stop=True)
                    lnT_of(pe, before, t)
                    nc.tensor.matmul(ps(k, P), wgt(n, "q"), cols(lnT, t), start=True, stop=True).then_inc(full[k], 1)
                t = step - 3
                if t.valid(TILES):
                    for b in range(2):
                        k = a.bank(f"t{b}", t)
                        fill(pe, a, f"t{b}", t)
                        pe.wait_ge(exped, t.times(2, b + 1))
                        for j in range(4):
                            m = nc.tensor.transpose(ps(k, P, j * P), e2[:, t.n % 2, b, 2 * j:2 * j + 2, :].rearrange("p g k -> p (g k)"), ident)
                        m.then_inc(full[k], 1)
                t = step - 8
                if t.valid(TILES):
                    tail.turn(pe, t)
                if late and (first - 1).valid(TILES):
                    before.turn(pe, first - 1)

            def on_act(act, first):
                step = first - late
                t = step - 2
                if t.valid(TILES):
                    for b in range(2):
                        stored(act, a, f"s{b}", t)
                        nc.scalar.activation(e2[:, t.n % 2, b, :, :], e2[:, t.n % 2, b, :, :], ACT.Exp).then_inc(exped, 1)
                t = step - 2
                if t.valid(TILES):
                    k = a.bank("vt", t)
                    filled(act, a, "vt", t)
                    if t.n == 0:
                        act.wait_ge(cleared, 1)
                    for r in range(2):
                        rows_ = slice(r * S, (r + 1) * S)
                        m = nc.scalar.activation(Vx[rows_, t.n % 2, :, :].rearrange("p b (j c) -> p b j c", c=32)[:, :, :, r * 16:(r + 1) * 16],
                                                  ps(k, 2 * D)[rows_, :].rearrange("p (b j c) -> p b j c", b=2, c=32)[:, :, :, r * 16:(r + 1) * 16], ACT.Copy)
                    m.then_inc(free[k], 1)
                t = step - 5
                if t.valid(TILES):
                    k = a.bank("cb", t)
                    filled(act, a, "cb", t)
                    nc.scalar.activation(oT2, ps(k, P), ACT.Copy).then_inc(free[k], 1)
                t = step
                if t.valid(TILES):
                    u, k = t.n % 2, a.bank("qkv", t)
                    filled(act, a, "qkv", t)
                    nc.scalar.activation(q2[:, u, :], ps(k, P), ACT.Identity, bias=bqs[:, n - 1:n], scale=DH2 ** -0.5)
                    nc.scalar.activation(kT2[:, u, :], ps(k, P, P), ACT.Identity, bias=vec(f"a{n}_bk"))
                    nc.scalar.activation(vT2[:, u, :, :, :],
                                         ps(k, P, 2 * P).rearrange("p (b k) -> p b k", b=2).unsqueeze(2).to_broadcast((P, 2, 2, S)),
                                         ACT.Identity, bias=vec(f"a{n}_bv")).then_inc(free[k], 1)
                t = step - 3
                if t.valid(TILES):
                    for b in range(2):
                        k = a.bank(f"t{b}", t)
                        filled(act, a, f"t{b}", t)
                        nc.scalar.activation(pT2[:, b, :, :], ps(k), ACT.Copy).then_inc(free[k], 1)
                t = step - 8
                if t.valid(TILES):
                    tail.store(act, t)
                if late and (first - 1).valid(TILES):
                    before.store(act, first - 1)

            def on_dve(dve, first):
                step = first - late
                t = step - 2
                if t.valid(TILES):
                    for b in range(2):
                        k = a.bank(f"s{b}", t)
                        filled(dve, a, f"s{b}", t)
                        nc.vector.tensor_reduce(max2[:, b, :], ps(k).rearrange("p (g k) -> p g k", g=PAIR2), AX.X, ALU.max).then_inc(maxed, 1)
                t = step - 2
                if t.valid(TILES):
                    for b in range(2):
                        k = a.bank(f"s{b}", t)
                        dve.wait_ge(maxed, t.times(2, b + 1))
                        nc.vector.tensor_tensor(e2[:, t.n % 2, b, :, :], ps(k).rearrange("p (g k) -> p g k", g=PAIR2),
                                                max2[:, b, :].unsqueeze(2).to_broadcast((P, PAIR2, S)), ALU.subtract) \
                            .then_inc(free[k], 1)
                t = step - 6
                if t.valid(TILES):
                    tail.add(dve, t, stats=False)
                t = step - 3
                if t.valid(TILES):
                    dve.wait_ge(exped, t.times(2, 2))
                    nc.vector.tensor_reduce(sum2, e2[:, t.n % 2, :, :, :], AX.X, ALU.add).then_inc(summed, 1)
                t = step - 6
                if t.valid(TILES):
                    tail.stats(dve, t)
                t = step - 4
                if t.valid(TILES):
                    k = a.bank("av", t)
                    filled(dve, a, "av", t)
                    dve.wait_ge(masked, t.times(1, 1))
                    nc.vector.tensor_tensor(o2[:, t.n % 2, :, :].rearrange("p b (h d) -> p (b h) d", d=DH2),
                                            ps(k, 2 * D).rearrange("p (h d) -> p h d", d=DH2),
                                            rsm2.rearrange("p g r -> p (g r)").unsqueeze(2).to_broadcast((P, 2 * H2, DH2)), ALU.mult) \
                        .then_inc(free[k], 1)
                t = step - 3
                if t.valid(TILES):
                    dve.wait_ge(summed, t.times(1, 1))
                    nc.vector.reciprocal(rsum2, sum2).then_inc(inverted, 1)
                t = step - 4
                if t.valid(TILES):
                    stored(dve, a, "av", t)
                    dve.sem_inc(scaled, 1)
                t = step - 7
                if t.valid(TILES):
                    tail.apply(dve, t)
                if late and (first - 1).valid(TILES):
                    before.apply(dve, first - 1)
                if late and first.valid(TILES):
                    if first.n == 0:
                        f1_over(dve)
                    before.norm.stats(dve, xt(first), first, before.base)
                t = step - 3
                if t.valid(TILES):
                    dve.wait_ge(inverted, t.times(1, 1))
                    nc.vector.tensor_tensor(rsm2, rsum2.rearrange("p b g -> p (b g)").unsqueeze(2).to_broadcast((P, 2 * PAIR2, 2)),
                                            mat(const, CONST, "half").unsqueeze(1).to_broadcast((P, 2 * PAIR2, 2)), ALU.mult) \
                        .then_inc(masked, 1)

            def on_pool(pool, first):
                step = first - late
                if late and first.valid(TILES):
                    before.root(pool, first)
                t = step - 6
                if t.valid(TILES):
                    tail.root(pool, t)
                t = step
                if t.valid(TILES):
                    u = t.n % 2
                    stored(pool, a, "qkv", t)
                    if t.n >= 2:
                        filled(pool, a, "s1", t - 2)
                    pool.tensor_tensor(qm[:, u, :, :, :], q2[:, u, :].rearrange("p (b q) -> p b q", b=2).unsqueeze(2).to_broadcast((P, 2, H2, S)),
                                       mat(const, CONST, "head").unsqueeze(1).unsqueeze(3).to_broadcast((P, 2, H2, S)), ALU.mult) \
                        .then_inc(spread, 1)
                t = step - 7
                if t.valid(TILES):
                    tail.add_bias(pool, t)
                if late and (first - 1).valid(TILES):
                    before.add_bias(pool, first - 1)

            def pool_clear(pool):
                if n == 2:
                    f1_over(pool)
                pool.memset(Vx.rearrange("p u b d -> p (u b d)"), 0.0).then_inc(cleared, 1)
                pool.wait_ge(cleared, 1)

            pe_parts.append(lambda e: run_steps(e, TILES, 8 + late, lambda s: on_pe(e, s)))
            act_parts.append(lambda e: e.preload_act_table(ACT.Exp))
            act_parts.append(lambda e: run_steps(e, TILES, 8 + late, lambda s: on_act(e, s)))
            dve_parts.append(lambda e: run_steps(e, TILES, 8 + late, lambda s: on_dve(e, s)))
            pool_parts.append(pool_clear)
            pool_parts.append(lambda e: run_steps(e, TILES, 8 + late, lambda s: on_pool(e, s)))
            return tail

        tail_a2 = attention(2, None, [mat(rows, ROWS, "f2_bo")], own=[mat(rows, ROWS, "a2_bo")])

        CHUNKS = B * S // C1
        used["n"] = 0
        hid2 = carve(FC * B * S).rearrange("p (c t) -> p c t", c=FC)
        hq2 = carve(2 * FC * P).rearrange("p (u c t) -> p u c t", u=2, c=FC)
        hr2 = carve(2 * FC * P).rearrange("p (u c t) -> p u c t", u=2, c=FC)
        win2 = carve(F0)
        win2t = carve(F0).rearrange("p (c k) -> p c k", c=FC)
        wout2 = carve(F0).rearrange("p (c d) -> p c d", c=FC)
        small, n_small = pack([("win_inv", FC), ("win_scale", FC), ("wout_inv", FC), ("wout_scale", FC), ("gelu", FC),
                               ("x_max", 1), ("x_all", 1), ("x_scale", 1), ("x_inv", 1),
                               ("h_maxes", FC * CHUNKS), ("h_max", 1), ("h_all", 1), ("h_scale", 1), ("h_inv", 1)])
        small2 = sb("small2", [P, n_small])

        def sm(name, i=0, n=None):
            s0, w = small[name]
            return small2[:, s0 + i:s0 + (w if n is None else i + n)]

        f2s = banks.plan([("xmax", 1, 0), ("xall", 2, 0), ("wt", 0, 0)], 1, 0)
        f2h = banks.plan([(f"h{i}{c}", 4 * (i % 2) + c, 0) for i in range(CHUNKS) for c in range(FC)]
                         + [("hmax", 0, 0), ("hall", 1, 0)], 1, 0)
        f2 = banks.plan([("out", (2, 3), 1), ("lnt", 7, 2)], TILES, 2)
        tail_f2 = Tail(f2, [mat(rows, ROWS, "a3_bo")])
        f2_step = sem("f2_step")
        f2_wt, f2_xmax, f2_xtop, f2_xq, f2_gelu, f2_wout, f2_hmax, f2_htop, f2_hscale, f2_rounded, f2_hq = (
            sem(f"f2_{x}") for x in ("wt", "xmax", "xtop", "xq", "gelu", "wout", "hmax", "htop", "hscale", "rounded", "hq"))
        ones_row = mat(const, CONST, "selw")[0:1, 0:P]

        def f2_dve_first(dve):
            count = [0]

            def link(m):
                count[0] += 1
                m.then_inc(f2_step, 1)
                dve.wait_ge(f2_step, count[0])

            def top(name, plan, job, done):
                k = plan.bank(job, T0)
                filled(dve, plan, job, T0)
                nc.vector.tensor_reduce(sm(name)[0:1, :], psum[0:1, k, 0:P], AX.X, ALU.max).then_inc(done, 1)
                dve.wait_ge(done, 1)
                dve.sem_inc(free[k], 1)

            def scale_of(name, plan, job):
                k = plan.bank(job, T0)
                filled(dve, plan, job, T0)
                link(nc.vector.tensor_scalar(sm(f"{name}_all"), ps(k, 1), 1e-8, None, ALU.max))
                dve.sem_inc(free[k], 1)
                link(nc.vector.reciprocal(sm(f"{name}_scale"), sm(f"{name}_all")))
                link(nc.vector.tensor_scalar(sm(f"{name}_scale"), sm(f"{name}_scale"), 32767.0, None, ALU.mult))
                link(nc.vector.tensor_scalar(sm(f"{name}_inv"), sm(f"{name}_all"), 1.0 / 32767.0, None, ALU.mult))

            have(dve, "w2f")
            for name, w, inv, scale in (("in", win2t, "win_inv", "win_scale"), ("out", wout2, "wout_inv", "wout_scale")):
                raw = mat(w2f, W2F, name).rearrange("p (c k) -> p c k", c=FC)
                link(nc.vector.tensor_reduce(sm(inv), raw, AX.X, ALU.max, apply_absolute_value=True))
                link(nc.vector.tensor_scalar(sm(inv), sm(inv), 1e-8, None, ALU.max))
                link(nc.vector.reciprocal(sm(scale), sm(inv)))
                link(nc.vector.tensor_scalar(sm(scale), sm(scale), 127.0, None, ALU.mult))
                link(nc.vector.tensor_scalar(sm(inv), sm(inv), 1.0 / 127.0, None, ALU.mult))
                link(nc.vector.tensor_tensor(w, raw, sm(scale).unsqueeze(2).to_broadcast((P, FC, D)), ALU.mult))
                link(nc.vector.tensor_scalar(w, w, MAGIC, None, ALU.add))
                m = nc.vector.tensor_scalar(w, w, MAGIC, 127.0, ALU.subtract, ALU.min)
                if name == "in":
                    m.then_inc(f2_wt, 1)
                else:
                    link(m)
            nc.vector.tensor_tensor(wout2, wout2, sm("wout_inv").unsqueeze(2).to_broadcast((P, FC, D)), ALU.mult).then_inc(f2_wout, 1)

            stored(dve, tail_a2.plan, "lnt", At(TILES - 1))
            nc.vector.tensor_reduce(sm("x_max"), lnT[:, :], AX.X, ALU.max, apply_absolute_value=True).then_inc(f2_xmax, 1)
            top("x_max", f2s, "xmax", f2_xtop)
            scale_of("x", f2s, "xall")
            for i in range(CHUNKS):
                x = lnT[:, i * C1:(i + 1) * C1]
                link(nc.vector.tensor_scalar(x, x, sm("x_scale"), MAGIC, ALU.mult, ALU.add))
                nc.vector.tensor_scalar(x, x, MAGIC, 32767.0, ALU.subtract, ALU.min).then_inc(f2_xq, 1)
            nc.vector.tensor_scalar(sm("gelu"), sm("win_inv"), sm("x_inv"), None, ALU.mult).then_inc(f2_gelu, 1)
            for i in range(CHUNKS):
                for c in range(FC):
                    stored(dve, f2h, f"h{i}{c}", T0)
                m = nc.vector.tensor_reduce(sm("h_maxes", FC * i, FC), hid2[:, :, i * C1:(i + 1) * C1], AX.X, ALU.max,
                                            apply_absolute_value=True)
            link(m)
            nc.vector.tensor_reduce(sm("h_max"), sm("h_maxes"), AX.X, ALU.max).then_inc(f2_hmax, 1)
            top("h_max", f2h, "hmax", f2_htop)
            scale_of("h", f2h, "hall")
            dve.sem_inc(f2_hscale, 1)

        def f2_pe_first(pe):
            def all_largest(name, plan, own, top, job, job_all):
                pe.wait_ge(own, 1)
                fill(pe, plan, job, T0)
                nc.tensor.transpose(psum[0:1, plan.bank(job, T0), 0:P], sm(name), ident).then_inc(full[plan.bank(job, T0)], 1)
                pe.wait_ge(top, 1)
                fill(pe, plan, job_all, T0)
                nc.tensor.matmul(ps(plan.bank(job_all, T0), 1), ones_row, sm(name)[0:1, :], start=True, stop=True) \
                    .then_inc(full[plan.bank(job_all, T0)], 1)

            all_largest("x_max", f2s, f2_xmax, f2_xtop, "xmax", "xall")
            pe.wait_ge(f2_wt, 1)
            fill(pe, f2s, "wt", T0)
            for c in range(FC):
                m = nc.tensor.transpose(ps(0, P, c * P), win2t[:, c, :], ident)
            m.then_inc(full[0], 1)
            stored(pe, f2s, "wt", T0)
            for i in range(CHUNKS):
                pe.wait_ge(f2_xq, i + 1)
                for c in range(FC):
                    k = f2h.bank(f"h{i}{c}", T0)
                    fill(pe, f2h, f"h{i}{c}", T0)
                    nc.tensor.matmul(ps(k), win2[:, c * P:(c + 1) * P], lnT[:, i * C1:(i + 1) * C1], start=True, stop=True).then_inc(full[k], 1)
            all_largest("h_max", f2h, f2_hmax, f2_htop, "hmax", "hall")

        def f2_act_first(act):
            act.preload_act_table(ACT.Gelu)
            filled(act, f2s, "wt", T0)
            nc.scalar.activation(win2, ps(0), ACT.Copy).then_inc(free[0], 1)
            act.wait_ge(f2_gelu, 1)
            for i in range(CHUNKS):
                for c in range(FC):
                    k = f2h.bank(f"h{i}{c}", T0)
                    filled(act, f2h, f"h{i}{c}", T0)
                    nc.scalar.activation(hid2[:, c, i * C1:(i + 1) * C1], ps(k), ACT.Gelu, bias=vec("f2_bin", c), scale=sm("gelu", c, 1)) \
                        .then_inc(free[k], 1)
            act.wait_ge(f2_hscale, 1)

        def f2_pe(pe, step):
            t = step - 1
            if t.valid(TILES):
                k = f2.bank("out", t)
                fill(pe, f2, "out", t)
                pe.wait_ge(f2_hq, t.times(1, 1))
                for c in range(FC):
                    m = nc.tensor.matmul(ps(k, D), hq2[:, t.n % 2, c, :], wout2[:, c, :], start=c == 0, stop=c == FC - 1)
                m.then_inc(full[k], 1)
            t = step - 2
            if t.valid(TILES):
                tail_f2.turn(pe, t)

        def f2_act(act, step):
            t = step
            if t.valid(TILES):
                if t.n >= 2:
                    act.wait_ge(f2_hq, (t - 2).times(1, 1))
                h = hid2[:, :, t.n * P:(t.n + 1) * P] if t.pair is None else hid2[:, :, bass.ds(t.times(P), P)]
                act.sem_inc(sem("act_carried"), 1)
                nc.scalar.activation(hr2[:, t.n % 2, :, :], h, ACT.Identity, bias=MAGIC, scale=sm("h_scale")).then_inc(f2_rounded, 1)
            t = step - 2
            if t.valid(TILES):
                tail_f2.store(act, t)

        def f2_dve(dve, step):
            t = step
            if t.valid(TILES):
                if t.n >= 2:
                    filled(dve, f2, "out", t - 2)
                dve.wait_ge(f2_rounded, t.times(1, 1))
                nc.vector.tensor_scalar(hq2[:, t.n % 2, :, :], hr2[:, t.n % 2, :, :], MAGIC, 32767.0, ALU.subtract, ALU.min).then_inc(f2_hq, 1)
            t = step - 1
            if t.valid(TILES):
                tail_f2.add(dve, t, scale=sm("h_inv"))
                tail_f2.apply(dve, t)

        def f2_pool(pool, step):
            t = step - 1
            if t.valid(TILES):
                tail_f2.root(pool, t)
                tail_f2.add_bias(pool, t)

        pe_parts.append(f2_pe_first)
        act_parts.append(f2_act_first)
        dve_parts.append(f2_dve_first)
        pe_parts.append(lambda e: run_steps(e, TILES, 2, lambda s: f2_pe(e, s)))
        act_parts.append(lambda e: run_steps(e, TILES, 2, lambda s: f2_act(e, s)))
        dve_parts.append(lambda e: run_steps(e, TILES, 2, lambda s: f2_dve(e, s)))
        pool_parts.append(lambda e: run_steps(e, TILES, 2, lambda s: f2_pool(e, s)))

        tail_a3 = attention(3, tail_f2, [])

        f3g = banks.plan([("gate", 4, 0)], 1, 0)
        f3 = banks.plan([("pa", (0, 2), 1), ("pb", (1, 3), 1)], TILES, 1)
        used["n"] = 0
        xs3 = carve(2 * P).rearrange("p (u t) -> p u t", u=2)
        prod3 = carve(2 * E * D).rearrange("p (u e d) -> p u e d", u=2, e=E)
        y3 = carve(2 * D).rearrange("p (u d) -> p u d", u=2)
        lg3, m3, w3, oh3 = (carve(TILES * E).rearrange("p (t e) -> p t e", e=E) for _ in range(4))
        ix3 = carve(TILES * E).bitcast(U32).rearrange("p (t e) -> p t e", e=E)
        ixf3 = carve(TILES * 2).rearrange("p (t k) -> p t k", k=2)
        gap3, ex3, w03, w13 = (carve(TILES) for _ in range(4))
        f3_step, f3_gap, f3_exp, f3_xs, f3_scaled, f3_half, f3_summed, f3_added = (
            sem(f"f3_{x}") for x in ("step", "gap", "exp", "xs", "scaled", "half", "summed", "added"))

        def f3_pe_first(pe):
            have(pe, "w3f")
            fill(pe, f3g, "gate", T0)
            stored(pe, tail_a3.plan, "lnt", At(TILES - 1))
            for n in range(TILES):
                m = nc.tensor.matmul(ps(4, E, n * E), lnT[:, n * P:(n + 1) * P], mat(w3f, W3F, "gate"), start=True, stop=True)
            m.then_inc(full[4], 1)

        def f3_act_first(act):
            act.wait_ge(f3_gap, 1)
            nc.scalar.activation(ex3, gap3, ACT.Exp).then_inc(f3_exp, 1)

        def f3_dve_first(dve):
            count = [0]

            def link(m):
                count[0] += 1
                m.then_inc(f3_step, 1)
                dve.wait_ge(f3_step, count[0])

            filled(dve, f3g, "gate", T0)
            nc.vector.tensor_copy(lg3, ps(4, TILES * E)).then_inc(free[4], 1)
            stored(dve, f3g, "gate", T0)
            for n in range(TILES):
                m = nc.vector.max(m3[:, n, :], lg3[:, n, :])
            link(m)
            nc.vector.tensor_tensor(gap3, m3[:, :, 1], m3[:, :, 0], ALU.subtract).then_inc(f3_gap, 1)
            for n in range(TILES):
                m = nc.vector.max_index(ix3[:, n, :], m3[:, n, :], lg3[:, n, :])
            link(m)
            link(nc.vector.tensor_copy(ixf3, ix3[:, :, 0:2]))
            dve.wait_ge(f3_exp, 1)
            link(nc.vector.tensor_scalar(w03, ex3, 1.0, None, ALU.add))
            link(nc.vector.reciprocal(w03, w03))
            link(nc.vector.tensor_tensor(w13, ex3, w03, ALU.mult))
            iota = mat(const, CONST, "iota").unsqueeze(1).to_broadcast((P, TILES, E))
            for k, (o, w) in enumerate(((w3, w03), (oh3, w13))):
                link(nc.vector.tensor_tensor(o, iota, ixf3[:, :, k:k + 1].to_broadcast((P, TILES, E)), ALU.is_equal))
                link(nc.vector.tensor_tensor(o, o, w.unsqueeze(2).to_broadcast((P, TILES, E)), ALU.mult))
            link(nc.vector.tensor_tensor(w3, w3, oh3, ALU.add))

        def f3_pe(pe, step):
            t = step - 1
            if t.valid(TILES):
                pe.wait_ge(f3_xs, t.times(1, 1))
                for i, job in enumerate(("pa", "pb")):
                    k = f3.bank(job, t)
                    fill(pe, f3, job, t)
                    nc.tensor.matmul(ps(k), xs3[:, t.n % 2, :], mat(w3f, W3F, "w")[:, i * 512:(i + 1) * 512], start=True, stop=True) \
                        .then_inc(full[k], 1)

        def f3_act(act, step):
            t = step
            if t.valid(TILES):
                if t.n >= 2:
                    filled(act, f3, "pb", t - 2)
                act.sem_inc(sem("act_carried"), 1)
                nc.scalar.activation(xs3[:, t.n % 2, :], cols(lnT, t), ACT.Copy).then_inc(f3_xs, 1)

        def f3_dve(dve, step):
            t = step - 1
            if t.valid(TILES):
                u = t.n % 2
                if t.n >= 2:
                    dve.wait_ge(f3_summed, (t - 2).times(1, 1))
                filled(dve, f3, "pa", t)
                filled(dve, f3, "pb", t)
                w = w3[:, t.n, :] if t.pair is None else w3.rearrange("p t e -> p (t e)")[:, bass.ds(t.times(E), E)]
                nc.vector.tensor_tensor(prod3[:, u, :, :], psum[:, 2 * u:2 * u + 2, :].rearrange("p a (e d) -> p (a e) d", d=D),
                                        w.unsqueeze(2).to_broadcast((P, E, D)), ALU.mult).then_inc(f3_scaled, 1)
                dve.wait_ge(f3_scaled, t.times(1, 1))
                dve.sem_inc(free[f3.bank("pa", t)], 1)
                dve.sem_inc(free[f3.bank("pb", t)], 1)
            t = step - 3
            if t.valid(TILES):
                dve.wait_ge(f3_summed, t.times(1, 1))
                nc.vector.tensor_tensor(xt(t), xt(t), y3[:, t.n % 2, :], ALU.add).then_inc(f3_added, 1)

        def f3_pool(pool, step):
            t = step - 2
            if t.valid(TILES):
                u = t.n % 2
                p = prod3[:, u, :, :].rearrange("p e d -> p (e d)")
                pool.wait_ge(f3_scaled, t.times(1, 1))
                pool.tensor_tensor(p[:, 0:512], p[:, 0:512], p[:, 512:1024], ALU.add).then_inc(f3_half, 1)
                pool.wait_ge(f3_half, t.times(2, 1))
                pool.tensor_tensor(p[:, 0:256], p[:, 0:256], p[:, 256:512], ALU.add).then_inc(f3_half, 1)
                pool.wait_ge(f3_half, t.times(2, 2))
                if t.n >= 2:
                    pool.wait_ge(f3_added, (t - 2).times(1, 1))
                pool.tensor_tensor(y3[:, u, :], p[:, 0:128], p[:, 128:256], ALU.add).then_inc(f3_summed, 1)

        pe_parts.append(f3_pe_first)
        act_parts.append(f3_act_first)
        dve_parts.append(f3_dve_first)
        pe_parts.append(lambda e: run_steps(e, TILES, 3, lambda s: f3_pe(e, s)))
        act_parts.append(lambda e: run_steps(e, TILES, 3, lambda s: f3_act(e, s)))
        dve_parts.append(lambda e: run_steps(e, TILES, 3, lambda s: f3_dve(e, s)))
        pool_parts.append(lambda e: run_steps(e, TILES, 3, lambda s: f3_pool(e, s)))

        out_stored = sem("out_stored")
        STORES = 4

        def sp_store(sp):
            for i in range(STORES):
                n = TILES // STORES
                sp.wait_ge(f3_added, n * (i + 1))
                sp.dma_start(out[:, i * n * D:(i + 1) * n * D], x_tok[:, i * n * D:(i + 1) * n * D]).then_inc(out_stored, 16)
            sp.wait_ge(out_stored, 16 * STORES)

        sp_parts.append(sp_store)
        block = ctx.enter_context(nc.Block())

        @block.sync
        def _(sp):
            for part in sp_parts:
                part(sp)

        @block.tensor
        def _(pe):
            for part in pe_parts:
                part(pe)

        @block.scalar
        def _(act):
            for part in act_parts:
                part(act)

        @block.vector
        def _(dve):
            for part in dve_parts:
                part(dve)

        @block.gpsimd
        def _(pool):
            for part in pool_parts:
                part(pool)


def _tokens(a):
    return np.ascontiguousarray(np.asarray(a).reshape(TILES, P, D).transpose(1, 0, 2).reshape(P, TILES * D))


def _columns(at, n, blocks):
    a = np.zeros((P, n), np.float32)
    for name, block in blocks.items():
        s, w = at[name]
        block = np.asarray(block).reshape(-1, w)
        a[:block.shape[0], s:s + w] = block
    return a


def _chunks(a, c):
    a = np.asarray(a)
    return a.reshape(c, P, -1).transpose(1, 0, 2).reshape(P, -1)


def _constants():
    p = np.arange(P)
    q, k = p[:, None] % S, np.arange(S)[None, :]
    sel = np.zeros((P, EC, P))
    for c in range(EC):
        for e in range(2):
            sel[2 * c + e, c, e * HE:(e + 1) * HE] = 1
    selw = np.zeros((P, 2, P))
    selw[0, 0, :] = 1
    selw[1, 1, :] = 1
    return _columns(CONST, NCONST, {
        "ident": np.eye(P), "two": (p[:, None] % S == np.arange(S)[None, :]), "head": (p[:, None] // DH2 == np.arange(H2)[None, :]),
        "half": (p[:, None] // S == np.arange(2)[None, :]), "iota": np.tile(np.arange(E), (P, 1)),
        "m1": np.where(p[:, None] // S == p[None, :] // S, 0.0, OFF), "m2": np.where(k > q, OFF, 0.0),
        "m3": (np.abs(q - k) > WIN // 2), "sel": sel.reshape(P, -1), "selw": selw.reshape(P, -1)})


def _heads(a):
    return _chunks(a, 8)


def kernel(**i):
    import concourse.bacc as bacc
    from concourse.bass_utils import run_bass_kernel_spmd as run

    i = {k: np.asarray(v) for k, v in i.items()}
    x0, a1, f1, a2, a3 = "L0_xattn_", "L1_xattn_", "L1_ffn_", "L2_xattn_", "L3_xattn_"
    vecs = {"ln1_g": i[x0 + "ln1_g"], "ln1_b": i[x0 + "ln1_b"], "ln2_g": i[x0 + "ln2_g"], "ln2_b": i[x0 + "ln2_b"],
            "f0_g": i["L0_ffn_ln_gamma"], "f0_b": i["L0_ffn_ln_beta"], "f0_b1": i["L0_ffn_fc1_bias"].reshape(FC, P).T,
            "f2_bin": i["L2_ffn_b_in"].reshape(FC, P).T, "b_r1": i[f1 + "b_r1"], "b_h1": i[f1 + "b_h1"],
            "b_h2": np.broadcast_to(i[f1 + "b_h2"], (P,)), "b_e1": i[f1 + "expert_b1"].reshape(EC, P).T,
            "b_s1": i[f1 + "b_s1"], "b_s2": i[f1 + "b_s2"].reshape(3, P).T, "b_f1": i[f1 + "b_f1"].reshape(2, P).T,
            "b_f2": i[f1 + "b_f2"], "iw": i[f1 + "integration_weight"], "mu": i[f1 + "mu"],
            "shared": np.broadcast_to(i[f1 + "shared_weight"], (P,))}
    for n, a in (("a1", a1), ("a2", a2), ("a3", a3)):
        vecs |= {f"{n}_b{w}": i[f"{a}b{w}"] for w in "qkv"}
    rows = {"f0_b2": i["L0_ffn_fc2_bias"], "a1_bo": i[a1 + "bo"], "a2_bo": i[a2 + "bo"], "a3_bo": i[a3 + "bo"],
            "f2_bo": i["L2_ffn_b_out"], "f0_s1": i["L0_ffn_fc1_scales"], "f0_s2": i["L0_ffn_fc2_scales"], "b_r2": i[f1 + "b_r2"]}
    wkv = i[x0 + "Wkv"]
    e1 = i[f1 + "expert_w1"].transpose(1, 0, 2).reshape(2 * D, E * HE)
    arrays = {
        "x_tok": _tokens(i["x"]), "ctx_tok": _tokens(i["ctx_1024"]),
        "cT": i["ctx_1024"].reshape(B * S, D).T,
        "vecs": _columns(VECS, NVECS, vecs),
        "rows": _columns(ROWS, NROWS, {k: v.reshape(1, -1) for k, v in rows.items()})[0],
        "w0": _columns(W0, NW0, {"q": _heads(i[x0 + "Wq"].T), "k": _heads(wkv[:, :1024].T),
                                 "v": _heads(wkv[:, 1024:].T), "o": _heads(i[x0 + "Wo"])}),
        "w0q": np.stack([i["L0_ffn_fc1_q"], _chunks(i["L0_ffn_fc2_q"], FC)], axis=1),
        "wa": _columns(WA, NWA, {f"{n}{w}": i[f"{a}W{w}"].T for n, a in (("a1", a1), ("a2", a2), ("a3", a3)) for w in "qkvo"}),
        "w1f": _columns(W1F, NW1F, {
            "e1x": e1[:D], "e1v": e1[D:], "e2": _chunks(i[f1 + "expert_w2"].reshape(E * HE, 3 * D), EC),
            "s1x": i[f1 + "w_s1"][:D], "s1v": i[f1 + "w_s1"][D:], "s2": i[f1 + "w_s2"], "r1": i[f1 + "w_r1"],
            "r2": i[f1 + "w_r2"], "h1": i[f1 + "w_h1"], "h2": np.broadcast_to(i[f1 + "w_h2"], (32, P)),
            "f1": i[f1 + "w_f1"], "f2": _chunks(i[f1 + "w_f2"], 2)}),
        "b_e2": i[f1 + "expert_b2"],
        "w2f": _columns(W2F, NW2F, {"in": _chunks(i["L2_ffn_W_in"].T, FC), "out": _chunks(i["L2_ffn_W_out"], FC)}),
        "w3f": _columns(W3F, NW3F, {"gate": i["L3_ffn_gate_w"].T, "w": i["L3_ffn_weight"].transpose(1, 0, 2).reshape(D, E * D)}),
        "const": _constants(),
    }
    nc = bacc.Bacc("TRN2", target_bir_lowering=False, num_devices=1)
    ins, args = {}, {}
    for name, a in arrays.items():
        a = np.ascontiguousarray(a)
        ins[f"in_{name}"] = a
        args[name] = nc.dram_tensor(f"in_{name}", a.shape, mybir.dt.from_np(a.dtype), kind="ExternalInput").ap()
    out = nc.dram_tensor("out_0", (P, TILES * D), F32, kind="ExternalOutput").ap()
    build(nc, args, out)
    r = run(nc, [ins], core_ids=[0])
    got = r.results[0]["out_0"]
    return np.ascontiguousarray(got.reshape(P, TILES, D).transpose(1, 0, 2)).reshape(B, S, D)
```

```python
from contextlib import ExitStack

import numpy as np
import concourse.bass as bass
from concourse import mybir

F32 = mybir.dt.float32
BF16 = mybir.dt.bfloat16
I32 = mybir.dt.int32
U32 = mybir.dt.uint32
ALU = mybir.AluOpType
ACT = mybir.ActivationFunctionType
AX = mybir.AxisListType

B, S, D = 32, 64, 128
P = 128
TILES = B * S // P
BANKS = 8
EPS = 1e-5
OFF = -1e30

H0, DH0 = 16, 64
H2 = 16
DH2 = D // H2
WIN = 32
F0 = 512
FC = F0 // P
E, HE = 8, 64
EC = E * HE // P
C1 = 512
MAGIC = 12582912.0


class At:

    def __init__(self, n, pair=None):
        self.n, self.pair = n, pair

    def __sub__(self, k):
        return At(self.n - k, self.pair)

    def times(self, a, b=0):
        v = a * self.n + b
        return v if self.pair is None else self.pair * (2 * a) + v

    def valid(self, tiles):
        return 0 <= self.n < tiles


class Banks:

    def __init__(self):
        self.count = [0] * BANKS

    def plan(self, order, tiles, last):
        fills = Fills({job: b if isinstance(b, tuple) else (b, b) for job, b, _ in order})
        for step in range(tiles + last):
            for job, _, lag in order:
                if 0 <= step - lag < tiles:
                    k = fills.banks[job][(step - lag) % 2]
                    fills.at[job, step - lag] = self.count[k]
                    self.count[k] += 1
        fills.per_pair = [sum((b[0] == k) + (b[1] == k) for b in fills.banks.values()) for k in range(BANKS)]
        return fills

    def plan_chunks(self, jobs, place, before, body, after, pairs):
        fills = Fills({})
        for (job, parity), k in place.items():
            fills.banks.setdefault(job, [None, None])[parity] = k
        loops = [[(x, n + 2 * p) for x, n in body] for p in range(pairs - 1)]
        for x, n in before + [xn for loop in loops for xn in loop] + after:
            for job in jobs.get(x, []):
                k = place[job, n % 2]
                fills.at[job, n] = self.count[k]
                self.count[k] += 1
        fills.per_pair = [sum(place[job, n % 2] == k for x, n in body for job in jobs.get(x, [])) for k in range(BANKS)]
        return fills


class Fills:
    def __init__(self, banks):
        self.at, self.banks, self.per_pair = {}, banks, None

    def bank(self, job, t):
        return self.banks[job][t.n % 2]

    def before(self, job, t, more=0):
        v = self.at[job, t.n] + more
        return v if t.pair is None else t.pair * self.per_pair[self.bank(job, t)] + v


def run_steps(engine, tiles, last, body):
    lead = last + last % 2
    for n in range(lead):
        body(At(n))
    if tiles > lead:
        with engine.Fori(0, (tiles - lead) // 2) as pair:
            body(At(lead, pair))
            body(At(lead + 1, pair))
    for n in range(max(tiles, lead), tiles + last):
        body(At(n))


def pack(parts):
    at, n = {}, 0
    for name, width in parts:
        at[name] = (n, width)
        n += width
    return at, n


VECS, NVECS = pack([
    ("ln1_g", 1), ("ln1_b", 1), ("ln2_g", 1), ("ln2_b", 1), ("f0_g", 1), ("f0_b", 1), ("f0_b1", FC),
    ("a1_bq", 1), ("a1_bk", 1), ("a1_bv", 1), ("a2_bq", 1), ("a2_bk", 1), ("a2_bv", 1),
    ("a3_bq", 1), ("a3_bk", 1), ("a3_bv", 1), ("f2_bin", FC),
    ("b_r1", 1), ("b_h1", 1), ("b_h2", 1), ("b_e1", EC), ("b_s1", 1), ("b_s2", 3), ("b_f1", 2),
    ("b_f2", 1), ("iw", 1), ("mu", 1), ("shared", 1),
])
ROWS, NROWS = pack([("f0_b2", D), ("a1_bo", D), ("a2_bo", D), ("a3_bo", D), ("f2_bo", D),
                    ("f0_s1", F0), ("f0_s2", FC * D), ("b_r2", E)])
W0, NW0 = pack([("q", 1024), ("k", 1024), ("v", 1024), ("o", 1024)])
WA, NWA = pack([(f"{a}{w}", D) for a in ("a1", "a2", "a3") for w in "qkvo"])
W1F, NW1F = pack([("e1x", 512), ("e1v", 512), ("e2", EC * 384), ("s1x", HE), ("s1v", HE), ("s2", 384),
                  ("r1", 32), ("r2", E), ("h1", 32), ("h2", P), ("f1", 256), ("f2", 256)])
W2F, NW2F = pack([("in", F0), ("out", F0)])
W3F, NW3F = pack([("gate", E), ("w", E * D)])
CONST, NCONST = pack([("ident", P), ("two", HE), ("head", H2), ("half", 2), ("iota", E), ("m1", P),
                      ("m2", S), ("m3", S), ("sel", EC * P), ("selw", 2 * P)])


def build(nc, A, out, stop=99):
    banks = Banks()
    ctx = ExitStack()
    with ctx:
        def sb(name, shape, dt=F32):
            return ctx.enter_context(nc.sbuf_tensor(name, shape, dt))

        sems = {}

        def sem(name):
            if name not in sems:
                sems[name] = ctx.enter_context(nc.semaphore(name))
            return sems[name]

        x_tok = sb("x_tok", [P, TILES * D])
        lnT = sb("lnT", [P, B * S])
        cT = sb("cT", [P, B * S])
        ctx_tok = sb("ctx_tok", [P, TILES * D])
        vecs = sb("vecs", [P, NVECS])
        rows = sb("rows", [P, NROWS])
        w0 = sb("w0", [P, NW0])
        wa = sb("wa", [P, NWA])
        w1f = sb("w1f", [P, NW1F])
        w2f = sb("w2f", [P, NW2F])
        w3f = w0[:, 0:NW3F]
        const = sb("const", [P, NCONST])
        w0q = sb("w0q", [P, 2, F0], I32)

        def col(table, at, name, i=0, n=1):
            s, _ = at[name]
            return table[:, s + i:s + i + n]

        def vec(name, i=0):
            return col(vecs, VECS, name, i)

        def over(table, sizes):
            views, n = [], 0
            for size in sizes:
                views.append(table[:, n:n + size])
                n += size
            return views

        def mat(table, at, name):
            s, n = at[name]
            return table[:, s:s + n]

        ident = mat(const, CONST, "ident")

        identb = sb("identb", [P, P], BF16)
        m1b = sb("m1b", [P, P], BF16)
        m23b = sb("m23b", [P, 2, 512], BF16)
        sclA = sb("sclA", [P, H0, D])
        prjB = sb("prjB", [P, H0, D])
        f0w1 = sb("f0w1", [P, F0])
        f0w2 = sb("f0w2", [P, FC, D])
        f0hb = sb("f0hb", [P, D])
        bqs = sb("bqs", [P, 3])
        epsv = sb("epsv", [P, 2])

        selb = sb("selb", [96, EC, P], BF16)
        be2b = sb("be2b", [96, 3 * D], BF16)
        DERIVED = ("sw", "omsw", "hba", "hbg", "hbh2", "hiw", "tanh", "x")
        derived = sb("derived", [P, len(DERIVED)])

        def dv(name):
            return derived[:, DERIVED.index(name):DERIVED.index(name) + 1]

        NORMS = 5
        st = sb("st", [P, 2, NORMS, 6])
        mv = sb("mv", [P, 2, NORMS, 2])
        ve = sb("ve", [P, 2, NORMS])
        rstd = sb("rstd", [P, 2, NORMS])
        yln = sb("yln", [P, 2, NORMS, D])

        ARENA = 18 * 1024 - 512
        arena = sb("arena", [P, ARENA])
        used = {"n": 0}

        def carve(n, start=None, dt=None):
            if start is not None:
                used["n"] = start
            a = arena[:, used["n"]:used["n"] + n]
            used["n"] += n
            assert used["n"] <= ARENA, used
            return a

        be2 = arena[0:96, ARENA - 3 * D:ARENA]
        be2p = arena[0:96, ARENA - 3 * D - 9 * D // 2:ARENA - 3 * D].bitcast(BF16).rearrange("p (q o) -> p q o", q=3)

        psum = ctx.enter_context(nc.psum_tensor("psum", [P, BANKS, 512], F32))

        def ps(k, n=512, m=0):
            return psum[:, k, m:m + n]

        full = [sem(f"bank_full{k}") for k in range(BANKS)]
        free = [sem(f"bank_free{k}") for k in range(BANKS)]

        def fill(pe, plan, job, t):
            pe.wait_ge(free[plan.bank(job, t)], plan.before(job, t, 1))

        def filled(eng, plan, job, t):
            eng.wait_ge(full[plan.bank(job, t)], plan.before(job, t, 1))

        def stored(eng, plan, job, t):
            eng.wait_ge(free[plan.bank(job, t)], plan.before(job, t, 2))

        pe_parts, act_parts, dve_parts, pool_parts, sp_parts = [], [], [], [], []

        LOADS = [("w0qk", w0[:, 0:2048], A["w0qk"]), ("vecs", vecs[:, :], A["vecs"]), ("const", const[:, :], A["const"]),
                 ("x_tok", x_tok[:, :], A["x_tok"]), ("w0vo", w0[:, 2048:4096], A["w0vo"]),
                 ("ctx_tok", ctx_tok[:, :], A["ctx_tok"]), ("rows", rows[:, :], A["rows"].partition_broadcast(P)),
                 ("w0q", w0q[:, :, :], A["w0q"]), ("cT", cT[:, :], A["cT"]), ("wa", wa[:, :], A["wa"]),
                 ("w1f", w1f[:, :], A["w1f"]), ("w2f", w2f[:, :], A["w2f"])]
        LATER = [("w3f", w3f, A["w3f"])]
        loaded = {name: sem(f"loaded_{name}") for name, _, _ in LOADS + LATER}

        def have(eng, *names):
            for n in names:
                eng.wait_ge(loaded[n], 16)

        def sp_load(sp):
            for name, dst, src in LOADS:
                sp.dma_start(dst, src).then_inc(loaded[name], 16)

        def sp_load_be2(sp):
            sp.wait_ge(zeroed, 1)
            for q in range(3):
                sp.dma_start(be2[32 * q:32 * q + E, :], A["b_e2"]).then_inc(loaded_be2, 16)

        sp_parts.append(sp_load)
        sp_parts.append(sp_load_be2)

        setup_plan = banks.plan([(f"A{c}", c, 0) for c in range(4)] + [(f"B{c}", 4 + c, 0) for c in range(4)], 1, 0)
        consts_ready = sem("consts_ready")
        bqs_ready = sem("bqs_ready")
        f0w_ready = sem("f0w_ready")
        f0_int = sem("f0_int")
        f1_derived_ready = sem("f1_derived_ready")
        sw_tanh = sem("sw_tanh")
        derived_step = sem("derived_step")
        zeroed = sem("zeroed")
        loaded_be2 = sem("loaded_be2")
        T0 = At(0)

        def pool_setup(pool):
            for k in range(BANKS):
                pool.memset(epsv[:, 0:1] if k % 2 == 0 else epsv[:, 1:2], EPS if k % 2 == 0 else -0.5) \
                    .then_inc(free[k], 1) if k < 2 else pool.sem_inc(free[k], 1)
            pool.wait_ge(free[0], 1)
            pool.wait_ge(free[1], 1)
            pool.memset(be2[:, :], 0.0).then_inc(zeroed, 1)

        def pe_setup(pe):
            have(pe, "w0qk")
            for c in range(4):
                fill(pe, setup_plan, f"A{c}", T0)
                for j in range(4):
                    h = 8 * (c // 2) + 2 * j + c % 2
                    p = 64 * (h % 2)
                    m = nc.tensor.matmul(ps(c, D, j * D), mat(w0, W0, "q")[p:p + 64, (h // 2) * D:(h // 2 + 1) * D],
                                         mat(w0, W0, "k")[p:p + 64, (h // 2) * D:(h // 2 + 1) * D], start=True, stop=True)
                m.then_inc(full[c], 1)
            have(pe, "w0vo")
            for c in range(4):
                fill(pe, setup_plan, f"B{c}", T0)
                for j in range(4):
                    h = 8 * (c // 2) + 2 * j + c % 2
                    p = 64 * (h % 2)
                    m = nc.tensor.matmul(ps(4 + c, D, j * D), mat(w0, W0, "v")[p:p + 64, (h // 2) * D:(h // 2 + 1) * D],
                                         mat(w0, W0, "o")[p:p + 64, (h // 2) * D:(h // 2 + 1) * D], start=True, stop=True)
                m.then_inc(full[4 + c], 1)

        def act_setup(act):
            act.preload_act_table(ACT.Exp)
            for c in range(4):
                filled(act, setup_plan, f"A{c}", T0)
                nc.scalar.activation(sclA[:, 8 * (c // 2) + c % 2:8 * (c // 2) + 8:2, :], ps(c).rearrange("p (h d) -> p h d", h=4), ACT.Copy, scale=1.0 / 8.0).then_inc(free[c], 1)
            have(act, "vecs")
            nc.scalar.activation(dv("tanh"), vec("shared"), ACT.Tanh, scale=0.5).then_inc(sw_tanh, 1)
            for n, scale in enumerate((D ** -0.5, DH2 ** -0.5, DH2 ** -0.5)):
                nc.scalar.activation(bqs[:, n:n + 1], vec(f"a{n + 1}_bq"), ACT.Copy, scale=scale).then_inc(bqs_ready, 1)

        def dve_setup(dve):
            have(dve, "const")
            nc.vector.tensor_copy(identb[:, :], ident)
            nc.vector.tensor_copy(m1b[:, :], mat(const, CONST, "m1"))
            for n in range(2):
                m = nc.vector.tensor_copy(m23b[:, n, :].rearrange("p (h k) -> p h k", k=S),
                                          mat(const, CONST, f"m{n + 2}").unsqueeze(1).to_broadcast((P, 8, S)))
            m.then_inc(consts_ready, 1)
            nc.vector.tensor_copy(selb[:, :, :], mat(const, CONST, "sel")[0:96, :])

        def dve_setup_b(dve):
            for c in range(4):
                filled(dve, setup_plan, f"B{c}", T0)
                nc.vector.tensor_copy(prjB[:, 8 * (c // 2) + c % 2:8 * (c // 2) + 8:2, :], ps(4 + c).rearrange("p (h d) -> p h d", h=4)).then_inc(free[4 + c], 1)

        def dve_setup_f0(dve):
            have(dve, "w0q", "rows")
            nc.vector.tensor_copy(f0w1[:, :], w0q[:, 0, :]).then_inc(f0_int, 1)
            nc.vector.tensor_copy(f0w2[:, :, :], w0q[:, 1, :]).then_inc(f0_int, 1)
            nc.vector.tensor_scalar(f0hb[:, :], mat(rows, ROWS, "f0_b2"), 0.5, None, ALU.mult).then_inc(f0_int, 1)
            dve.wait_ge(f0_int, 2)
            nc.vector.scalar_tensor_tensor(out=f0w1[:, :], in0=f0w1[:, :], scalar=-128.0, in1=mat(rows, ROWS, "f0_s1"),
                                           op0=ALU.add, op1=ALU.mult).then_inc(f0w_ready, 1)
            nc.vector.tensor_scalar(f0w2[:, :, :], f0w2[:, :, :], -128.0, 0.5, ALU.add, ALU.mult).then_inc(f0_int, 1)
            dve.wait_ge(f0_int, 4)
            nc.vector.tensor_tensor(f0w2[:, :, :].rearrange("p c d -> p (c d)"), f0w2[:, :, :].rearrange("p c d -> p (c d)"),
                                    mat(rows, ROWS, "f0_s2"), ALU.mult).then_inc(f0w_ready, 1)

        def dve_setup2(dve):
            have(dve, "vecs")
            link_n = [0]

            def link(m):
                link_n[0] += 1
                m.then_inc(derived_step, 1)
                dve.wait_ge(derived_step, link_n[0])

            nc.vector.tensor_scalar(dv("hba"), vec("b_s2", 0), 0.5, None, ALU.mult)
            nc.vector.tensor_scalar(dv("hbg"), vec("b_s2", 2), 0.5, None, ALU.mult)
            nc.vector.tensor_scalar(dv("hbh2"), vec("b_h2"), 0.5, None, ALU.mult)
            nc.vector.tensor_scalar(dv("hiw"), vec("iw"), 0.5, None, ALU.mult)
            dve.wait_ge(sw_tanh, 1)
            nc.vector.tensor_scalar(dv("omsw"), dv("tanh"), -0.5, 0.5, ALU.mult, ALU.add)
            nc.vector.tensor_scalar(dv("sw"), dv("tanh"), 0.5, 0.5, ALU.mult, ALU.add).then_inc(f1_derived_ready, 1)
            dve.wait_ge(loaded_be2, 48)
            link(nc.vector.tensor_copy(be2p[:, 0, :], be2[:, :]))
            link(nc.vector.tensor_tensor(be2[:, :], be2[:, :], be2p[:, 0, :], ALU.subtract))
            link(nc.vector.tensor_copy(be2p[:, 1, :], be2[:, :]))
            link(nc.vector.tensor_tensor(be2[:, :], be2[:, :], be2p[:, 1, :], ALU.subtract))
            link(nc.vector.tensor_copy(be2p[:, 2, :], be2[:, :]))
            for q in range(3):
                m = nc.vector.tensor_copy(be2b[32 * q:32 * q + 32, :], be2p[32 * q:32 * q + 32, q, :])
            m.then_inc(f1_derived_ready, 1)

        pe_parts.append(pe_setup)
        act_parts.append(act_setup)
        dve_parts.append(dve_setup)
        pool_parts.append(pool_setup)

        class Norm:

            def __init__(self, name, i):
                self.i, self.tiles = i, 0
                self.stats_done, self.var_done, self.eps_added, self.rstd_done, self.y_ready = (
                    sem(f"{name}_{x}") for x in ("stats", "var", "eps", "rstd", "y"))

            def take(self):
                self.tiles += TILES
                return self.tiles - TILES

            def stats(self, dve, src, t, base):
                u, n = t.n % 2, t.times(1, base + 1)
                carry(dve, "dve")
                nc.vector.bn_stats(st[:, u, self.i, :], src).then_inc(self.stats_done, 1)
                dve.wait_ge(self.stats_done, n)
                carry(dve, "dve")
                nc.vector.bn_aggr(mv[:, u, self.i, :], st[:, u, self.i, :]).then_inc(self.var_done, 1)

            def root(self, pool, t, base):
                u, n = t.n % 2, t.times(1, base + 1)
                pool.wait_ge(self.var_done, n)
                pool.tensor_tensor(ve[:, u, self.i:self.i + 1], mv[:, u, self.i, 1:2], epsv[:, 0:1], ALU.add) \
                    .then_inc(self.eps_added, 1)
                pool.wait_ge(self.eps_added, n)
                pool.tensor_tensor(rstd[:, u, self.i:self.i + 1], ve[:, u, self.i:self.i + 1], epsv[:, 1:2], ALU.pow) \
                    .then_inc(self.rstd_done, 1)

            def apply(self, dve, src, t, base):
                u, n = t.n % 2, t.times(1, base + 1)
                dve.wait_ge(self.rstd_done, n)
                nc.vector.tensor_scalar(yln[:, u, self.i, :], src, mv[:, u, self.i, 0:1], rstd[:, u, self.i:self.i + 1],
                                        ALU.subtract, ALU.mult).then_inc(self.y_ready, 1)

        def carry(eng, name):
            eng.sem_inc(sem(f"{name}_carried"), 1)

        normA = Norm("norm", 0)
        normB = Norm("norm2", 1)
        norm0 = Norm("norm0", 2)
        norm02 = Norm("norm02", 3)
        normC = Norm("normc", 4)
        normF = Norm("normf", 2)

        tails = []

        def cols(table, t, n=P):
            return table[:, t.n * n:(t.n + 1) * n] if t.pair is None else table[:, bass.ds(t.times(n), n)]

        def xt(t):
            return cols(x_tok, t)

        class Tail:

            def __init__(self, plan, bias, double=False, affine=None, ready=None, job="lnt", norm=None):
                self.job, self.norm = job, norm or normA
                self.ready = ready
                self.plan, self.bias, self.double, self.affine = plan, bias, double, affine
                self.l = len(tails)
                self.base = self.norm.take()
                self.base2 = normB.take() if double else None
                self.prev = tails[-1] if tails else None
                self.bias_added = sem(f"bias_added{self.l}")
                tails.append(self)

            def add(self, dve, t, job="out", scale=None, stats=True):
                k = self.plan.bank(job, t)
                filled(dve, self.plan, job, t)
                if self.prev is not None and self.prev.bias:
                    n = len(self.prev.bias)
                    dve.wait_ge(self.prev.bias_added, t.times(n, n))
                if scale is None:
                    nc.vector.tensor_tensor(xt(t), xt(t), ps(k, P), ALU.add).then_inc(free[k], 1)
                else:
                    nc.vector.scalar_tensor_tensor(out=xt(t), in0=ps(k, P), scalar=scale, in1=xt(t),
                                                   op0=ALU.mult, op1=ALU.add).then_inc(free[k], 1)
                if stats:
                    self.stats(dve, t, job)

            def stats(self, dve, t, job="out"):
                stored(dve, self.plan, job, t)
                self.norm.stats(dve, xt(t), t, self.base)

            def root(self, pool, t):
                self.norm.root(pool, t, self.base)

            def turned(self, dve, t):
                k = self.plan.bank(self.job, t)
                if t.n >= 2:
                    filled(dve, self.plan, self.job, t - 2)
                elif t.pair is not None:
                    dve.wait_ge(full[k], self.plan.before(self.job, t, 1 - self.plan.per_pair[k]))

            def apply(self, dve, t):
                if not self.double:
                    self.turned(dve, t)
                self.norm.apply(dve, xt(t), t, self.base)

            def add_bias(self, pool, t):
                n = len(self.bias)
                if n:
                    pool.wait_ge(self.norm.y_ready, t.times(1, self.base + 1))
                for k, b in enumerate(self.bias):
                    b = yln[:, t.n % 2, self.norm.i, :] if isinstance(b, str) else b
                    if k:
                        pool.wait_ge(self.bias_added, t.times(n, k))
                    carry(pool, "pool")
                    pool.tensor_tensor(xt(t), xt(t), b, ALU.add).then_inc(self.bias_added, 1)

            def stats2(self, dve, t):
                dve.wait_ge(self.norm.y_ready, t.times(1, self.base + 1))
                normB.stats(dve, yln[:, t.n % 2, self.norm.i, :], t, self.base2)

            def root2(self, pool, t):
                normB.root(pool, t, self.base2)

            def apply2(self, dve, t):
                self.turned(dve, t)
                normB.apply(dve, yln[:, t.n % 2, self.norm.i, :], t, self.base2)

            def turn(self, pe, t):
                norm, base = (normB, self.base2) if self.double else (self.norm, self.base)
                k = self.plan.bank(self.job, t)
                fill(pe, self.plan, self.job, t)
                pe.wait_ge(norm.y_ready, t.times(1, base + 1))
                nc.tensor.transpose(ps(k, P), yln[:, t.n % 2, norm.i, :], ident).then_inc(full[k], 1)

            def store(self, act, t):
                k = self.plan.bank(self.job, t)
                filled(act, self.plan, self.job, t)
                if self.affine:
                    m = nc.scalar.activation(cols(lnT, t), ps(k, P), ACT.Identity, bias=vec(self.affine + "_b"),
                                             scale=vec(self.affine + "_g"))
                else:
                    m = nc.scalar.activation(cols(lnT, t), ps(k, P), ACT.Copy)
                m.then_inc(free[k], 1)
                if self.ready is not None:
                    stored(act, self.plan, self.job, t)
                    act.sem_inc(self.ready, 1)

        def lnT_of(eng, tail, t):
            if tail.ready is not None:
                eng.wait_ge(tail.ready, t.times(1, 1))
            else:
                stored(eng, tail.plan, tail.job, t)

        a0 = banks.plan([("s0a", 0, 4), ("s0b", 1, 4), ("s1a", 2, 4), ("s1b", 3, 4), ("out", 4, 5),
                         ("q0", 5, 3), ("q1", 6, 3), ("q2", 7, 3), ("t0a", 0, 4), ("t0b", 1, 4),
                         ("key", 5, 3), ("lat", 7, 2), ("lnt", 6, 7), ("u0a", 4, 4), ("u0b", 5, 4),
                         ("t1a", 2, 4), ("t1b", 3, 4), ("q3", 0, 3), ("u1a", 6, 4), ("u1b", 7, 4)], TILES, 7)
        tail_a0 = Tail(a0, ["y", f0hb[:, :]], double=True, affine="f0", ready=sem("a0_lnT_ready"))
        used["n"] = 0
        kvT = carve(2 * 2 * P).rearrange("p (u b k) -> p u b k", u=2, b=2)
        kvk = carve(2 * 2 * D).rearrange("p (u b d) -> p u b d", u=2, b=2)
        q0T = carve(2 * H0 * P).rearrange("p (u b h q) -> p u b h q", u=2, b=2, h=H0)
        e0 = carve(2 * 8 * P).rearrange("p (b g k) -> p b g k", b=2, g=8)
        p0 = carve(2 * 8 * P).rearrange("p (b g k) -> p b g k", b=2, g=8)
        pT0 = carve(2 * 8 * P).rearrange("p (b g q) -> p b g q", b=2, g=8)
        u0T = carve(2 * H0 * P).rearrange("p (u h q) -> p u h q", u=2, h=H0)
        negmax0 = sb("negmax0", [P, 2, 8])
        sum0 = sb("sum0", [P, 2, 8])
        rsum0 = sb("rsum0", [P, 2, 8])
        a0_max = sem("a0_max")
        a0_rsum = sem("a0_rsum")
        a0_probs = sem("a0_probs")

        def queries(pe, t, c):
            k = a0.bank(f"q{c}", t)
            fill(pe, a0, f"q{c}", t)
            for j in range(4):
                m = nc.tensor.matmul(ps(k, P, j * P), sclA[:, 4 * c + j, :], kvT[:, t.n % 2, :, S:P], start=True, stop=True)
            m.then_inc(full[k], 1)

        def turn_probs(pe, t, b):
            for half in range(2):
                job = f"t{b}{'ab'[half]}"
                fill(pe, a0, job, t)
                pe.wait_ge(a0_probs, t.times(4, 2 * b + half + 1))
                for j in range(4):
                    m = nc.tensor.transpose(ps(a0.bank(job, t), P, j * P), p0[:, b, 4 * half + j, :], ident)
                m.then_inc(full[a0.bank(job, t)], 1)

        def weigh_keys(pe, t, b):
            for half in range(2):
                job = f"u{b}{'ab'[half]}"
                fill(pe, a0, job, t)
                stored(pe, a0, f"t{b}{'ab'[half]}", t)
                nc.tensor.matmul(ps(a0.bank(job, t)), kvk[:, t.n % 2, b, :], pT0[:, b, 4 * half:4 * half + 4, :],
                                 start=True, stop=True).then_inc(full[a0.bank(job, t)], 1)

        def a0_pe(pe, step):
            t = step - 4
            if t.valid(TILES):
                u = t.n % 2
                for b in range(2):
                    for half in range(2):
                        job = f"s{b}{'ab'[half]}"
                        fill(pe, a0, job, t)
                        if b == 0 and half == 0:
                            for c in range(4):
                                stored(pe, a0, f"q{c}", t)
                        for j in range(4):
                            h = 8 * half + 2 * j
                            m = nc.tensor.matmul(ps(a0.bank(job, t), P, j * P), q0T[:, u, b, h:h + 2, :].rearrange("p h q -> p (h q)"),
                                                 kvT[:, u, b, :], start=True, stop=True)
                        m.then_inc(full[a0.bank(job, t)], 1)
            t = step - 5
            if t.valid(TILES):
                u = t.n % 2
                fill(pe, a0, "out", t)
                for job in ("u0a", "u0b", "u1a", "u1b"):
                    stored(pe, a0, job, t)
                for h in range(H0):
                    m = nc.tensor.matmul(ps(a0.bank("out", t), D), u0T[:, u, h, :], prjB[:, h, :], start=h == 0, stop=h == H0 - 1)
                m.then_inc(full[a0.bank("out", t)], 1)
            t = step - 3
            if t.valid(TILES):
                stored(pe, a0, "lat", t)
                for c in range(3):
                    queries(pe, t, c)
            t = step - 4
            if t.valid(TILES):
                turn_probs(pe, t, 0)
            t = step - 3
            if t.valid(TILES):
                fill(pe, a0, "key", t)
                for b in range(2):
                    m = nc.tensor.transpose(ps(a0.bank("key", t), P, b * P), kvT[:, t.n % 2, b, :], ident)
                m.then_inc(full[a0.bank("key", t)], 1)
            t = step - 2
            if t.valid(TILES):
                u = t.n % 2
                fill(pe, a0, "lat", t)
                pe.wait_ge(normC.y_ready, t.times(1, 1))
                nc.tensor.transpose(ps(a0.bank("lat", t), P), yln[:, u, normC.i, :], ident)
                pe.wait_ge(norm02.y_ready, t.times(1, 1))
                nc.tensor.transpose(ps(a0.bank("lat", t), P, P), yln[:, u, norm02.i, :], ident).then_inc(full[a0.bank("lat", t)], 1)
            t = step - 7
            if t.valid(TILES):
                tail_a0.turn(pe, t)
            t = step - 4
            if t.valid(TILES):
                stored(pe, a0, "key", t)
                weigh_keys(pe, t, 0)
                turn_probs(pe, t, 1)
            t = step - 3
            if t.valid(TILES):
                queries(pe, t, 3)
            t = step - 4
            if t.valid(TILES):
                weigh_keys(pe, t, 1)

        def a0_act(act, step):
            t = step - 4
            if t.valid(TILES):
                for b in range(2):
                    for half in range(2):
                        filled(act, a0, f"s{b}{'ab'[half]}", t)
                    act.wait_ge(a0_max, t.times(2, b + 1))
                    for half in range(2):
                        k = a0.bank(f"s{b}{'ab'[half]}", t)
                        for j in range(4):
                            g = 4 * half + j
                            m = nc.scalar.activation(e0[:, b, g, :], ps(k, P, j * P), ACT.Exp, bias=negmax0[:, b, g:g + 1],
                                                     accum_out=sum0[:, b, g:g + 1])
                        m.then_inc(free[k], 1)
            t = step - 4
            if t.valid(TILES):
                k = a0.bank("t0a", t)
                filled(act, a0, "t0a", t)
                nc.scalar.activation(pT0[:, 0, 0:4, :], ps(k), ACT.Copy).then_inc(free[k], 1)
            t = step - 3
            if t.valid(TILES):
                k = a0.bank("key", t)
                filled(act, a0, "key", t)
                nc.scalar.activation(kvk[:, t.n % 2, :, :], ps(k, 2 * P), ACT.Copy).then_inc(free[k], 1)
            t = step - 2
            if t.valid(TILES):
                u, k = t.n % 2, a0.bank("lat", t)
                filled(act, a0, "lat", t)
                nc.scalar.activation(kvT[:, u, :, 0:S], ps(k, P).rearrange("p (b k) -> p b k", b=2), ACT.Identity,
                                     bias=vec("ln1_b"), scale=vec("ln1_g"))
                nc.scalar.activation(kvT[:, u, :, S:P], ps(k, P, P).rearrange("p (b k) -> p b k", b=2), ACT.Identity,
                                     bias=vec("ln2_b"), scale=vec("ln2_g")).then_inc(free[k], 1)
            t = step - 7
            if t.valid(TILES):
                tail_a0.store(act, t)
            t = step - 4
            if t.valid(TILES):
                for half in range(2):
                    k = a0.bank(f"u0{'ab'[half]}", t)
                    filled(act, a0, f"u0{'ab'[half]}", t)
                    nc.scalar.activation(u0T[:, t.n % 2, 8 * half:8 * half + 8, 0 * S:1 * S],
                                         ps(k).rearrange("p (h q) -> p h q", h=8), ACT.Copy).then_inc(free[k], 1)
                k = a0.bank("t1a", t)
                filled(act, a0, "t1a", t)
                nc.scalar.activation(pT0[:, 1, 0:4, :], ps(k), ACT.Copy).then_inc(free[k], 1)
                for half in range(2):
                    k = a0.bank(f"u1{'ab'[half]}", t)
                    filled(act, a0, f"u1{'ab'[half]}", t)
                    nc.scalar.activation(u0T[:, t.n % 2, 8 * half:8 * half + 8, 1 * S:2 * S],
                                         ps(k).rearrange("p (h q) -> p h q", h=8), ACT.Copy).then_inc(free[k], 1)

        def keep_queries(dve, t, c):
            k = a0.bank(f"q{c}", t)
            filled(dve, a0, f"q{c}", t)
            nc.vector.tensor_copy(q0T[:, t.n % 2, :, 4 * c:4 * c + 4, :], ps(k).rearrange("p (h b q) -> p b h q", h=4, b=2)) \
                .then_inc(free[k], 1)

        def keep_probs(dve, t, b):
            k = a0.bank(f"t{b}b", t)
            filled(dve, a0, f"t{b}b", t)
            nc.vector.tensor_copy(pT0[:, b, 4:8, :], ps(k)).then_inc(free[k], 1)

        SETUP_STEPS = {2: dve_setup_b, 5: dve_setup_f0, 7: dve_setup2}

        def a0_dve(dve, step):
            if step.pair is None and step.n in SETUP_STEPS:
                SETUP_STEPS[step.n](dve)
            t = step - 4
            if t.valid(TILES):
                for b in range(2):
                    filled(dve, a0, f"s{b}a", t)
                    filled(dve, a0, f"s{b}b", t)
                    nc.vector.tensor_reduce(negmax0[:, b, :], psum[:, 2 * b:2 * b + 2, :].rearrange("p a (g k) -> p (a g) k", g=4),
                                            AX.X, ALU.max, negate=True).then_inc(a0_max, 1)
            t = step
            if t.valid(TILES):
                if t.n == 0:
                    have(dve, "x_tok", "ctx_tok")
                norm0.stats(dve, xt(t), t, 0)
            t = step - 1
            if t.valid(TILES):
                normC.stats(dve, cols(ctx_tok, t), t, 0)
                norm02.stats(dve, yln[:, t.n % 2, norm0.i, :], t, 0)
            t = step - 6
            if t.valid(TILES):
                tail_a0.stats2(dve, t)
            t = step - 4
            if t.valid(TILES):
                stored(dve, a0, "s0a", t)
                stored(dve, a0, "s0b", t)
                nc.vector.reciprocal(rsum0[:, 0, :], sum0[:, 0, :]).then_inc(a0_rsum, 1)
            t = step - 5
            if t.valid(TILES):
                tail_a0.add(dve, t)
            t = step - 4
            if t.valid(TILES):
                stored(dve, a0, "s1a", t)
                stored(dve, a0, "s1b", t)
                nc.vector.reciprocal(rsum0[:, 1, :], sum0[:, 1, :]).then_inc(a0_rsum, 1)
            t = step - 3
            if t.valid(TILES):
                for c in range(3):
                    keep_queries(dve, t, c)
            t = step
            if t.valid(TILES):
                norm0.apply(dve, xt(t), t, 0)
            t = step - 4
            if t.valid(TILES):
                keep_probs(dve, t, 0)
            t = step - 1
            if t.valid(TILES):
                normC.apply(dve, cols(ctx_tok, t), t, 0)
                norm02.apply(dve, yln[:, t.n % 2, norm0.i, :], t, 0)
            t = step - 5
            if t.valid(TILES):
                tail_a0.apply(dve, t)
            t = step - 6
            if t.valid(TILES):
                tail_a0.apply2(dve, t)
            t = step - 4
            if t.valid(TILES):
                keep_probs(dve, t, 1)
            t = step - 3
            if t.valid(TILES):
                keep_queries(dve, t, 3)

        def a0_pool(pool, step):
            t = step
            if t.valid(TILES):
                norm0.root(pool, t, 0)
            t = step - 1
            if t.valid(TILES):
                normC.root(pool, t, 0)
                norm02.root(pool, t, 0)
            t = step - 6
            if t.valid(TILES):
                tail_a0.root2(pool, t)
            for b in range(2):
                t = step - 4
                if t.valid(TILES):
                    pool.wait_ge(a0_rsum, t.times(2, b + 1))
                    for half in range(2):
                        g = slice(4 * half, 4 * half + 4)
                        pool.tensor_tensor(p0[:, b, g, :], e0[:, b, g, :], rsum0[:, b, g].unsqueeze(2).to_broadcast((P, 4, P)),
                                           ALU.mult).then_inc(a0_probs, 1)
                t = step - 5
                if b == 0 and t.valid(TILES):
                    tail_a0.root(pool, t)
            t = step - 6
            if t.valid(TILES):
                if t.n == 0:
                    pool.wait_ge(f0w_ready, 1)
                tail_a0.add_bias(pool, t)

        pe_parts.append(lambda e: run_steps(e, TILES, 7, lambda s: a0_pe(e, s)))
        act_parts.append(lambda e: run_steps(e, TILES, 7, lambda s: a0_act(e, s)))
        dve_parts.append(lambda e: run_steps(e, TILES, 7, lambda s: a0_dve(e, s)))
        pool_parts.append(lambda e: run_steps(e, TILES, 7, lambda s: a0_pool(e, s)))


        f0 = banks.plan([("h", (0, 1), 0), ("out", (2, 3), 1), ("lnt", 4, 3)], TILES, 3)
        tail_f0 = Tail(f0, [mat(rows, ROWS, "a1_bo")])
        hT0 = carve(2 * FC * P).rearrange("p (u c t) -> p u c t", u=2, c=FC)

        def f0_pe(pe, step):
            t = step
            if t.valid(TILES):
                k = f0.bank("h", t)
                if t.n == 0:
                    pe.wait_ge(f0w_ready, 2)
                fill(pe, f0, "h", t)
                lnT_of(pe, tail_a0, t)
                for c in range(FC):
                    m = nc.tensor.matmul(ps(k, P, c * P), f0w1[:, c * P:(c + 1) * P], cols(lnT, t), start=True, stop=True)
                m.then_inc(full[k], 1)
            t = step - 1
            if t.valid(TILES):
                k = f0.bank("out", t)
                if t.n == 0:
                    pe.wait_ge(f0w_ready, 2)
                fill(pe, f0, "out", t)
                stored(pe, f0, "h", t)
                for c in range(FC):
                    m = nc.tensor.matmul(ps(k, D), hT0[:, t.n % 2, c, :], f0w2[:, c, :], start=c == 0, stop=c == FC - 1)
                m.then_inc(full[k], 1)
            t = step - 3
            if t.valid(TILES):
                tail_f0.turn(pe, t)

        def f0_act(act, step):
            t = step
            if t.valid(TILES):
                k = f0.bank("h", t)
                filled(act, f0, "h", t)
                for c in range(FC):
                    m = nc.scalar.activation(hT0[:, t.n % 2, c, :], ps(k, P, c * P), ACT.Silu, bias=vec("f0_b1", c))
                m.then_inc(free[k], 1)
            t = step - 3
            if t.valid(TILES):
                tail_f0.store(act, t)

        def f0_dve(dve, step):
            t = step - 1
            if t.valid(TILES):
                tail_f0.add(dve, t, stats=False)
            t = step - 2
            if t.valid(TILES):
                tail_f0.apply(dve, t)
            t = step - 1
            if t.valid(TILES):
                tail_f0.stats(dve, t)

        def f0_pool(pool, step):
            t = step - 1
            if t.valid(TILES):
                tail_f0.root(pool, t)
            t = step - 2
            if t.valid(TILES):
                tail_f0.add_bias(pool, t)

        pe_parts.append(lambda e: run_steps(e, TILES, 3, lambda s: f0_pe(e, s)))
        act_parts.append(lambda e: e.preload_act_table(ACT.Silu))
        act_parts.append(lambda e: run_steps(e, TILES, 3, lambda s: f0_act(e, s)))
        dve_parts.append(lambda e: run_steps(e, TILES, 3, lambda s: f0_dve(e, s)))
        pool_parts.append(lambda e: run_steps(e, TILES, 3, lambda s: f0_pool(e, s)))

        a1 = banks.plan([("s", (2, 3), 1), ("att", 5, 3), ("out", 6, 4), ("v", 1, 1), ("qk", 0, 0), ("pt", 4, 2),
                         ("lnt", 7, 6)], TILES, 6)
        tail_a1 = Tail(a1, [])
        buffers1 = [v.rearrange("p (u k) -> p u k", u=2) for v in over(ctx_tok, [2 * P] * 6)]
        ctile, v1, e1, p1, pT1, y1 = buffers1
        qk1 = ctx_tok[:, 12 * P:16 * P].rearrange("p (u w k) -> p u w k", u=2, w=2)
        sm1 = sb("sm1", [P, 2, 3])
        a1_ctile, a1_max, a1_exp, a1_rsum, a1_probs = (
            sem(f"a1_{x}") for x in ("ctile", "max", "exp", "rsum", "probs"))

        def wgt(n, w):
            return mat(wa, WA, f"a{n}{w}")

        def a1_pe(pe, step):
            t = step - 1
            if t.valid(TILES):
                u, k = t.n % 2, a1.bank("s", t)
                fill(pe, a1, "s", t)
                nc.tensor.matmul(ps(k, P), identb[:, :], m1b[:, :], start=True, stop=False)
                stored(pe, a1, "qk", t)
                nc.tensor.matmul(ps(k, P), qk1[:, u, 0, :], qk1[:, u, 1, :], start=False, stop=True).then_inc(full[k], 1)
            t = step - 3
            if t.valid(TILES):
                u, k = t.n % 2, a1.bank("att", t)
                fill(pe, a1, "att", t)
                stored(pe, a1, "v", t)
                stored(pe, a1, "pt", t)
                nc.tensor.matmul(ps(k, P), v1[:, u, :], pT1[:, u, :], start=True, stop=True).then_inc(full[k], 1)
            t = step - 4
            if t.valid(TILES):
                u, k = t.n % 2, a1.bank("out", t)
                fill(pe, a1, "out", t)
                stored(pe, a1, "att", t)
                nc.tensor.matmul(ps(k, D), y1[:, u, :], wgt(1, "o"), start=True, stop=True).then_inc(full[k], 1)
            t = step - 1
            if t.valid(TILES):
                u, k = t.n % 2, a1.bank("v", t)
                fill(pe, a1, "v", t)
                nc.tensor.matmul(ps(k, P), ctile[:, u, :], wgt(1, "v"), start=True, stop=True).then_inc(full[k], 1)
            t = step
            if t.valid(TILES):
                u, k = t.n % 2, a1.bank("qk", t)
                if t.n == 0:
                    have(pe, "wa")
                    pe.wait_ge(consts_ready, 1)
                fill(pe, a1, "qk", t)
                pe.wait_ge(a1_ctile, t.times(1, 1))
                nc.tensor.matmul(ps(k, P, P), wgt(1, "k"), ctile[:, u, :], start=True, stop=True)
                lnT_of(pe, tail_f0, t)
                nc.tensor.matmul(ps(k, P), wgt(1, "q"), cols(lnT, t), start=True, stop=True).then_inc(full[k], 1)
            t = step - 2
            if t.valid(TILES):
                u, k = t.n % 2, a1.bank("pt", t)
                fill(pe, a1, "pt", t)
                pe.wait_ge(a1_probs, t.times(1, 1))
                nc.tensor.transpose(ps(k, P), p1[:, u, :], ident).then_inc(full[k], 1)
            t = step - 6
            if t.valid(TILES):
                tail_a1.turn(pe, t)

        def a1_act(act, step):
            t = step - 1
            if t.valid(TILES):
                u, k = t.n % 2, a1.bank("s", t)
                act.wait_ge(a1_max, t.times(1, 1))
                nc.scalar.activation(e1[:, u, :], ps(k, P), ACT.Exp, bias=sm1[:, u, 0:1], accum_out=sm1[:, u, 1:2]) \
                    .then_inc(free[k], 1)
            t = step
            if t.valid(TILES):
                u, k = t.n % 2, a1.bank("qk", t)
                if t.n == 0:
                    act.wait_ge(bqs_ready, 3)
                filled(act, a1, "qk", t)
                nc.scalar.activation(qk1[:, u, 0, :], ps(k, P), ACT.Identity, bias=bqs[:, 0:1], scale=D ** -0.5)
                nc.scalar.activation(qk1[:, u, 1, :], ps(k, P, P), ACT.Identity, bias=vec("a1_bk")).then_inc(free[k], 1)
            t = step - 2
            if t.valid(TILES):
                u, k = t.n % 2, a1.bank("pt", t)
                filled(act, a1, "pt", t)
                nc.scalar.activation(pT1[:, u, :], ps(k, P), ACT.Copy).then_inc(free[k], 1)
            t = step - 6
            if t.valid(TILES):
                tail_a1.store(act, t)

        def a1_dve(dve, step):
            t = step - 2
            if t.valid(TILES):
                u = t.n % 2
                stored(dve, a1, "s", t)
                nc.vector.reciprocal(sm1[:, u, 2:3], sm1[:, u, 1:2]).then_inc(a1_rsum, 1)
            t = step - 1
            if t.valid(TILES):
                u, k = t.n % 2, a1.bank("s", t)
                filled(dve, a1, "s", t)
                nc.vector.tensor_reduce(sm1[:, u, 0:1], ps(k, P), AX.X, ALU.max, negate=True).then_inc(a1_max, 1)
            t = step - 2
            if t.valid(TILES):
                u = t.n % 2
                dve.wait_ge(a1_rsum, t.times(1, 1))
                nc.vector.tensor_scalar(p1[:, u, :], e1[:, u, :], sm1[:, u, 2:3], None, ALU.mult).then_inc(a1_probs, 1)
            t = step - 3
            if t.valid(TILES):
                u, k = t.n % 2, a1.bank("att", t)
                filled(dve, a1, "att", t)
                nc.vector.scalar_tensor_tensor(out=y1[:, u, :], in0=ps(k, P), scalar=vec("a1_bv"), in1=cols(lnT, t),
                                               op0=ALU.add, op1=ALU.add).then_inc(free[k], 1)
            t = step - 4
            if t.valid(TILES):
                tail_a1.add(dve, t, stats=False)
            t = step - 1
            if t.valid(TILES):
                u, k = t.n % 2, a1.bank("v", t)
                filled(dve, a1, "v", t)
                nc.vector.tensor_copy(v1[:, u, :], ps(k, P)).then_inc(free[k], 1)
            t = step - 5
            if t.valid(TILES):
                tail_a1.apply(dve, t)
            t = step - 4
            if t.valid(TILES):
                tail_a1.stats(dve, t)

        def a1_pool(pool, step):
            t = step
            if t.valid(TILES):
                if t.n == 0:
                    have(pool, "cT")
                if t.n >= 2:
                    filled(pool, a1, "v", t - 2)
                pool.tensor_copy(ctile[:, t.n % 2, :], cols(cT, t)).then_inc(a1_ctile, 1)
            t = step - 4
            if t.valid(TILES):
                tail_a1.root(pool, t)

        pe_parts.append(lambda e: run_steps(e, TILES, 6, lambda s: a1_pe(e, s)))
        act_parts.append(lambda e: e.preload_act_table(ACT.Exp))
        act_parts.append(lambda e: run_steps(e, TILES, 6, lambda s: a1_act(e, s)))
        dve_parts.append(lambda e: run_steps(e, TILES, 6, lambda s: a1_dve(e, s)))
        pool_parts.append(lambda e: run_steps(e, TILES, 6, lambda s: a1_pool(e, s)))

        PAIRS = B * S // C1 // 2
        TC = C1 // P
        SRC = ("s", 0, 1)
        ITER = range(2)
        ALPHA, BETA, GATE = range(3)

        def parts(it):
            return (BETA, GATE) if it == 0 else (ALPHA, BETA, GATE)

        def start(c):
            return [(x, c) for x in ("R", "H0", "L")]

        def turn(new, it, old, it_old, then=()):
            return ([(x, new) for x in (("O", "W") if it == 0 else ("H1",))] + [(f"D{it_old}", old), (f"M{it}", new)]
                    + [(f"S{it_old}", old), (f"U{it_old}", old), (f"E{it_old}", old), (f"Ca{it}", new), (f"Cb{it}", new)]
                    + [(f"F{it_old}", old), (f"G{it_old}", old), (f"Cc{it}", new)] + list(then) + [(f"Cd{it}", new)])

        def pair_stages(a, following):
            b = a + 1
            stages = turn(b, 0, a, 0) + turn(a, 1, b, 0)
            if following:
                return (stages + turn(b, 1, a, 1, [("Z", a), ("X", a + 2)] + start(a + 2))
                        + turn(a + 2, 0, b, 1, [("Z", b), ("X", a + 3)] + start(a + 3)))
            last = turn(b, 1, a, 1)
            last = last[:last.index(("F1", a))]
            return stages + last + [("D1", b), ("S1", b), ("U1", b), ("Cc1", b), ("Cd1", b), ("F1", a), ("E1", b), ("G1", a),
                                    ("F1", b), ("Z", a), ("G1", b), ("Z", b)]

        OWN = ["R", "H0", "L", "O", "W", "M0", "Ca0", "Cb0", "F0", "G0", "Cc0", "Cd0", "H1", "M1", "Ca1", "Cb1", "F1", "G1", "Cc1", "Cd1", "Z"]
        BEFORE = [("X", 0), ("X", 1)] + start(0) + start(1) + [(x, 0) for x in ("O", "W", "M0", "Ca0", "Cb0", "Cc0", "Cd0")]
        BODY = pair_stages(0, True)
        AFTER = pair_stages(2 * (PAIRS - 1), False)

        def controls(x):
            it = int(x[-1])
            if x[1] == "a":
                return [(s, BETA) for s in SRC]
            others = [(s, p) for p in (ALPHA, GATE) if p in parts(it) for s in SRC]
            cut = (3, 5) if it else (1, 2)
            return {"b": others[:cut[0]], "c": others[cut[0]:cut[1]], "d": others[cut[1]:]}[x[1]]

        JOBS = {"R": ["r1"], "L": ["lg"], "O": ["oh", "wt"], "W": ["cw0", "cw1"], "Z": ["xo"]}
        for it in ITER:
            JOBS[f"H{it}"] = [f"h{it}{c}" for c in range(EC)] + [f"hs{it}"]
            JOBS[f"M{it}"] = [f"m{it}{k}{c}" for k in range(2) for c in range(EC)]
            for x in (f"Ca{it}", f"Cb{it}", f"Cc{it}", f"Cd{it}"):
                JOBS[x] = [f"c{it}{s}{p}" for s, p in controls(x)]
            JOBS[f"F{it}"] = [f"hh{it}", f"f1{it}0", f"f1{it}1"]
            JOBS[f"G{it}"] = [f"ha{it}", f"f2{it}"]
        places = {(job, n): 4 * n + i % 4 for n in range(2) for i, job in enumerate(j for x in OWN for j in JOBS.get(x, []))}
        f1 = banks.plan_chunks(JOBS, places, BEFORE, BODY, AFTER, PAIRS)

        used["n"] = 0
        f1_X = carve(2 * C1).rearrange("p (n t) -> p n t", n=2)
        f1_V = carve(2 * C1).rearrange("p (n t) -> p n t", n=2)
        f1_H = carve(2 * EC * C1).rearrange("p (n c t) -> p n c t", n=2, c=EC)
        f1_Hm = carve(2 * 2 * EC * C1).rearrange("p (n k c t) -> p n k c t", n=2, k=2, c=EC)
        f1_bb = carve(2 * 3 * C1).rearrange("p (n s t) -> p n s t", n=2, s=3)
        f1_Hs = w0[:, 0:2 * C1].rearrange("p (n t) -> p n t", n=2)
        f1_cw = w0[:, 2 * C1:8 * C1].rearrange("p (n s t) -> p n s t", n=2, s=3)
        f1_tg = f1_H[:, :, 0:3, :]
        f1_ta = [sclA[:, 0:12, :].rearrange("p h d -> p (h d)").rearrange("p (s t) -> p s t", s=3),
                 prjB[:, 0:12, :].rearrange("p h d -> p (h d)").rearrange("p (s t) -> p s t", s=3)]
        f1_N = [sclA[:, 12:16, :].rearrange("p h d -> p (h d)"),
                prjB[:, 12:16, :].rearrange("p h d -> p (h d)")]
        f1_lb = sb("f1_lb", [P, 2, 3, C1])
        f1_lg = sb("f1_lg", [P, 2, TC, E])
        f1_m8 = sb("f1_m8", [P, 2, TC, 8])
        f1_ix = sb("f1_ix", [P, 2, TC, 8], U32)
        f1_ixf = sb("f1_ixf", [P, 2, TC, 2])
        f1_d = sb("f1_d", [P, 2, TC])
        f1_th = sb("f1_th", [P, 2, TC])
        f1_w = sb("f1_w", [P, 2, TC, 2])
        f1_ohT, f1_oh = over(ctx_tok, [2 * C1, 2 * TC * 96])
        f1_ohT = f1_ohT[0:96, :].bitcast(BF16).rearrange("p (n s t) -> p n s t", n=2, s=2)
        f1_oh = f1_oh.bitcast(BF16).rearrange("p (n i s e) -> p n i s e", n=2, i=TC, s=2)
        f1_wT = w0q[0:2, :, :].bitcast(F32)

        def s1(name):
            return [sem(f"f1_{name}{n}") for n in range(2)]

        f1_xin, f1_gap, f1_tanh, f1_weights, f1_onehot = (s1(x) for x in ("xin", "gap", "tanh", "weights", "onehot"))
        f1_clamped, f1_exped, f1_log, f1_err, f1_beta, f1_betaerr = (
            s1(x) for x in ("clamped", "exped", "log", "err", "beta", "betaerr"))
        f1_v, f1_xnext, f1_x = (s1(x) for x in ("v", "xnext", "x"))
        f1_chain = sem("f1_chain")
        CHAIN = 32

        def f1n(t, per, k):
            k += t.n // 2 * per
            return k if t.pair is None else t.pair * per + k

        def tiles_ready(eng, tail, t):
            eng.wait_ge(free[tail.plan.banks["lnt"][0]], t.times(TC, tail.plan.at["lnt", 0] + TC + 1))

        def w1(name, a=0, b=None, rows_=P):
            s0, n = W1F[name]
            return w1f[0:rows_, s0 + a:s0 + (n if b is None else b)]

        def f1_pe(pe, x, t):
            n = t.n % 2
            it = int(x[-1]) if x[-1].isdigit() else 0

            def start(job):
                fill(pe, f1, job, t)
                return f1.bank(job, t)

            if x == "R":
                k = start("r1")
                pe.wait_ge(f1_xin[n], f1n(t, 1, 1))
                nc.tensor.matmul(psum[0:32, k, :], w1("r1"), f1_X[:, n, :], start=True, stop=True).then_inc(full[k], 1)
            if x == "L":
                k = start("lg")
                stored(pe, f1, "r1", t)
                for i in range(TC):
                    m = nc.tensor.matmul(ps(k, E, E * i), f1_bb[0:32, n, 1, i * P:(i + 1) * P], w1("r2", rows_=32), start=True, stop=True)
                m.then_inc(full[k], 1)
            if x == "O":
                k = start("oh")
                pe.wait_ge(f1_onehot[n], f1n(t, 2, 2))
                bank = psum[0:96, k, :].bitcast(BF16)
                for s in range(2):
                    for i in range(TC):
                        m = nc.tensor.transpose(bank[:, (s * TC + i) * P:(s * TC + i + 1) * P], f1_oh[:, n, i, s, :], identb[:, :])
                m.then_inc(full[k], 1)
                k = start("wt")
                pe.wait_ge(f1_weights[n], f1n(t, 2, 2))
                for i in range(TC):
                    m = nc.tensor.transpose(psum[0:2, k, i * P:(i + 1) * P], f1_w[:, n, i, :], ident)
                m.then_inc(full[k], 1)
            if x == "W":
                stored(pe, f1, "wt", t)
                for s in range(2):
                    k = start(f"cw{s}")
                    nc.tensor.matmul(ps(k), mat(const, CONST, "selw")[0:2, s * P:(s + 1) * P], f1_wT[:, n, :], start=True, stop=True) \
                        .then_inc(full[k], 1)
            if x[0] == "H":
                if it == 0:
                    pe.wait_ge(f1_xin[n], f1n(t, 1, 1))
                else:
                    pe.wait_ge(f1_x[n], f1n(t, 2, 1))
                    pe.wait_ge(f1_v[n], f1n(t, 1, 1))
                for c in range(EC + 1):
                    k = start(f"h{it}{c}" if c < EC else f"hs{it}")
                    o, a, b = (ps(k), c * P, (c + 1) * P) if c < EC else (psum[0:HE, k, :], 0, HE)
                    wx, wv = ("e1x", "e1v") if c < EC else ("s1x", "s1v")
                    m = nc.tensor.matmul(o, w1(wx, a, b), f1_X[:, n, :], start=True, stop=it == 0)
                    if it:
                        m = nc.tensor.matmul(o, w1(wv, a, b), f1_V[:, n, :], start=False, stop=True)
                    m.then_inc(full[k], 1)
            if x[0] == "M":
                if it == 0:
                    stored(pe, f1, "oh", t)
                for s in range(2):
                    for c in range(EC):
                        k = start(f"m{it}{s}{c}")
                        nc.tensor.matmul(ps(k), selb[:, c, :], f1_ohT[:, n, s, :], start=True, stop=True).then_inc(full[k], 1)
            if x[0] == "C":
                for s, p in controls(x):
                    k = start(f"c{it}{s}{p}")
                    if s == "s":
                        stored(pe, f1, f"hs{it}", t)
                        m = nc.tensor.matmul(ps(k), w1("s2", p * D, (p + 1) * D, HE), f1_Hs[0:HE, n, :], start=True, stop=True)
                    else:
                        nc.tensor.matmul(ps(k), be2b[:, p * D:(p + 1) * D], f1_ohT[:, n, s, :], start=True, stop=False)
                        for c in range(EC):
                            if p == BETA:
                                stored(pe, f1, f"m{it}{s}{c}", t)
                            m = nc.tensor.matmul(ps(k), w1("e2", c * 384 + p * D, c * 384 + (p + 1) * D), f1_Hm[:, n, s, c, :],
                                                 start=False, stop=c == EC - 1)
                    m.then_inc(full[k], 1)
            if x[0] == "F":
                pe.wait_ge(f1_xnext[n], f1n(t, 2, it + 1))
                k = start(f"hh{it}")
                nc.tensor.matmul(psum[0:32, k, :], w1("h1"), f1_N[n], start=True, stop=True).then_inc(full[k], 1)
                for j in range(2):
                    k = start(f"f1{it}{j}")
                    nc.tensor.matmul(ps(k), w1("f1", j * P, (j + 1) * P), f1_N[n], start=True, stop=True).then_inc(full[k], 1)
            if x[0] == "G":
                k = start(f"ha{it}")
                stored(pe, f1, f"hh{it}", t)
                nc.tensor.matmul(ps(k), w1("h2", rows_=32), f1_bb[0:32, n, 0, :], start=True, stop=True).then_inc(full[k], 1)
                k = start(f"f2{it}")
                for j in range(2):
                    stored(pe, f1, f"f1{it}{j}", t)
                    m = nc.tensor.matmul(ps(k), w1("f2", j * D, (j + 1) * D), f1_bb[:, n, 1 + j, :], start=j == 0, stop=j == 1)
                m.then_inc(full[k], 1)
            if x == "Z":
                k = start("xo")
                pe.wait_ge(f1_x[n], f1n(t, 2, 2))
                for i in range(TC):
                    m = nc.tensor.transpose(ps(k, P, i * P), f1_X[:, n, i * P:(i + 1) * P], ident)
                m.then_inc(full[k], 1)

        def f1_act(act, x, t):
            n = t.n % 2
            it = int(x[-1]) if x[-1].isdigit() else 0

            def take(job):
                filled(act, f1, job, t)
                return f1.bank(job, t)

            if x == "R":
                k = take("r1")
                nc.scalar.activation(f1_bb[0:32, n, 1, :], psum[0:32, k, :], ACT.Gelu, bias=vec("b_r1")[0:32, :]).then_inc(free[k], 1)
            if x == "L":
                act.wait_ge(f1_gap[n], f1n(t, 1, 1))
                nc.scalar.activation(f1_th[:, n, :], f1_d[:, n, :], ACT.Tanh, scale=0.5).then_inc(f1_tanh[n], 1)
            if x == "O":
                k = take("oh")
                nc.scalar.activation(f1_ohT[:, n, :, :].rearrange("p s t -> p (s t)"), psum[0:96, k, :].bitcast(BF16), ACT.Copy) \
                    .then_inc(free[k], 1)
                k = take("wt")
                nc.scalar.activation(f1_wT[:, n, :], psum[0:2, k, :], ACT.Copy).then_inc(free[k], 1)
            if x == "W":
                for s in range(2):
                    k = take(f"cw{s}")
                    nc.scalar.activation(f1_cw[:, n, 1 + s, :], ps(k), ACT.Identity, scale=dv("omsw")).then_inc(free[k], 1)
            if x[0] == "H":
                for c in range(EC):
                    k = take(f"h{it}{c}")
                    nc.scalar.activation(f1_H[:, n, c, :], ps(k), ACT.Gelu, bias=vec("b_e1", c)).then_inc(free[k], 1)
                k = take(f"hs{it}")
                nc.scalar.activation(f1_Hs[0:HE, n, :], psum[0:HE, k, :], ACT.Gelu, bias=vec("b_s1")[0:HE, :]).then_inc(free[k], 1)
            if x[0] == "C":
                for s, p in controls(x):
                    i = SRC.index(s)
                    k = take(f"c{it}{s}{p}")
                    if p == BETA:
                        m = nc.scalar.activation(f1_bb[:, n, i, :], ps(k), ACT.Identity, bias=vec("b_s2", BETA) if s == "s" else 0.0)
                    else:
                        o = f1_tg[:, n, i, :] if p == GATE else f1_ta[n][:, i, :]
                        bias = (dv("hbg") if p == GATE else dv("hba")) if s == "s" else 0.0
                        m = nc.scalar.activation(o, ps(k), ACT.Tanh, bias=bias, scale=0.5)
                    m.then_inc(free[k], 1)
            if x[0] == "D":
                act.preload_act_table_set("natural_log_exp_and_others")
                act.wait_ge(f1_clamped[n], f1n(t, 2, it + 1))
                nc.scalar.activation(f1_lb[:, n, :, :], f1_lb[:, n, :, :], ACT.Exp).then_inc(f1_exped[n], 1)
                act.wait_ge(f1_exped[n], f1n(t, 2, it + 1))
                nc.scalar.activation(f1_lb[:, n, :, :], f1_lb[:, n, :, :], ACT.Ln, bias=1.0).then_inc(f1_log[n], 1)
                act.preload_act_table(ACT.Gelu)
            if x[0] == "F":
                k = take(f"hh{it}")
                nc.scalar.activation(f1_bb[0:32, n, 0, :], psum[0:32, k, :], ACT.Gelu, bias=vec("b_h1")[0:32, :]).then_inc(free[k], 1)
                for j in range(2):
                    k = take(f"f1{it}{j}")
                    nc.scalar.activation(f1_bb[:, n, 1 + j, :], ps(k), ACT.Gelu, bias=vec("b_f1", j)).then_inc(free[k], 1)
            if x[0] == "G":
                k = take(f"ha{it}")
                if it == 0:
                    act.wait_ge(f1_v[n], f1n(t, 1, 1))
                nc.scalar.activation(f1_lb[:, n, 0, :], ps(k), ACT.Tanh, bias=dv("hbh2"), scale=0.5).then_inc(free[k], 1)

        def f1_dve(dve, x, t, chain):
            n = t.n % 2
            it = int(x[-1]) if x[-1].isdigit() else 0

            def link(m):
                chain[0] += 1
                m.then_inc(f1_chain, 1)
                dve.wait_ge(f1_chain, chain[0] if t.pair is None else t.pair * CHAIN + chain[0])

            if x == "L":
                k = f1.bank("lg", t)
                filled(dve, f1, "lg", t)
                b_r2 = mat(rows, ROWS, "b_r2").unsqueeze(1).to_broadcast((P, TC, E))
                nc.vector.tensor_tensor(f1_lg[:, n, :, :], ps(k, TC * E).rearrange("p (i e) -> p i e", i=TC), b_r2, ALU.add) \
                    .then_inc(free[k], 1)
                stored(dve, f1, "lg", t)
                carry(dve, "dve")
                for i in range(TC):
                    m = nc.vector.max(f1_m8[:, n, i, :], f1_lg[:, n, i, :])
                link(m)
                nc.vector.tensor_tensor(f1_d[:, n, :], f1_m8[:, n, :, 1], f1_m8[:, n, :, 0], ALU.subtract).then_inc(f1_gap[n], 1)
                for i in range(TC):
                    m = nc.vector.max_index(f1_ix[:, n, i, :], f1_m8[:, n, i, :], f1_lg[:, n, i, :])
                link(m)
                link(nc.vector.tensor_copy(f1_ixf[:, n, :, :], f1_ix[:, n, :, 0:2]))
                iota = mat(const, CONST, "iota").unsqueeze(1).unsqueeze(1).to_broadcast((P, TC, 3, E))
                for s in range(2):
                    o = f1_oh[:, n, :, s, :].rearrange("p i (r e) -> p i r e", r=3)[:, :, :, 0:E]
                    ix = f1_ixf[:, n, :, s:s + 1].unsqueeze(3).to_broadcast((P, TC, 3, E))
                    nc.vector.tensor_tensor(o, iota, ix, ALU.is_equal).then_inc(f1_onehot[n], 1)
                dve.wait_ge(f1_tanh[n], f1n(t, 1, 1))
                for s, sign in ((0, -0.5), (1, 0.5)):
                    nc.vector.tensor_scalar(f1_w[:, n, :, s], f1_th[:, n, :], sign, 0.5, ALU.mult, ALU.add).then_inc(f1_weights[n], 1)
            if x[0] == "M":
                for s in range(2):
                    for c in range(EC):
                        k = f1.bank(f"m{it}{s}{c}", t)
                        if s == 0:
                            stored(dve, f1, f"h{it}{c}", t)
                        filled(dve, f1, f"m{it}{s}{c}", t)
                        nc.vector.tensor_tensor(f1_Hm[:, n, s, c, :], f1_H[:, n, c, :], ps(k), ALU.mult).then_inc(free[k], 1)
            if x[:2] == "Ca":
                if it == 0:
                    dve.wait_ge(f1_xin[n], f1n(t, 1, 1))
                else:
                    dve.wait_ge(f1_x[n], f1n(t, 2, 1))
                nc.vector.tensor_scalar(f1_N[n], f1_X[:, n, :], -1.0, vec("mu"), ALU.mult, ALU.add).then_inc(f1_err[n], 1)
                for s in SRC:
                    stored(dve, f1, f"c{it}{s}{BETA}", t)
                nc.vector.tensor_scalar(f1_lb[:, n, :, :], f1_bb[:, n, :, :], 40.0, None, ALU.min).then_inc(f1_clamped[n], 1)
            if x[0] == "S":
                dve.wait_ge(f1_log[n], f1n(t, 2, it + 1))
                nc.vector.tensor_tensor(f1_lb[:, n, :, :], f1_bb[:, n, :, :], f1_lb[:, n, :, :], ALU.max).then_inc(f1_beta[n], 1)
            if x[0] == "U":
                if it:
                    for s in SRC:
                        stored(dve, f1, f"c{it}{s}{ALPHA}", t)
                    v = f1_V[:, n, :].unsqueeze(1).to_broadcast((P, 3, C1))
                    link(nc.vector.scalar_tensor_tensor(out=f1_ta[n], in0=f1_ta[n], scalar=1.0, in1=v, op0=ALU.add, op1=ALU.mult))
                dve.wait_ge(f1_betaerr[n], f1n(t, 2, it + 1))
                if it:
                    link(nc.vector.scalar_tensor_tensor(out=f1_lb[:, n, :, :], in0=f1_ta[n], scalar=0.5, in1=f1_lb[:, n, :, :],
                                                        op0=ALU.mult, op1=ALU.add))
                link(nc.vector.tensor_tensor(f1_lb[:, n, :, :], f1_lb[:, n, :, :], f1_cw[:, n, :, :], ALU.mult))
            if x[0] == "E":
                for s in SRC:
                    stored(dve, f1, f"c{it}{s}{GATE}", t)
                link(nc.vector.scalar_tensor_tensor(out=f1_tg[:, n, :, :], in0=f1_tg[:, n, :, :], scalar=1.0, in1=f1_lb[:, n, :, :],
                                                    op0=ALU.add, op1=ALU.mult))
                link(nc.vector.tensor_tensor(f1_tg[:, n, 0, :], f1_tg[:, n, 0, :], f1_tg[:, n, 1, :], ALU.add))
                link(nc.vector.tensor_tensor(f1_tg[:, n, 0, :], f1_tg[:, n, 0, :], f1_tg[:, n, 2, :], ALU.add))
                nc.vector.scalar_tensor_tensor(out=f1_N[n], in0=f1_tg[:, n, 0, :], scalar=0.05, in1=f1_X[:, n, :],
                                               op0=ALU.mult, op1=ALU.add).then_inc(f1_xnext[n], 1)
                if it == 0:
                    link(nc.vector.tensor_tensor(f1_V[:, n, :], f1_lb[:, n, 0, :], f1_lb[:, n, 1, :], ALU.add))
                    nc.vector.tensor_tensor(f1_V[:, n, :], f1_V[:, n, :], f1_lb[:, n, 2, :], ALU.add).then_inc(f1_v[n], 1)
            if x[0] == "G":
                k = f1.bank(f"f2{it}", t)
                filled(dve, f1, f"f2{it}", t)
                if it == 0:
                    dve.wait_ge(f1_v[n], f1n(t, 1, 1))
                nc.vector.tensor_scalar(f1_lb[:, n, 1, :], ps(k), vec("b_f2"), dv("hiw"), ALU.add, ALU.mult).then_inc(free[k], 1)
                stored(dve, f1, f"f2{it}", t)
                stored(dve, f1, f"ha{it}", t)
                link(nc.vector.scalar_tensor_tensor(out=f1_lb[:, n, 1, :], in0=f1_lb[:, n, 0, :], scalar=1.0, in1=f1_lb[:, n, 1, :],
                                                    op0=ALU.add, op1=ALU.mult))
                nc.vector.tensor_tensor(f1_X[:, n, :], f1_X[:, n, :], f1_lb[:, n, 1, :], ALU.add).then_inc(f1_x[n], 1)
            if x == "Z":
                k = f1.bank("xo", t)
                filled(dve, f1, "xo", t)
                nc.vector.tensor_tensor(cols(x_tok, t, C1), cols(x_tok, t, C1), ps(k), ALU.add).then_inc(free[k], 1)

        def f1_pool(pool, x, t):
            n = t.n % 2
            if x == "X":
                tiles_ready(pool, tail_a1, t)
                pool.tensor_copy(f1_X[:, n, :], cols(lnT, t, C1)).then_inc(f1_xin[n], 1)
            if x[0] == "S":
                it = int(x[-1])
                pool.wait_ge(f1_err[n], f1n(t, 2, it + 1))
                pool.wait_ge(f1_beta[n], f1n(t, 2, it + 1))
                err = f1_N[n].unsqueeze(1).to_broadcast((P, 3, C1))
                pool.tensor_tensor(f1_lb[:, n, :, :], f1_lb[:, n, :, :], err, ALU.mult).then_inc(f1_betaerr[n], 1)
            if x == "Z":
                filled(pool, f1, "xo", t)

        def f1_run(engine, stage, meanwhile=lambda: None):
            chain = [0]
            for x, n in BEFORE:
                stage(x, At(n), chain)
            meanwhile()
            start = chain[0]
            with engine.Fori(0, PAIRS - 1) as pair:
                for x, n in BODY:
                    stage(x, At(n, pair), chain)
            assert chain[0] - start in (0, CHAIN), chain
            chain[0] = start + (PAIRS - 1) * (chain[0] - start)
            for x, n in AFTER:
                stage(x, At(n), chain)

        def f1_dve_setup(dve):
            dve.wait_ge(f1_derived_ready, 1)
            nc.vector.memset(f1_oh, 0.0)
            for n in range(2):
                nc.vector.tensor_scalar(f1_cw[:, n, 0, :], f1_cw[:, n, 0, :], 0.0, dv("sw"), ALU.mult, ALU.add)

        def f1_pe_first(pe):
            have(pe, "w1f")
            pe.wait_ge(f1_derived_ready, 2)

        pe_parts.append(f1_pe_first)
        pe_parts.append(lambda e: f1_run(e, lambda x, t, c: f1_pe(e, x, t)))
        act_parts.append(lambda e: e.wait_ge(f1_derived_ready, 1))
        act_parts.append(lambda e: e.preload_act_table(ACT.Gelu))
        act_parts.append(lambda e: f1_run(e, lambda x, t, c: f1_act(e, x, t)))
        dve_parts.append(f1_dve_setup)
        dve_parts.append(lambda e: f1_run(e, lambda x, t, c: f1_dve(e, x, t, c), lambda: f2_dve_weights(e)))
        pool_parts.append(lambda e: f1_run(e, lambda x, t, c: f1_pool(e, x, t)))

        def f1_over(eng):
            for n in range(2 * PAIRS - 2, 2 * PAIRS):
                stored(eng, f1, "xo", At(n))

        def sp_load_later(sp):
            f1_over(sp)
            for name, dst, src in LATER:
                sp.dma_start(dst, src).then_inc(loaded[name], 16)

        sp_parts.append(sp_load_later)

        HALF = H2 // 2
        used["n"] = 0
        km = carve(2 * 2 * H2 * S).rearrange("p (u b h k) -> p u b h k", u=2, b=2, h=H2)
        qz = carve(2 * 2 * P).rearrange("p (u b q) -> p u b q", u=2, b=2)
        kT2 = carve(2 * P).rearrange("p (u k) -> p u k", u=2)
        e2 = carve(2 * H2 * S).rearrange("p (u h k) -> p u h k", u=2, h=H2)
        pn2 = carve(2 * H2 * S).rearrange("p (u h k) -> p u h k", u=2, h=H2)
        pT2 = carve(HALF * P).rearrange("p (g q) -> p g q", g=HALF)
        Vx = carve(2 * 2 * HALF * 32).rearrange("p (u g c) -> p u g c", u=2, c=32)
        cdup = carve(2 * 2 * P).rearrange("p (u b r k) -> p u b r k", u=2, b=2, r=2)
        oT2 = carve(P)
        max2, sum2, rsum2 = (carve(H2) for _ in range(3))

        def attention(n, before, bias, own=None):
            late = 0 if own is None else 2
            jobs = [("s0", 0, 2), ("out", 6, 6), ("av", 4, 5), ("s1", 1, 2), ("v", 5, 4), ("qk", 6, 0),
                    ("t0", 2, 4), ("t1", 3, 4), ("lnt", 7, 8)]
            jobs = [(job, k, lag + late) for job, k, lag in jobs] + ([("lnt0", 7, 1)] if late else [])
            a = banks.plan(jobs, TILES, 8 + late)
            if late:
                before = Tail(a, own, job="lnt0", norm=normF)
            tail = Tail(a, bias)
            cleared, spread, maxed, exped, summed, inverted, pool_probs, dve_probs, doubled = (
                sem(f"a{n}_{x}") for x in ("cleared", "spread", "max", "exp", "sum", "rsum", "probs_pool", "probs_dve", "ctx2"))

            def heads(i):
                return slice(i * HALF, (i + 1) * HALF)

            def pe_scores(pe, t, i):
                u, k = t.n % 2, a.bank(f"s{i}", t)
                fill(pe, a, f"s{i}", t)
                nc.tensor.matmul(ps(k), identb[:, :], m23b[:, n - 2, :], start=True, stop=False)
                if i == 0:
                    pe.wait_ge(spread, t.times(1, 1))
                for b in range(2):
                    m = nc.tensor.matmul(ps(k), qz[:, u, b, :], km[:, u, b, heads(i), :].rearrange("p h k -> p (h k)"),
                                         start=False, stop=b == 1)
                m.then_inc(full[k], 1)

            def on_pe(pe, first):
                step = first - late
                t = step - 2
                if t.valid(TILES):
                    pe_scores(pe, t, 0)
                t = step - 6
                if t.valid(TILES):
                    k = a.bank("out", t)
                    fill(pe, a, "out", t)
                    stored(pe, a, "av", t)
                    nc.tensor.matmul(ps(k, D), oT2, wgt(n, "o"), start=True, stop=True).then_inc(full[k], 1)
                t = step - 5
                if t.valid(TILES):
                    k = a.bank("av", t)
                    fill(pe, a, "av", t)
                    stored(pe, a, "v", t)
                    for i in range(2):
                        stored(pe, a, f"t{i}", t)
                    for b in range(2):
                        for g in range(HALF):
                            r = slice(g // 2 * 32, g // 2 * 32 + 32)
                            m = nc.tensor.matmul(psum[r, k, b * S:(b + 1) * S], Vx[:, t.n % 2, b * HALF + g, :], pT2[:, g, b * S:(b + 1) * S],
                                                 start=g % 2 == 0, stop=g % 2 == 1)
                    m.then_inc(full[k], 1)
                t = step - 2
                if t.valid(TILES):
                    pe_scores(pe, t, 1)
                t = step - 8
                if late and t.valid(TILES):
                    tail.turn(pe, t)
                t = step - 4
                if t.valid(TILES):
                    k = a.bank("v", t)
                    fill(pe, a, "v", t)
                    pe.wait_ge(doubled, t.times(1, 1))
                    for b in range(2):
                        m = nc.tensor.matmul(ps(k, D, b * D), cdup[:, t.n % 2, b, :, :].rearrange("p r k -> p (r k)"), wgt(n, "v"),
                                             start=True, stop=True)
                    m.then_inc(full[k], 1)
                t = step
                if t.valid(TILES):
                    k = a.bank("qk", t)
                    if t.n == 0:
                        have(pe, "cT")
                    fill(pe, a, "qk", t)
                    nc.tensor.matmul(ps(k, P, P), wgt(n, "k"), cols(cT, t), start=True, stop=True)
                    lnT_of(pe, before, t)
                    nc.tensor.matmul(ps(k, P), wgt(n, "q"), cols(lnT, t), start=True, stop=True).then_inc(full[k], 1)
                t = step - 4
                if t.valid(TILES):
                    pe.wait_ge(pool_probs, t.times(1, 1))
                    pe.wait_ge(dve_probs, t.times(1, 1))
                    for i in range(2):
                        k = a.bank(f"t{i}", t)
                        fill(pe, a, f"t{i}", t)
                        for j in range(4):
                            h = i * HALF + 2 * j
                            m = nc.tensor.transpose(ps(k, P, j * P), pn2[:, t.n % 2, h:h + 2, :].rearrange("p h k -> p (h k)"), ident)
                        m.then_inc(full[k], 1)
                if late and (first - 1).valid(TILES):
                    before.turn(pe, first - 1)
                if not late and (step - 8).valid(TILES):
                    tail.turn(pe, step - 8)

            def act_exp(act, t, i):
                stored(act, a, f"s{i}", t)
                nc.scalar.activation(e2[:, t.n % 2, heads(i), :], e2[:, t.n % 2, heads(i), :], ACT.Exp).then_inc(exped, 1)

            def on_act(act, first):
                step = first - late
                t = step - 3
                if t.valid(TILES):
                    if t.n >= 2:
                        filled(act, a, "v", t - 2)
                    act.sem_inc(sem("act_carried"), 1)
                    nc.scalar.activation(cdup[:, t.n % 2, :, :, :],
                                         cols(cT, t).rearrange("p (b k) -> p b k", b=2).unsqueeze(2).to_broadcast((P, 2, 2, S)),
                                         ACT.Copy).then_inc(doubled, 1)
                t = step - 2
                if t.valid(TILES):
                    act_exp(act, t, 0)
                t = step - 5
                if t.valid(TILES):
                    k = a.bank("av", t)
                    filled(act, a, "av", t)
                    nc.scalar.activation(oT2, ps(k, P), ACT.Identity, bias=vec(f"a{n}_bv")).then_inc(free[k], 1)
                t = step - 2
                if t.valid(TILES):
                    act_exp(act, t, 1)
                t = step - 8
                if late and t.valid(TILES):
                    tail.store(act, t)
                t = step
                if t.valid(TILES):
                    u, k = t.n % 2, a.bank("qk", t)
                    if t.n == 0:
                        act.wait_ge(cleared, 2)
                    filled(act, a, "qk", t)
                    for b in range(2):
                        nc.scalar.activation(qz[:, u, b, b * S:(b + 1) * S], ps(k, S, b * S), ACT.Identity, bias=bqs[:, n - 1:n],
                                             scale=DH2 ** -0.5)
                    nc.scalar.activation(kT2[:, u, :], ps(k, P, P), ACT.Identity, bias=vec(f"a{n}_bk")).then_inc(free[k], 1)
                t = step - 4
                if t.valid(TILES):
                    for i in range(2):
                        k = a.bank(f"t{i}", t)
                        filled(act, a, f"t{i}", t)
                        nc.scalar.activation(pT2[:, 4 * i:4 * i + 4, :], ps(k), ACT.Copy).then_inc(free[k], 1)
                if late and (first - 1).valid(TILES):
                    before.store(act, first - 1)
                if not late and (step - 8).valid(TILES):
                    tail.store(act, step - 8)

            def dve_scores(dve, t, i):
                k = a.bank(f"s{i}", t)
                s = ps(k).rearrange("p (h k) -> p h k", h=HALF)
                filled(dve, a, f"s{i}", t)
                nc.vector.tensor_reduce(max2[:, heads(i)], s, AX.X, ALU.max).then_inc(maxed, 1)
                if i == 0 and t.n >= 2:
                    dve.wait_ge(pool_probs, (t - 2).times(1, 1))
                dve.wait_ge(maxed, t.times(2, i + 1))
                nc.vector.tensor_tensor(e2[:, t.n % 2, heads(i), :], s, max2[:, heads(i)].unsqueeze(2).to_broadcast((P, HALF, S)),
                                        ALU.subtract).then_inc(free[k], 1)

            def on_dve(dve, first):
                step = first - late
                if late and first.valid(TILES):
                    if first.n == 0:
                        f1_over(dve)
                    before.norm.stats(dve, xt(first), first, before.base)
                t = step - 7
                if t.valid(TILES):
                    tail.apply(dve, t)
                t = step - 3
                if t.valid(TILES):
                    dve.wait_ge(exped, t.times(2, 2))
                    nc.vector.tensor_reduce(sum2, e2[:, t.n % 2, :, :], AX.X, ALU.add).then_inc(summed, 1)
                t = step - 2
                if t.valid(TILES):
                    dve_scores(dve, t, 0)
                t = step - 3
                if t.valid(TILES):
                    if t.n >= 1:
                        dve.wait_ge(pool_probs, (t - 1).times(1, 1))
                    dve.wait_ge(summed, t.times(1, 1))
                    nc.vector.reciprocal(rsum2, sum2).then_inc(inverted, 1)
                t = step - 6
                if t.valid(TILES):
                    tail.add(dve, t, stats=False)
                t = step - 3
                if t.valid(TILES):
                    if t.n >= 2:
                        filled(dve, a, "t1", t - 2)
                    dve.wait_ge(inverted, t.times(1, 1))
                    nc.vector.tensor_tensor(pn2[:, t.n % 2, heads(1), :], e2[:, t.n % 2, heads(1), :],
                                            rsum2[:, heads(1)].unsqueeze(2).to_broadcast((P, HALF, S)), ALU.mult).then_inc(dve_probs, 1)
                t = step - 6
                if t.valid(TILES):
                    tail.stats(dve, t)
                t = step - 2
                if t.valid(TILES):
                    dve_scores(dve, t, 1)
                if late and first.valid(TILES):
                    before.apply(dve, first)
                t = step - 4
                if t.valid(TILES):
                    k = a.bank("v", t)
                    filled(dve, a, "v", t)
                    if t.n == 0:
                        dve.wait_ge(cleared, 2)
                    for r in range(2):
                        rows_ = slice(r * S, (r + 1) * S)
                        c = slice(r * DH2, (r + 1) * DH2)
                        m = nc.vector.tensor_copy(
                            Vx[rows_, t.n % 2, :, :].rearrange("p g c -> p (g c)").rearrange("p (g q c) -> p g q c", q=4, c=16)[:, :, 0:4:3, c],
                            ps(k, 2 * D)[rows_, :].rearrange("p (g q c) -> p g q c", q=2, c=16)[:, :, :, c])
                    m.then_inc(free[k], 1)

            def on_pool(pool, first):
                step = first - late
                if late and first.valid(TILES):
                    before.root(pool, first)
                t = step - 1
                if t.valid(TILES):
                    u = t.n % 2
                    stored(pool, a, "qk", t)
                    if t.n >= 2:
                        filled(pool, a, "s1", t - 2)
                    pool.tensor_tensor(km[:, u, :, :, :], kT2[:, u, :].rearrange("p (b k) -> p b k", b=2).unsqueeze(2).to_broadcast((P, 2, H2, S)),
                                       mat(const, CONST, "head").unsqueeze(1).unsqueeze(3).to_broadcast((P, 2, H2, S)), ALU.mult) \
                        .then_inc(spread, 1)
                t = step - 3
                if t.valid(TILES):
                    if t.n >= 2:
                        filled(pool, a, "t0", t - 2)
                    pool.wait_ge(inverted, t.times(1, 1))
                    pool.tensor_tensor(pn2[:, t.n % 2, heads(0), :], e2[:, t.n % 2, heads(0), :],
                                       rsum2[:, heads(0)].unsqueeze(2).to_broadcast((P, HALF, S)), ALU.mult).then_inc(pool_probs, 1)
                t = step - 6
                if t.valid(TILES):
                    tail.root(pool, t)
                t = step - 7
                if t.valid(TILES):
                    tail.add_bias(pool, t)
                if late and (first - 1).valid(TILES):
                    before.add_bias(pool, first - 1)

            def pool_clear(pool):
                if n == 2:
                    f1_over(pool)
                pool.memset(qz.rearrange("p u b q -> p (u b q)"), 0.0).then_inc(cleared, 1)
                pool.memset(Vx.rearrange("p u g c -> p (u g c)"), 0.0).then_inc(cleared, 1)

            pe_parts.append(lambda e: run_steps(e, TILES, 8 + late, lambda s: on_pe(e, s)))
            act_parts.append(lambda e: e.preload_act_table(ACT.Exp))
            act_parts.append(lambda e: run_steps(e, TILES, 8 + late, lambda s: on_act(e, s)))
            dve_parts.append(lambda e: run_steps(e, TILES, 8 + late, lambda s: on_dve(e, s)))
            pool_parts.append(pool_clear)
            pool_parts.append(lambda e: run_steps(e, TILES, 8 + late, lambda s: on_pool(e, s)))
            return tail

        tail_a2 = attention(2, None, [mat(rows, ROWS, "f2_bo")], own=[mat(rows, ROWS, "a2_bo")])

        CHUNKS = B * S // C1
        used["n"] = 0
        hid2 = carve(FC * B * S).rearrange("p (c t) -> p c t", c=FC)
        hq2 = carve(2 * FC * P).rearrange("p (u c t) -> p u c t", u=2, c=FC)
        hr2 = carve(2 * FC * P).rearrange("p (u c t) -> p u c t", u=2, c=FC)
        win2 = carve(F0)
        win2t, wout2 = (mat(w2f, W2F, name).rearrange("p (c k) -> p c k", c=FC) for name in ("in", "out"))
        small, n_small = pack([("win_inv", FC), ("win_scale", FC), ("wout_inv", FC), ("wout_scale", FC), ("gelu", FC),
                               ("x_max", 1), ("x_all", 1), ("x_scale", 1), ("x_inv", 1),
                               ("h_maxes", FC * CHUNKS), ("h_max", 1), ("h_all", 1), ("h_scale", 1), ("h_inv", 1)])
        small2 = sb("small2", [P, n_small])

        def sm(name, i=0, n=None):
            s0, w = small[name]
            return small2[:, s0 + i:s0 + (w if n is None else i + n)]

        f2s = banks.plan([("wt", 0, 0), ("xmax", 1, 0), ("xall", 2, 0)], 1, 0)
        f2h = banks.plan([(f"h{i}{c}", 4 * (i % 2) + c, 0) for i in range(CHUNKS) for c in range(FC)]
                         + [("hmax", 0, 0), ("hall", 1, 0)], 1, 0)
        f2 = banks.plan([("out", (2, 3), 2), ("lnt", 7, 5)], TILES, 5)
        tail_f2 = Tail(f2, [mat(rows, ROWS, "a3_bo")])
        f2_step = sem("f2_step")
        f2_wt, f2_xmax, f2_xtop, f2_xq, f2_gelu, f2_wout, f2_hmax, f2_htop, f2_hscale, f2_rounded, f2_hq = (
            sem(f"f2_{x}") for x in ("wt", "xmax", "xtop", "xq", "gelu", "wout", "hmax", "htop", "hscale", "rounded", "hq"))
        ones_row = mat(const, CONST, "selw")[0:1, 0:P]

        f2_links = [0]

        def f2_link(dve, m):
            f2_links[0] += 1
            m.then_inc(f2_step, 1)
            dve.wait_ge(f2_step, f2_links[0])

        def f2_dve_weights(dve):
            def link(m):
                f2_link(dve, m)

            have(dve, "w2f")
            for name, w, inv, scale in (("in", win2t, "win_inv", "win_scale"), ("out", wout2, "wout_inv", "wout_scale")):
                link(nc.vector.tensor_reduce(sm(inv), w, AX.X, ALU.max, apply_absolute_value=True))
                link(nc.vector.tensor_scalar(sm(inv), sm(inv), 1e-8, None, ALU.max))
                link(nc.vector.reciprocal(sm(scale), sm(inv)))
                link(nc.vector.tensor_scalar(sm(scale), sm(scale), 127.0, None, ALU.mult))
                link(nc.vector.tensor_scalar(sm(inv), sm(inv), 1.0 / 127.0, None, ALU.mult))
                link(nc.vector.tensor_tensor(w, w, sm(scale).unsqueeze(2).to_broadcast((P, FC, D)), ALU.mult))
                link(nc.vector.tensor_scalar(w, w, MAGIC, None, ALU.add))
                m = nc.vector.tensor_scalar(w, w, MAGIC, 127.0, ALU.subtract, ALU.min)
                if name == "in":
                    m.then_inc(f2_wt, 1)
                else:
                    link(m)
            nc.vector.tensor_tensor(wout2, wout2, sm("wout_inv").unsqueeze(2).to_broadcast((P, FC, D)), ALU.mult).then_inc(f2_wout, 1)

        def f2_dve_first(dve):
            def link(m):
                f2_link(dve, m)

            def top(name, plan, job, done):
                k = plan.bank(job, T0)
                filled(dve, plan, job, T0)
                nc.vector.tensor_reduce(sm(name)[0:1, :], psum[0:1, k, 0:P], AX.X, ALU.max).then_inc(done, 1)
                dve.wait_ge(done, 1)
                dve.sem_inc(free[k], 1)

            def scale_of(name, plan, job):
                k = plan.bank(job, T0)
                filled(dve, plan, job, T0)
                link(nc.vector.tensor_scalar(sm(f"{name}_all"), ps(k, 1), 1e-8, None, ALU.max))
                dve.sem_inc(free[k], 1)
                link(nc.vector.reciprocal(sm(f"{name}_scale"), sm(f"{name}_all")))
                link(nc.vector.tensor_scalar(sm(f"{name}_scale"), sm(f"{name}_scale"), 32767.0, None, ALU.mult))
                link(nc.vector.tensor_scalar(sm(f"{name}_inv"), sm(f"{name}_all"), 1.0 / 32767.0, None, ALU.mult))

            stored(dve, tail_a2.plan, "lnt", At(TILES - 1))
            nc.vector.tensor_reduce(sm("x_max"), lnT[:, :], AX.X, ALU.max, apply_absolute_value=True).then_inc(f2_xmax, 1)
            top("x_max", f2s, "xmax", f2_xtop)
            scale_of("x", f2s, "xall")
            nc.vector.tensor_scalar(sm("gelu"), sm("win_inv"), sm("x_inv"), None, ALU.mult).then_inc(f2_gelu, 1)
            for i in range(CHUNKS):
                x = lnT[:, i * C1:(i + 1) * C1]
                link(nc.vector.tensor_scalar(x, x, sm("x_scale"), MAGIC, ALU.mult, ALU.add))
                nc.vector.tensor_scalar(x, x, MAGIC, 32767.0, ALU.subtract, ALU.min).then_inc(f2_xq, 1)
            for i in range(CHUNKS - 1):
                for c in range(FC):
                    stored(dve, f2h, f"h{i}{c}", T0)
                nc.vector.tensor_reduce(sm("h_maxes", FC * i, FC), hid2[:, :, i * C1:(i + 1) * C1], AX.X, ALU.max,
                                        apply_absolute_value=True)
            i = CHUNKS - 1
            for c in range(FC):
                stored(dve, f2h, f"h{i}{c}", T0)
                m = nc.vector.tensor_reduce(sm("h_maxes", FC * i + c, 1), hid2[:, c, i * C1:(i + 1) * C1], AX.X, ALU.max,
                                            apply_absolute_value=True)
            link(m)
            nc.vector.tensor_reduce(sm("h_max"), sm("h_maxes"), AX.X, ALU.max).then_inc(f2_hmax, 1)
            top("h_max", f2h, "hmax", f2_htop)
            scale_of("h", f2h, "hall")
            dve.sem_inc(f2_hscale, 1)

        def f2_pe_first(pe):
            def all_largest(name, plan, own, top, job, job_all):
                pe.wait_ge(own, 1)
                fill(pe, plan, job, T0)
                nc.tensor.transpose(psum[0:1, plan.bank(job, T0), 0:P], sm(name), ident).then_inc(full[plan.bank(job, T0)], 1)
                pe.wait_ge(top, 1)
                fill(pe, plan, job_all, T0)
                nc.tensor.matmul(ps(plan.bank(job_all, T0), 1), ones_row, sm(name)[0:1, :], start=True, stop=True) \
                    .then_inc(full[plan.bank(job_all, T0)], 1)

            pe.wait_ge(f2_wt, 1)
            fill(pe, f2s, "wt", T0)
            for c in range(FC):
                m = nc.tensor.transpose(ps(0, P, c * P), win2t[:, c, :], ident)
            m.then_inc(full[0], 1)
            all_largest("x_max", f2s, f2_xmax, f2_xtop, "xmax", "xall")
            stored(pe, f2s, "wt", T0)
            for i in range(CHUNKS):
                pe.wait_ge(f2_xq, i + 1)
                for c in range(FC):
                    k = f2h.bank(f"h{i}{c}", T0)
                    fill(pe, f2h, f"h{i}{c}", T0)
                    nc.tensor.matmul(ps(k), win2[:, c * P:(c + 1) * P], lnT[:, i * C1:(i + 1) * C1], start=True, stop=True).then_inc(full[k], 1)
            all_largest("h_max", f2h, f2_hmax, f2_htop, "hmax", "hall")

        def f2_act_first(act):
            act.preload_act_table(ACT.Gelu)
            filled(act, f2s, "wt", T0)
            nc.scalar.activation(win2, ps(0), ACT.Copy).then_inc(free[0], 1)
            act.wait_ge(f2_gelu, 1)
            for i in range(CHUNKS):
                for c in range(FC):
                    k = f2h.bank(f"h{i}{c}", T0)
                    filled(act, f2h, f"h{i}{c}", T0)
                    nc.scalar.activation(hid2[:, c, i * C1:(i + 1) * C1], ps(k), ACT.Gelu, bias=vec("f2_bin", c), scale=sm("gelu", c, 1)) \
                        .then_inc(free[k], 1)
            act.wait_ge(f2_hscale, 1)

        def f2_pe(pe, step):
            t = step - 2
            if t.valid(TILES):
                k = f2.bank("out", t)
                fill(pe, f2, "out", t)
                pe.wait_ge(f2_hq, t.times(1, 1))
                for c in range(FC):
                    m = nc.tensor.matmul(ps(k, D), hq2[:, t.n % 2, c, :], wout2[:, c, :], start=c == 0, stop=c == FC - 1)
                m.then_inc(full[k], 1)
            t = step - 5
            if t.valid(TILES):
                tail_f2.turn(pe, t)

        def f2_act(act, step):
            t = step
            if t.valid(TILES):
                if t.n >= 2:
                    act.wait_ge(f2_hq, (t - 2).times(1, 1))
                h = hid2[:, :, t.n * P:(t.n + 1) * P] if t.pair is None else hid2[:, :, bass.ds(t.times(P), P)]
                act.sem_inc(sem("act_carried"), 1)
                nc.scalar.activation(hr2[:, t.n % 2, :, :], h, ACT.Identity, bias=MAGIC, scale=sm("h_scale")).then_inc(f2_rounded, 1)
            t = step - 5
            if t.valid(TILES):
                tail_f2.store(act, t)

        def f2_dve(dve, step):
            t = step - 1
            if t.valid(TILES):
                if t.n >= 2:
                    filled(dve, f2, "out", t - 2)
                dve.wait_ge(f2_rounded, t.times(1, 1))
                nc.vector.tensor_scalar(hq2[:, t.n % 2, :, :], hr2[:, t.n % 2, :, :], MAGIC, 32767.0, ALU.subtract, ALU.min).then_inc(f2_hq, 1)
            t = step - 3
            if t.valid(TILES):
                tail_f2.add(dve, t, scale=sm("h_inv"), stats=False)
            t = step - 4
            if t.valid(TILES):
                tail_f2.apply(dve, t)
            t = step - 3
            if t.valid(TILES):
                tail_f2.stats(dve, t)

        def f2_pool(pool, step):
            t = step - 3
            if t.valid(TILES):
                tail_f2.root(pool, t)
            t = step - 4
            if t.valid(TILES):
                tail_f2.add_bias(pool, t)

        pe_parts.append(f2_pe_first)
        act_parts.append(f2_act_first)
        dve_parts.append(f2_dve_first)
        pe_parts.append(lambda e: run_steps(e, TILES, 5, lambda s: f2_pe(e, s)))
        act_parts.append(lambda e: run_steps(e, TILES, 5, lambda s: f2_act(e, s)))
        dve_parts.append(lambda e: run_steps(e, TILES, 5, lambda s: f2_dve(e, s)))
        pool_parts.append(lambda e: run_steps(e, TILES, 5, lambda s: f2_pool(e, s)))

        tail_a3 = attention(3, tail_f2, [])

        f3g = banks.plan([("gate", 4, 0)], 1, 0)
        f3 = banks.plan([("pa", (0, 2), 1), ("pb", (1, 3), 1)], TILES, 1)
        used["n"] = 0
        xs3 = carve(2 * P).rearrange("p (u t) -> p u t", u=2)
        prod3 = carve(2 * E * D).rearrange("p (u e d) -> p u e d", u=2, e=E)
        quarter3 = carve(2 * 2 * D).rearrange("p (u d) -> p u d", u=2)
        y3 = carve(2 * D).rearrange("p (u d) -> p u d", u=2)
        lg3, m3, w3, oh3 = (carve(TILES * E).rearrange("p (t e) -> p t e", e=E) for _ in range(4))
        ix3 = carve(TILES * E).bitcast(U32).rearrange("p (t e) -> p t e", e=E)
        ixf3 = carve(TILES * 2).rearrange("p (t k) -> p t k", k=2)
        gap3, ex3, w03, w13 = (carve(TILES) for _ in range(4))
        f3_step, f3_gap, f3_exp, f3_xs, f3_scaled, f3_half, f3_quarter, f3_summed, f3_added = (
            sem(f"f3_{x}") for x in ("step", "gap", "exp", "xs", "scaled", "half", "quarter", "summed", "added"))

        def f3_pe_first(pe):
            have(pe, "w3f")
            fill(pe, f3g, "gate", T0)
            stored(pe, tail_a3.plan, "lnt", At(TILES - 1))
            for n in range(TILES):
                m = nc.tensor.matmul(ps(4, E, n * E), lnT[:, n * P:(n + 1) * P], mat(w3f, W3F, "gate"), start=True, stop=True)
            m.then_inc(full[4], 1)

        def f3_act_first(act):
            act.wait_ge(f3_gap, 1)
            nc.scalar.activation(ex3, gap3, ACT.Exp).then_inc(f3_exp, 1)

        def f3_dve_first(dve):
            count = [0]

            def link(m):
                count[0] += 1
                m.then_inc(f3_step, 1)
                dve.wait_ge(f3_step, count[0])

            filled(dve, f3g, "gate", T0)
            nc.vector.tensor_copy(lg3, ps(4, TILES * E)).then_inc(free[4], 1)
            stored(dve, f3g, "gate", T0)
            for n in range(TILES):
                m = nc.vector.max(m3[:, n, :], lg3[:, n, :])
            link(m)
            nc.vector.tensor_tensor(gap3, m3[:, :, 1], m3[:, :, 0], ALU.subtract).then_inc(f3_gap, 1)
            for n in range(TILES):
                m = nc.vector.max_index(ix3[:, n, :], m3[:, n, :], lg3[:, n, :])
            link(m)
            link(nc.vector.tensor_copy(ixf3, ix3[:, :, 0:2]))
            dve.wait_ge(f3_exp, 1)
            link(nc.vector.tensor_scalar(w03, ex3, 1.0, None, ALU.add))
            link(nc.vector.reciprocal(w03, w03))
            link(nc.vector.tensor_tensor(w13, ex3, w03, ALU.mult))
            iota = mat(const, CONST, "iota").unsqueeze(1).to_broadcast((P, TILES, E))
            for k, (o, w) in enumerate(((w3, w03), (oh3, w13))):
                link(nc.vector.tensor_tensor(o, iota, ixf3[:, :, k:k + 1].to_broadcast((P, TILES, E)), ALU.is_equal))
                link(nc.vector.tensor_tensor(o, o, w.unsqueeze(2).to_broadcast((P, TILES, E)), ALU.mult))
            link(nc.vector.tensor_tensor(w3, w3, oh3, ALU.add))

        def f3_pe(pe, step):
            t = step - 1
            if t.valid(TILES):
                pe.wait_ge(f3_xs, t.times(1, 1))
                for i, job in enumerate(("pa", "pb")):
                    k = f3.bank(job, t)
                    fill(pe, f3, job, t)
                    nc.tensor.matmul(ps(k), xs3[:, t.n % 2, :], mat(w3f, W3F, "w")[:, i * 512:(i + 1) * 512], start=True, stop=True) \
                        .then_inc(full[k], 1)

        def f3_act(act, step):
            t = step
            if t.valid(TILES):
                if t.n >= 2:
                    filled(act, f3, "pb", t - 2)
                act.sem_inc(sem("act_carried"), 1)
                nc.scalar.activation(xs3[:, t.n % 2, :], cols(lnT, t), ACT.Copy).then_inc(f3_xs, 1)

        def f3_dve(dve, step):
            t = step - 1
            if t.valid(TILES):
                u = t.n % 2
                if t.n >= 2:
                    dve.wait_ge(f3_quarter, (t - 2).times(1, 1))
                filled(dve, f3, "pa", t)
                filled(dve, f3, "pb", t)
                w = w3[:, t.n, :] if t.pair is None else w3.rearrange("p t e -> p (t e)")[:, bass.ds(t.times(E), E)]
                nc.vector.tensor_tensor(prod3[:, u, :, :], psum[:, 2 * u:2 * u + 2, :].rearrange("p a (e d) -> p (a e) d", d=D),
                                        w.unsqueeze(2).to_broadcast((P, E, D)), ALU.mult).then_inc(f3_scaled, 1)
            t = step - 2
            if t.valid(TILES):
                if t.n >= 2:
                    dve.wait_ge(f3_summed, (t - 2).times(1, 1))
                p = prod3[:, t.n % 2, :, :].rearrange("p e d -> p (e d)")
                dve.wait_ge(f3_half, t.times(1, 1))
                nc.vector.tensor_tensor(quarter3[:, t.n % 2, :], p[:, 0:256], p[:, 256:512], ALU.add).then_inc(f3_quarter, 1)
            t = step - 1
            if t.valid(TILES):
                dve.wait_ge(f3_scaled, t.times(1, 1))
                dve.sem_inc(free[f3.bank("pa", t)], 1)
                dve.sem_inc(free[f3.bank("pb", t)], 1)
            t = step - 3
            if t.valid(TILES):
                if t.n >= 2:
                    dve.wait_ge(f3_added, (t - 2).times(1, 1))
                q = quarter3[:, t.n % 2, :]
                dve.wait_ge(f3_quarter, t.times(1, 1))
                nc.vector.tensor_tensor(y3[:, t.n % 2, :], q[:, 0:D], q[:, D:2 * D], ALU.add).then_inc(f3_summed, 1)
            t = step - 4
            if t.valid(TILES):
                dve.wait_ge(f3_summed, t.times(1, 1))
                nc.vector.tensor_tensor(xt(t), xt(t), y3[:, t.n % 2, :], ALU.add).then_inc(f3_added, 1)

        def f3_pool(pool, step):
            t = step - 1
            if t.valid(TILES):
                p = prod3[:, t.n % 2, :, :].rearrange("p e d -> p (e d)")
                pool.wait_ge(f3_scaled, t.times(1, 1))
                pool.tensor_tensor(p[:, 0:512], p[:, 0:512], p[:, 512:1024], ALU.add).then_inc(f3_half, 1)

        pe_parts.append(f3_pe_first)
        act_parts.append(f3_act_first)
        dve_parts.append(f3_dve_first)
        pe_parts.append(lambda e: run_steps(e, TILES, 4, lambda s: f3_pe(e, s)))
        act_parts.append(lambda e: run_steps(e, TILES, 4, lambda s: f3_act(e, s)))
        dve_parts.append(lambda e: run_steps(e, TILES, 4, lambda s: f3_dve(e, s)))
        pool_parts.append(lambda e: run_steps(e, TILES, 4, lambda s: f3_pool(e, s)))

        out_stored = sem("out_stored")
        STORES = 4

        def sp_store(sp):
            for i in range(STORES):
                n = TILES // STORES
                sp.wait_ge(f3_added, n * (i + 1))
                sp.dma_start(out[:, i * n * D:(i + 1) * n * D], x_tok[:, i * n * D:(i + 1) * n * D]).then_inc(out_stored, 16)
            sp.wait_ge(out_stored, 16 * STORES)

        sp_parts.append(sp_store)
        block = ctx.enter_context(nc.Block())

        @block.sync
        def _(sp):
            for part in sp_parts:
                part(sp)

        @block.tensor
        def _(pe):
            for part in pe_parts:
                part(pe)

        @block.scalar
        def _(act):
            for part in act_parts:
                part(act)

        @block.vector
        def _(dve):
            for part in dve_parts:
                part(dve)

        @block.gpsimd
        def _(pool):
            for part in pool_parts:
                part(pool)


def _tokens(a):
    return np.ascontiguousarray(np.asarray(a).reshape(TILES, P, D).transpose(1, 0, 2).reshape(P, TILES * D))


def _columns(at, n, blocks):
    a = np.zeros((P, n), np.float32)
    for name, block in blocks.items():
        s, w = at[name]
        block = np.asarray(block).reshape(-1, w)
        a[:block.shape[0], s:s + w] = block
    return a


def _chunks(a, c):
    a = np.asarray(a)
    return a.reshape(c, P, -1).transpose(1, 0, 2).reshape(P, -1)


def _constants():
    p = np.arange(P)
    q, k = p[:, None] % S, np.arange(S)[None, :]
    sel = np.zeros((P, EC, P))
    for c in range(EC):
        for e in range(2):
            sel[2 * c + e, c, e * HE:(e + 1) * HE] = 1
    selw = np.zeros((P, 2, P))
    selw[0, 0, :] = 1
    selw[1, 1, :] = 1
    return _columns(CONST, NCONST, {
        "ident": np.eye(P), "two": (p[:, None] % S == np.arange(S)[None, :]), "head": (p[:, None] // DH2 == np.arange(H2)[None, :]),
        "half": (p[:, None] // S == np.arange(2)[None, :]), "iota": np.tile(np.arange(E), (P, 1)),
        "m1": np.where(p[:, None] // S == p[None, :] // S, 0.0, OFF), "m2": np.where(k > q, OFF, 0.0),
        "m3": (np.abs(q - k) > WIN // 2), "sel": sel.reshape(P, -1), "selw": selw.reshape(P, -1)})


def _heads(a):
    return _chunks(a, 8)


def kernel(**i):
    import concourse.bacc as bacc
    from concourse.bass_utils import run_bass_kernel_spmd as run

    i = {k: np.asarray(v) for k, v in i.items()}
    x0, a1, f1, a2, a3 = "L0_xattn_", "L1_xattn_", "L1_ffn_", "L2_xattn_", "L3_xattn_"
    vecs = {"ln1_g": i[x0 + "ln1_g"], "ln1_b": i[x0 + "ln1_b"], "ln2_g": i[x0 + "ln2_g"], "ln2_b": i[x0 + "ln2_b"],
            "f0_g": i["L0_ffn_ln_gamma"], "f0_b": i["L0_ffn_ln_beta"], "f0_b1": i["L0_ffn_fc1_bias"].reshape(FC, P).T,
            "f2_bin": i["L2_ffn_b_in"].reshape(FC, P).T, "b_r1": i[f1 + "b_r1"], "b_h1": i[f1 + "b_h1"],
            "b_h2": np.broadcast_to(i[f1 + "b_h2"], (P,)), "b_e1": i[f1 + "expert_b1"].reshape(EC, P).T,
            "b_s1": i[f1 + "b_s1"], "b_s2": i[f1 + "b_s2"].reshape(3, P).T, "b_f1": i[f1 + "b_f1"].reshape(2, P).T,
            "b_f2": i[f1 + "b_f2"], "iw": i[f1 + "integration_weight"], "mu": i[f1 + "mu"],
            "shared": np.broadcast_to(i[f1 + "shared_weight"], (P,))}
    for n, a in (("a1", a1), ("a2", a2), ("a3", a3)):
        vecs |= {f"{n}_b{w}": i[f"{a}b{w}"] for w in "qkv"}
    rows = {"f0_b2": i["L0_ffn_fc2_bias"], "a1_bo": i[a1 + "bo"], "a2_bo": i[a2 + "bo"], "a3_bo": i[a3 + "bo"],
            "f2_bo": i["L2_ffn_b_out"], "f0_s1": i["L0_ffn_fc1_scales"], "f0_s2": i["L0_ffn_fc2_scales"], "b_r2": i[f1 + "b_r2"]}
    wkv = i[x0 + "Wkv"]
    e1 = i[f1 + "expert_w1"].transpose(1, 0, 2).reshape(2 * D, E * HE)
    arrays = {
        "x_tok": _tokens(i["x"]), "ctx_tok": _tokens(i["ctx_1024"]),
        "cT": i["ctx_1024"].reshape(B * S, D).T,
        "vecs": _columns(VECS, NVECS, vecs),
        "rows": _columns(ROWS, NROWS, {k: v.reshape(1, -1) for k, v in rows.items()})[0],
        "w0qk": np.concatenate([_heads(i[x0 + "Wq"].T), _heads(wkv[:, :1024].T)], axis=1),
        "w0vo": np.concatenate([_heads(wkv[:, 1024:].T), _heads(i[x0 + "Wo"])], axis=1),
        "w0q": np.stack([i["L0_ffn_fc1_q"], _chunks(i["L0_ffn_fc2_q"], FC)], axis=1),
        "wa": _columns(WA, NWA, {f"{n}{w}": i[f"{a}W{w}"].T for n, a in (("a1", a1), ("a2", a2), ("a3", a3)) for w in "qkvo"}),
        "w1f": _columns(W1F, NW1F, {
            "e1x": e1[:D], "e1v": e1[D:], "e2": _chunks(i[f1 + "expert_w2"].reshape(E * HE, 3 * D), EC),
            "s1x": i[f1 + "w_s1"][:D], "s1v": i[f1 + "w_s1"][D:], "s2": i[f1 + "w_s2"], "r1": i[f1 + "w_r1"],
            "r2": i[f1 + "w_r2"], "h1": i[f1 + "w_h1"], "h2": np.broadcast_to(i[f1 + "w_h2"], (32, P)),
            "f1": i[f1 + "w_f1"], "f2": _chunks(i[f1 + "w_f2"], 2)}),
        "b_e2": i[f1 + "expert_b2"],
        "w2f": _columns(W2F, NW2F, {"in": _chunks(i["L2_ffn_W_in"].T, FC), "out": _chunks(i["L2_ffn_W_out"], FC)}),
        "w3f": _columns(W3F, NW3F, {"gate": i["L3_ffn_gate_w"].T, "w": i["L3_ffn_weight"].transpose(1, 0, 2).reshape(D, E * D)}),
        "const": _constants(),
    }
    nc = bacc.Bacc("TRN2", target_bir_lowering=False, num_devices=1)
    ins, args = {}, {}
    for name, a in arrays.items():
        a = np.ascontiguousarray(a)
        ins[f"in_{name}"] = a
        args[name] = nc.dram_tensor(f"in_{name}", a.shape, mybir.dt.from_np(a.dtype), kind="ExternalInput").ap()
    out = nc.dram_tensor("out_0", (P, TILES * D), F32, kind="ExternalOutput").ap()
    build(nc, args, out)
    r = run(nc, [ins], core_ids=[0])
    got = r.results[0]["out_0"]
    return np.ascontiguousarray(got.reshape(P, TILES, D).transpose(1, 0, 2)).reshape(B, S, D)
```
